# Optimizing a Trainium2 kernel written in Bass

```python
import numpy as np
import jax
import jax.numpy as jnp

def _softmax(x, axis=-1):
    return jax.nn.softmax(x, axis=axis)

def _gelu(x):
    return jax.nn.gelu(x, approximate=True)

def _silu(x):
    return jax.nn.silu(x)

def _sigmoid(x):
    return jax.nn.sigmoid(x)

def _layernorm(x, axis=-1, eps=1e-05):
    m = jnp.mean(x, axis=axis, keepdims=True)
    v = jnp.var(x, axis=axis, keepdims=True)
    return (x - m) / jnp.sqrt(v + eps)

def _scatter_add(tgt, idx, src, axis=0):
    return tgt.at[idx].add(src)

def _segment_sum(src, seg, n):
    return jax.ops.segment_sum(src, seg, n)
kernel_name = 'mk_vit_tower_d2_tok_img1024_r4_2649e9'

def setup_inputs(seed: int=0):
    np.random.seed(seed)
    _w = jnp.asarray

    def _rec_inputs():
        import jax
        import jax.numpy as jnp
        _rk = jax.random.key(seed)
        x = -0.00016672 + 0.999947 * jax.random.normal(jax.random.fold_in(_rk, 1), (16, 3, 96, 96), jnp.float32)
        return x
    x = _rec_inputs()

    def _L0_tok_setup():
        import jax, jax.numpy as jnp
        import numpy as np
        IMG = 96
        PATCH = 16
        C_IN = 3
        EMBED = 256
        NPH = IMG // PATCH
        NUM_PATCHES = NPH * NPH
        PATCH_DIM = PATCH * PATCH * C_IN
        key = jax.random.key(seed)
        k_x, k_w, k_b, k_cls, k_pos = jax.random.split(key, 5)
        x = jax.random.normal(k_x, (64, C_IN, IMG, IMG), dtype=jnp.float32)
        W = jax.random.normal(k_w, (EMBED, PATCH_DIM), dtype=jnp.float32) * (1.0 / np.sqrt(PATCH_DIM))
        b = jax.random.normal(k_b, (EMBED,), dtype=jnp.float32) * 0.01
        cls_token = jax.random.normal(k_cls, (1, 1, EMBED), dtype=jnp.float32) * 0.02
        pos_embed = jax.random.normal(k_pos, (1, NUM_PATCHES + 1, EMBED), dtype=jnp.float32) * 0.02
        return {'x': x, 'W': W, 'b': b, 'cls_token': cls_token, 'pos_embed': pos_embed}
    _L0_tok_all = _L0_tok_setup()
    _L0_tok_in = {k: v for k, v in _L0_tok_all.items() if k in ('W', 'b', 'cls_token', 'pos_embed')}
    del _L0_tok_all

    def _L0_attn_setup():
        import jax, jax.numpy as jnp
        import numpy as np
        B, T, C = (64, 64, 256)
        N_HEAD, HEAD_SIZE, KV_RANK = (16, 64, 128)
        BLOCK_SIZE = 64
        key = jax.random.key(seed)
        ks = jax.random.split(key, 5)
        HD = N_HEAD * HEAD_SIZE

        def init(k, shape):
            fan_in = shape[0]
            bound = 1.0 / np.sqrt(fan_in)
            return jax.random.uniform(k, shape, jnp.float32, -bound, bound)
        return {'x': jax.random.normal(ks[0], (B, T, C), jnp.float32), 'w_kv_down': init(ks[1], (C, KV_RANK)), 'w_kv_up': init(ks[2], (KV_RANK, 2 * HD)), 'w_q': init(ks[3], (C, HD)), 'w_out': init(ks[4], (HD, C))}
    _L0_attn_all = _L0_attn_setup()
    _L0_attn_in = {k: v for k, v in _L0_attn_all.items() if k in ('w_kv_down', 'w_kv_up', 'w_q', 'w_out')}
    del _L0_attn_all

    def _L0_ffn_setup():
        import jax, jax.numpy as jnp
        import numpy as np
        CAPACITY = 2
        B, S, D, E, I = (4, 1024, 256, 8, 1024)
        key = jax.random.key(seed)
        k0, k1, k2, k3, k4 = jax.random.split(key, 5)
        x = jax.random.normal(k0, (B, S, D), dtype=jnp.float32)
        gate_w = jax.random.normal(k1, (E, D), dtype=jnp.float32) * 0.006
        w_gate = jax.random.normal(k2, (E, I, D), dtype=jnp.float32) * (1.0 / np.sqrt(D))
        w_up = jax.random.normal(k3, (E, I, D), dtype=jnp.float32) * (1.0 / np.sqrt(D))
        w_down = jax.random.normal(k4, (E, D, I), dtype=jnp.float32) * (1.0 / np.sqrt(I))
        return {'x': x, 'gate_w': gate_w, 'w_gate': w_gate, 'w_up': w_up, 'w_down': w_down}
    _L0_ffn_all = _L0_ffn_setup()
    _L0_ffn_in = {k: v for k, v in _L0_ffn_all.items() if k in ('gate_w', 'w_gate', 'w_up', 'w_down')}
    del _L0_ffn_all

    def _L1_attn_setup():
        import jax, jax.numpy as jnp
        import numpy as np
        B, T, D = (1, 512, 256)
        H, DH, DV, DF = (16, 64, 64, 1024)
        EPS_LN = 1e-05
        EPS_DEN = 1e-06

        def _layernorm(x, g, b):
            m = jnp.mean(x, axis=-1, keepdims=True)
            v = jnp.mean((x - m) ** 2, axis=-1, keepdims=True)
            return (x - m) / jnp.sqrt(v + EPS_LN) * g + b

        def _phi(x):
            return jax.nn.elu(x) + 1.0

        def _linear_attention(x, Wq, Wk, Wv, Wo):
            b, t, d = x.shape
            Q = _phi((x @ Wq).reshape(b, t, H, DH)).transpose(0, 2, 1, 3)
            K = _phi((x @ Wk).reshape(b, t, H, DH)).transpose(0, 2, 1, 3)
            V = (x @ Wv).reshape(b, t, H, DV).transpose(0, 2, 1, 3)
            KV = jnp.einsum('bhti,bhtj->bhtij', K, V)
            S = jnp.cumsum(KV, axis=2)
            z = jnp.cumsum(K, axis=2)
            num = jnp.einsum('bhti,bhtij->bhtj', Q, S)
            den = jnp.maximum(jnp.einsum('bhti,bhti->bht', Q, z), EPS_DEN)[..., None]
            out = (num / den).transpose(0, 2, 1, 3).reshape(b, t, H * DV)
            return out @ Wo
        key = jax.random.key(seed)
        ks = jax.random.split(key, 8)
        s = 0.02
        return {'x': jax.random.normal(ks[0], (B, T, D), dtype=jnp.float32), 'ln1_g': jnp.ones((D,), jnp.float32), 'ln1_b': jnp.zeros((D,), jnp.float32), 'Wq': jax.random.normal(ks[1], (D, H * DH), jnp.float32) * s, 'Wk': jax.random.normal(ks[2], (D, H * DH), jnp.float32) * s, 'Wv': jax.random.normal(ks[3], (D, H * DV), jnp.float32) * s, 'Wo': jax.random.normal(ks[4], (H * DV, D), jnp.float32) * s, 'ln2_g': jnp.ones((D,), jnp.float32), 'ln2_b': jnp.zeros((D,), jnp.float32), 'Wf1': jax.random.normal(ks[5], (D, DF), jnp.float32) * s, 'Wf2': jax.random.normal(ks[6], (DF, D), jnp.float32) * s}
    _L1_attn_all = _L1_attn_setup()
    _L1_attn_in = {k: v for k, v in _L1_attn_all.items() if k in ('ln1_g', 'ln1_b', 'Wq', 'Wk', 'Wv', 'Wo', 'ln2_g', 'ln2_b', 'Wf1', 'Wf2')}
    del _L1_attn_all

    def _L1_ffn_setup():
        import jax, jax.numpy as jnp
        import numpy as np
        DIM = 256
        HIDDEN = 512
        N_EXPERTS = 8
        TOP_K = 2
        EPS = 1e-06

        def rms_norm(x, scale, eps=EPS):
            ms = jnp.mean(jnp.square(x.astype(jnp.float32)), axis=-1, keepdims=True)
            s = scale.astype(jnp.float32) * jax.lax.rsqrt(ms + eps)
            return x * s.astype(x.dtype)

        def moe_linear(xf, ids, W):
            E = W.shape[0]
            out = jnp.zeros((xf.shape[0], W.shape[1]), dtype=xf.dtype)
            for e in range(E):
                out = out + jnp.where((ids == e)[:, None], xf @ W[e].T, 0.0)
            return out
        key = jax.random.key(seed)
        k1, k2, k3, k4 = jax.random.split(key, 4)
        x = jax.random.normal(k1, (4, 1024, DIM), dtype=jnp.float32)
        norm_scale = jnp.ones((DIM,), dtype=jnp.float32)
        w_router = jax.random.normal(k2, (N_EXPERTS, DIM), dtype=jnp.float32) / np.sqrt(DIM)
        lim_up = np.sqrt(6.0 / (DIM + 2 * HIDDEN))
        w_up = jax.random.uniform(k3, (N_EXPERTS, 2 * HIDDEN, DIM), dtype=jnp.float32, minval=-lim_up, maxval=lim_up)
        lim_dn = np.sqrt(6.0 / (HIDDEN + DIM))
        w_down = jax.random.uniform(k4, (N_EXPERTS, DIM, HIDDEN), dtype=jnp.float32, minval=-lim_dn, maxval=lim_dn)
        return {'x': x, 'norm_scale': norm_scale, 'w_router': w_router, 'w_up': w_up, 'w_down': w_down}
    _L1_ffn_all = _L1_ffn_setup()
    _L1_ffn_in = {k: v for k, v in _L1_ffn_all.items() if k in ('norm_scale', 'w_router', 'w_up', 'w_down')}
    del _L1_ffn_all
    return {'x': x, 'L0_tok_W': _L0_tok_in['W'], 'L0_tok_b': _L0_tok_in['b'], 'L0_tok_cls_token': _L0_tok_in['cls_token'], 'L0_tok_pos_embed': _L0_tok_in['pos_embed'], 'L0_attn_w_kv_down': _L0_attn_in['w_kv_down'], 'L0_attn_w_kv_up': _L0_attn_in['w_kv_up'], 'L0_attn_w_q': _L0_attn_in['w_q'], 'L0_attn_w_out': _L0_attn_in['w_out'], 'L0_ffn_gate_w': _L0_ffn_in['gate_w'], 'L0_ffn_w_gate': _L0_ffn_in['w_gate'], 'L0_ffn_w_up': _L0_ffn_in['w_up'], 'L0_ffn_w_down': _L0_ffn_in['w_down'], 'L1_attn_ln1_g': _L1_attn_in['ln1_g'], 'L1_attn_ln1_b': _L1_attn_in['ln1_b'], 'L1_attn_Wq': _L1_attn_in['Wq'], 'L1_attn_Wk': _L1_attn_in['Wk'], 'L1_attn_Wv': _L1_attn_in['Wv'], 'L1_attn_Wo': _L1_attn_in['Wo'], 'L1_attn_ln2_g': _L1_attn_in['ln2_g'], 'L1_attn_ln2_b': _L1_attn_in['ln2_b'], 'L1_attn_Wf1': _L1_attn_in['Wf1'], 'L1_attn_Wf2': _L1_attn_in['Wf2'], 'L1_ffn_norm_scale': _L1_ffn_in['norm_scale'], 'L1_ffn_w_router': _L1_ffn_in['w_router'], 'L1_ffn_w_up': _L1_ffn_in['w_up'], 'L1_ffn_w_down': _L1_ffn_in['w_down']}

def reference(x, L0_tok_W, L0_tok_b, L0_tok_cls_token, L0_tok_pos_embed, L0_attn_w_kv_down, L0_attn_w_kv_up, L0_attn_w_q, L0_attn_w_out, L0_ffn_gate_w, L0_ffn_w_gate, L0_ffn_w_up, L0_ffn_w_down, L1_attn_ln1_g, L1_attn_ln1_b, L1_attn_Wq, L1_attn_Wk, L1_attn_Wv, L1_attn_Wo, L1_attn_ln2_g, L1_attn_ln2_b, L1_attn_Wf1, L1_attn_Wf2, L1_ffn_norm_scale, L1_ffn_w_router, L1_ffn_w_up, L1_ffn_w_down):
    import jax
    import jax.numpy as jnp

    def _L0_tok_ref(x, W, b, cls_token, pos_embed):
        import jax, jax.numpy as jnp
        import numpy as np
        IMG = 96
        PATCH = 16
        C_IN = 3
        EMBED = 256
        NPH = IMG // PATCH
        NUM_PATCHES = NPH * NPH
        PATCH_DIM = PATCH * PATCH * C_IN
        B, C, H, Wd = x.shape
        nph, npw = (H // PATCH, Wd // PATCH)
        patches = x.reshape(B, C, nph, PATCH, npw, PATCH)
        patches = patches.transpose(0, 2, 4, 1, 3, 5)
        patches = patches.reshape(B, nph * npw, C * PATCH * PATCH)
        proj = jnp.einsum('bnd,ed->bne', patches, W) + b
        cls = jnp.broadcast_to(cls_token, (B, 1, cls_token.shape[-1]))
        out = jnp.concatenate([cls, proj], axis=1) + pos_embed
        return out

    def _L0_attn_ref(x, w_kv_down, w_kv_up, w_q, w_out):
        import jax, jax.numpy as jnp
        import numpy as np
        B, T, C = (64, 64, 256)
        N_HEAD, HEAD_SIZE, KV_RANK = (16, 64, 128)
        BLOCK_SIZE = 64
        Bx, Tx, Cx = x.shape
        HD = N_HEAD * HEAD_SIZE
        latent_kv = x @ w_kv_down
        kv = latent_kv @ w_kv_up
        k, v = (kv[..., :HD], kv[..., HD:])
        k = k.reshape(Bx, Tx, N_HEAD, HEAD_SIZE)
        v = v.reshape(Bx, Tx, N_HEAD, HEAD_SIZE)
        q = (x @ w_q).reshape(Bx, Tx, N_HEAD, HEAD_SIZE)
        scale = HEAD_SIZE ** (-0.5)
        att = jnp.einsum('bqhd,bkhd->bhqk', q, k) * scale
        causal = jnp.tril(jnp.ones((Tx, Tx), dtype=bool))
        att = jnp.where(causal, att, -jnp.inf)
        att = jax.nn.softmax(att, axis=-1)
        y = jnp.einsum('bhqk,bkhd->bqhd', att, v)
        y = y.reshape(Bx, Tx, HD)
        return y @ w_out

    def _L0_ffn_ref(x, gate_w, w_gate, w_up, w_down):
        import jax, jax.numpy as jnp
        import numpy as np
        CAPACITY = 2
        B, S, D = x.shape
        E = gate_w.shape[0]
        k = S // E * CAPACITY
        logits = jnp.einsum('bsd,ed->bse', x, gate_w)
        affinity = jax.nn.softmax(logits, axis=-1)
        affinity = jnp.transpose(affinity, (0, 2, 1))
        gating, idx = jax.lax.top_k(affinity, k)
        bidx = jnp.arange(B)[:, None, None]
        x_in = x[bidx, idx]
        h = jax.nn.silu(jnp.einsum('bekd,eid->beki', x_in, w_gate)) * jnp.einsum('bekd,eid->beki', x_in, w_up)
        x_e = jnp.einsum('beki,edi->bekd', h, w_down)
        out = jnp.zeros_like(x).at[bidx, idx].add(gating[..., None] * x_e)
        return out

    def _L1_attn_ref(x, ln1_g, ln1_b, Wq, Wk, Wv, Wo, ln2_g, ln2_b, Wf1, Wf2):
        import jax, jax.numpy as jnp
        import numpy as np
        B, T, D = (1, 512, 256)
        H, DH, DV, DF = (16, 64, 64, 1024)
        EPS_LN = 1e-05
        EPS_DEN = 1e-06

        def _layernorm(x, g, b):
            m = jnp.mean(x, axis=-1, keepdims=True)
            v = jnp.mean((x - m) ** 2, axis=-1, keepdims=True)
            return (x - m) / jnp.sqrt(v + EPS_LN) * g + b

        def _phi(x):
            return jax.nn.elu(x) + 1.0

        def _linear_attention(x, Wq, Wk, Wv, Wo):
            b, t, d = x.shape
            Q = _phi((x @ Wq).reshape(b, t, H, DH)).transpose(0, 2, 1, 3)
            K = _phi((x @ Wk).reshape(b, t, H, DH)).transpose(0, 2, 1, 3)
            V = (x @ Wv).reshape(b, t, H, DV).transpose(0, 2, 1, 3)
            KV = jnp.einsum('bhti,bhtj->bhtij', K, V)
            S = jnp.cumsum(KV, axis=2)
            z = jnp.cumsum(K, axis=2)
            num = jnp.einsum('bhti,bhtij->bhtj', Q, S)
            den = jnp.maximum(jnp.einsum('bhti,bhti->bht', Q, z), EPS_DEN)[..., None]
            out = (num / den).transpose(0, 2, 1, 3).reshape(b, t, H * DV)
            return out @ Wo
        x = x + _linear_attention(_layernorm(x, ln1_g, ln1_b), Wq, Wk, Wv, Wo)
        h = _layernorm(x, ln2_g, ln2_b)
        x = x + jax.nn.gelu(h @ Wf1, approximate=False) @ Wf2
        return x

    def _L1_ffn_ref(x, norm_scale, w_router, w_up, w_down):
        import jax, jax.numpy as jnp
        import numpy as np
        DIM = 256
        HIDDEN = 512
        N_EXPERTS = 8
        TOP_K = 2
        EPS = 1e-06

        def rms_norm(x, scale, eps=EPS):
            ms = jnp.mean(jnp.square(x.astype(jnp.float32)), axis=-1, keepdims=True)
            s = scale.astype(jnp.float32) * jax.lax.rsqrt(ms + eps)
            return x * s.astype(x.dtype)

        def moe_linear(xf, ids, W):
            E = W.shape[0]
            out = jnp.zeros((xf.shape[0], W.shape[1]), dtype=xf.dtype)
            for e in range(E):
                out = out + jnp.where((ids == e)[:, None], xf @ W[e].T, 0.0)
            return out
        B, S, D = x.shape
        skip = x
        xn = rms_norm(x, norm_scale)
        scores = (xn @ w_router.T).astype(jnp.float32)
        scores_topk, idx = jax.lax.top_k(scores, TOP_K)
        weights = jax.nn.softmax(scores_topk, axis=-1)
        xf = jnp.broadcast_to(xn[..., None, :], (B, S, TOP_K, D)).reshape(-1, D)
        ids = idx.reshape(-1)
        up = moe_linear(xf, ids, w_up)
        u, gate = jnp.split(up, 2, axis=-1)
        h = u * jax.nn.silu(gate)
        down = moe_linear(h, ids, w_down)
        down = down.reshape(B, S, TOP_K, D)
        out = jnp.sum(down * weights[..., None].astype(down.dtype), axis=-2)
        return out + skip
    h = _L0_tok_ref(x, L0_tok_W, L0_tok_b, L0_tok_cls_token, L0_tok_pos_embed)
    h = h + _L0_attn_ref(_layernorm(h, axis=-1), L0_attn_w_kv_down, L0_attn_w_kv_up, L0_attn_w_q, L0_attn_w_out)
    h = h + _L0_ffn_ref(_layernorm(h, axis=-1), L0_ffn_gate_w, L0_ffn_w_gate, L0_ffn_w_up, L0_ffn_w_down)
    h = h + _L1_attn_ref(_layernorm(h, axis=-1), L1_attn_ln1_g, L1_attn_ln1_b, L1_attn_Wq, L1_attn_Wk, L1_attn_Wv, L1_attn_Wo, L1_attn_ln2_g, L1_attn_ln2_b, L1_attn_Wf1, L1_attn_Wf2)
    h = h + _L1_ffn_ref(_layernorm(h, axis=-1), L1_ffn_norm_scale, L1_ffn_w_router, L1_ffn_w_up, L1_ffn_w_down)
    return h

_drawn_inputs = setup_inputs


def setup_inputs(seed=0):
    import zlib

    import numpy as np

    out = dict(_drawn_inputs(seed))
    spreads = {'L1_attn_ln1_g': (1.0, 0.6),
     'L1_attn_ln1_b': (0.0, 0.698),
     'L1_attn_ln2_g': (1.0, 0.6),
     'L1_attn_ln2_b': (0.0, 0.8),
     'L1_ffn_norm_scale': (1.0, 0.2)}
    factors = {'L0_tok_b': 2.84, 'L0_attn_w_q': 2.692, 'L1_attn_Wq': 8.0, 'L1_attn_Wk': 8.0}
    for name, (base, spread) in spreads.items():
        noise = np.random.default_rng([zlib.crc32(name.encode()), seed]).standard_normal(out[name].shape)
        drawn = base * np.exp(spread * noise) if base else spread * noise
        out[name] = jnp.asarray(drawn.astype(out[name].dtype))
    for name, factor in factors.items():
        out[name] = (out[name] * factor).astype(out[name].dtype)
    return out
```

```python
from contextlib import ExitStack

import concourse.bass as bass
from concourse import mybir

ALU = mybir.AluOpType
ACT = mybir.ActivationFunctionType
AXX = mybir.AxisListType.X
F32 = mybir.dt.float32
U32 = mybir.dt.uint32

P = 128
IMAGES, D, SEQ = 16, 256, 37
TOK = IMAGES * SEQ
KD = D // P
NG, TG = IMAGES // 2, 2 * SEQ
GROUPS = [(TG * g, TG) for g in range(NG)]
TILES = [(t, min(P, TOK - t)) for t in range(0, TOK, P)]
NT = len(TILES)
HALF = TOK // 2
PD = 768
KP = PD // P
HEADS, DH = 16, 64
HD = HEADS * DH
KH = HD // P
RANK = 128
HU = 8
UNITS = NG * HEADS // HU
LAG = 3
NPM = LAG + 1
EXPERTS = 8
PICKS = SEQ // EXPERTS * 2
I0 = 1024
K0 = I0 // P
I1 = 512
K1 = I1 // P
DF = 1024
KF = DF // P
EPS_LN, EPS_RMS, EPS_DEN = 1e-5, 1e-6, 1e-6
SCALE = DH ** -0.5
MASKED = -1e30
W0 = 2 * KD * I0 + K0 * D
W1 = KD * 2 * I1 + K1 * D
BANK = 512

CONST = {}
_at = 0
for _name, _width in [("ident", P), ("addmask", TG), ("mulmask", TG), ("same_image", IMAGES),
                      ("same_expert", EXPERTS), ("fold", SEQ), ("which", 2), ("row", 1),
                      ("base_local", 1), ("base_global", 1), ("tokens", TOK), ("experts", EXPERTS)]:
    CONST[_name] = (_at, _at + _width)
    _at += _width
NCONST = _at
GAIN1, BIAS1, GAIN2, BIAS2, NSCALE = range(5)


def column_pieces(t0, n):
    out = []
    if t0 < BANK:
        w = min(n, BANK - t0)
        out.append((lambda m: m, lambda m: t0, 0, w))
    if t0 + n > BANK:
        a = max(t0, BANK)
        out.append((lambda m: 2, lambda m: a - BANK + m * (TOK - BANK), a - t0, t0 + n - a))
    return out


def vit_tower(nc, patches, tok_w, add_a, add_b, w_q, w_kvd, w_kvu, w_out, gate_w, w_e0,
              l1_wq, l1_wk, l1_wv, l1_wo, l1_wf1, l1_wf2, params, router, w_e1, consts, out):
    with ExitStack() as ctx:
        base = (nc.sbuf_base + 31) // 32 * 32
        end = nc.sbuf_usable_end

        def put(name, shape, offset, dt=F32):
            size = 4
            for n in shape[1:]:
                size *= n
            return nc.alloc_sbuf_tensor_at(name, shape, dt, offset=offset), offset + (size + 31) // 32 * 32

        def sem(name):
            return ctx.enter_context(nc.semaphore(name))

        at = base
        cst, at = put("cst", [P, NCONST], at)
        ones, at = put("ones", [P, P], at)
        neg_half, at = put("neg_half", [P, 1], at)
        par, at = put("par", [P, KD, 5], at)
        gw, at = put("gw", [P, KD, EXPERTS], at)
        rw, at = put("rw", [P, KD, EXPERTS], at)
        stat = []
        for n in range(6):
            s_, at = put(f"stat{n}", [P, 8, 12], at)
            stat.append(s_)
        att_small, at = put("att_small", [P, 2, NPM, 3, HU], at)
        rsm, at = put("rsm", [P, 4, 8 * 8], at)
        idx_u, at = put("idx_u", [P, NT, 8], at, U32)
        picks, at = put("picks", [P, 6, NT * 8], at)
        g_rows, at = put("g_rows", [P, 4, NT * 8], at)
        gt, at = put("gt", [P, TOK], at)
        rows_at = at
        h, at = put("h", [P, NG, D], at)
        x, at = put("x", [P, NG, D], at)
        h2, r_ = put("h2", [P, NT, D], rows_at)
        z, r_ = put("z", [P, NT, D], r_)
        nrm, r_ = put("nrm", [P, NT, D], r_)
        assert r_ <= at
        xt_a, at = put("xt_a", [P, KD, TOK], at)
        xt_b, at = put("xt_b", [P, KD, TOK], at)
        st, at = put("st", [P, KD, TOK], at)
        B = at
        qt, at = put("qt", [P, KH, TOK], at)
        kt, at = put("kt", [P, KH, TOK], at)
        v, at = put("v", [P, NG, HD], at)
        pm, at = put("pm", [P, NPM, HU * TG], at)
        pt, at = put("pt", [P, 2, HU * TG], at)
        B_end = at
        b = B
        apad, b = put("apad", [P, NG * (P + 16)], b)
        d_idx, b = put("d_idx", [P, P * PICKS], b)
        onehot, b = put("onehot", [P, P * PICKS], b)
        d_pick, b = put("d_pick", [P, 2, P], b)
        aff, b = put("aff", [P, 64], b)
        xin, b = put("xin", [P, KD, EXPERTS * P], b)
        spread, b = put("spread", [P, EXPERTS, TOK], b)
        hid0, b = put("hid0", [P, 3, K0, P], b)
        sg0, b = put("sg0", [P, 2, BANK], b)
        xe, b = put("xe", [P, D], b)
        slot2_at = b
        assert b + W0 * 4 <= B_end, (b + W0 * 4, B_end)
        b = B
        gbc, b = put("gbc", [P, EXPERTS, TOK], b)
        hid1, b = put("hid1", [P, 2, K1, TOK], b)
        sg1, b = put("sg1", [P, 4, HALF], b)
        ug1, b = put("ug1", [P, 4, HALF], b)
        assert b <= B + 64 * 1024
        b = B + 64 * 1024
        s_sum, b = put("s_sum", [P, NT, D], b)
        xn1, b = put("xn1", [P, NT, D], b)
        w_rows, b = put("w_rows", [P, NT, D], b)
        assert b <= B_end
        ft, b = put("ft", [P, KF, TOK], B)
        oute, b = put("oute", [P, KD, TOK], b)
        phi, b = put("phi", [P, 4, 2, HALF], B + (KH * TOK * 2 + NG * HD) * 4)
        assert b <= B_end
        at = B_end
        C = at
        wq0, c_ = put("wq0", [P, KD, HD], C)
        wkvd, c_ = put("wkvd", [P, KD, RANK], c_)
        wkvu, c_ = put("wkvu", [P, 2 * HD], c_)
        wout, c_ = put("wout", [P, KH, D], c_)
        wq1, at = put("wq1", [P, KD, HD], C)
        wk1, at = put("wk1", [P, KD, HD], at)
        wv1, at = put("wv1", [P, KD, HD], at)
        wo1, at = put("wo1", [P, KH, D], at)
        at = max(at, c_)
        E = at
        slot0 = []
        for n in range(2):
            s_, at = put(f"slot0_{n}", [P, W0], at)
            slot0.append(s_)
        slot0.append(put("slot0_2", [P, W0], slot2_at)[0])
        E1 = E + W0 * 4
        assert at <= end, (at, end)
        pat, e_ = put("pat", [P, 2, KP, HALF], E1)
        wtok, e_ = put("wtok", [P, KP, D], e_)
        assert e_ <= at
        slot1 = []
        e_ = E
        for n in range(2):
            s_, e_ = put(f"slot1_{n}", [P, W1], e_)
            slot1.append(s_)
        assert e_ <= E1
        wf1, e_ = put("wf1", [P, KD, DF], E1)
        wf2, e_ = put("wf2", [P, KF, D], e_)
        assert e_ <= at
        addp, _ = put("addp", [P, 2, D], B)

        ps = ctx.enter_context(nc.psum_tensor("ps", [P, 8, BANK], F32))

        def const(name, rows=P):
            a, z_ = CONST[name]
            return cst[0:rows, a:z_]

        ident = const("ident")

        d_const, d_par = sem("d_const"), sem("d_par")
        d_add, d_tok, d_qkv, d_out0, d_gw = sem("d_add"), sem("d_tok"), sem("d_qkv"), sem("d_out0"), sem("d_gw")
        d_pat = [sem("d_pat_0"), sem("d_pat_1")]
        d_e0 = [sem(f"d_e0_{n}") for n in range(3)]
        d_e1 = [sem("d_e1_0"), sem("d_e1_1")]
        d_l1, d_ffn, d_final = sem("d_l1"), sem("d_ffn"), sem("d_final")
        consts_set = sem("consts_set")
        dve_step = sem("dve_step")

        class Rows:
            def __init__(self, name):
                self.made, self.added = sem(name + "_made"), sem(name + "_added")
                self.var, self.rstd = sem(name + "_var"), sem(name + "_rstd")
                self.var2, self.rstd2 = sem(name + "_var2"), sem(name + "_rstd2")
                self.normed, self.turned, self.xt = sem(name + "_normed"), sem(name + "_turned"), sem(name + "_xt")
        r_tok, r_out0, r_mid, r_out1, r_ffn = [Rows(n) for n in ("tok", "out0", "mid", "out1", "ffn")]

        class Att:
            def __init__(self, name):
                self.made = sem(name + "_proj")
                self.by_act, self.by_dve = sem(name + "_by_act"), sem(name + "_by_dve")
                self.relu = sem(name + "_relu")
                self.scored, self.masked, self.maxed = sem(name + "_scored"), sem(name + "_masked"), sem(name + "_maxed")
                self.shifted, self.expd, self.summed = sem(name + "_shifted"), sem(name + "_expd"), sem(name + "_summed")
                self.p, self.pt_made, self.pt = sem(name + "_p"), sem(name + "_pt_made"), sem(name + "_pt")
                self.y_made, self.y = sem(name + "_y_made"), sem(name + "_y")
        a0, a1 = Att("a0"), Att("a1")

        logits0, shifted0, exped0 = sem("logits0"), sem("shifted0"), sem("exped0")
        apad_set, affinity_made, d_ready, picks_made, onehot_set = (
            sem("apad_set"), sem("affinity_made"), sem("d_ready"), sem("picks_made"), sem("onehot_set"))
        gathered, xin_act, xin_dve, pick_cols, spread_set = (
            sem("gathered"), sem("xin_act"), sem("xin_dve"), sem("pick_cols"), sem("spread_set"))
        gu0, silu0, hid0_set, down0, xe_set, comb0 = (
            sem("gu0"), sem("silu0"), sem("hid0_set"), sem("down0"), sem("xe_set"), sem("comb0"))
        h2t_set = sem("h2t_set")
        ffn_made, ffn_act = sem("hidden_made"), sem("hidden_act")
        s_set, s_turned, st_set = sem("s_set"), sem("s_turned"), sem("st_set")
        logits1, logits_out, diff1, exped1, gates_set, gt_made, gt_set = (
            sem("logits1"), sem("logits_out"), sem("diff1"), sem("exped1"), sem("gates_set"), sem("gt_made"), sem("gt_set"))
        gbc_made, gbc_set = sem("gbc_made"), sem("gbc_set")
        gu1, silu1, ug_set, hid1_set, down1 = sem("gu1"), sem("silu1"), sem("ug_set"), sem("hid1_set"), sem("down1")
        out_set = sem("out_set")

        block = ctx.enter_context(nc.Block())

        @block.sync
        def _(sp):
            sp.dma_start(pat[:, 0], patches[0]).then_inc(d_pat[0], 16)
            sp.dma_start(wtok[:], tok_w).then_inc(d_tok, 16)
            sp.dma_start(addp[0:TG, 0, :], add_a).then_inc(d_add, 16)
            sp.dma_start(addp[0:TG, 1, :], add_b).then_inc(d_add, 16)
            sp.dma_start(cst[:], consts).then_inc(d_const, 16)
            sp.dma_start(pat[:, 1], patches[1]).then_inc(d_pat[1], 16)
            sp.dma_start(wkvd[:], w_kvd).then_inc(d_qkv, 16)
            sp.dma_start(wq0[:], w_q).then_inc(d_qkv, 16)
            sp.dma_start(wkvu[:], w_kvu).then_inc(d_qkv, 16)
            sp.dma_start(wout[:], w_out).then_inc(d_out0, 16)
            sp.dma_start(gw[:], gate_w).then_inc(d_gw, 16)
            sp.dma_start(rw[:], router).then_inc(d_par, 16)
            sp.dma_start(par[:], params).then_inc(d_par, 16)
            sp.dma_start(slot0[0][:], w_e0[0]).then_inc(d_e0[0], 16)
            sp.wait_ge(r_tok.made, NG)
            sp.dma_start(slot0[1][:], w_e0[1]).then_inc(d_e0[1], 16)
            sp.wait_ge(r_out0.made, NG)
            sp.dma_start(slot0[2][:], w_e0[2]).then_inc(d_e0[2], 16)
            for e in range(3, EXPERTS):
                sp.wait_ge(down0, e - 2)
                sp.dma_start(slot0[e % 3][:], w_e0[e]).then_inc(d_e0[e % 3], 16)
                if e == 4:
                    for dst, src in ((wq1, l1_wq), (wk1, l1_wk), (wv1, l1_wv), (wo1, l1_wo)):
                        sp.dma_start(dst[:], src).then_inc(d_l1, 16)
            sp.wait_ge(down0, EXPERTS)
            sp.dma_start(wf1[:], l1_wf1).then_inc(d_ffn, 16)
            sp.dma_start(wf2[:], l1_wf2).then_inc(d_ffn, 16)
            for n in range(2):
                sp.dma_start(slot1[n][:], w_e1[n]).then_inc(d_e1[n], 16)
            with sp.Fori(0, EXPERTS // 2 - 1) as i:
                for n in range(2):
                    sp.wait_ge(down1, 2 * i + n + 1)
                    src = w_e1[bass.ds(2 * i + n + 2, 1)].rearrange("e p w -> (e p) w")
                    sp.dma_start(slot1[n][:], src).then_inc(d_e1[n], 16)
            sp.wait_ge(out_set, 3)
            sp.dma_start(out.rearrange("(k p) t -> p k t", p=P), oute[:]).then_inc(d_final, 16)
            sp.wait_ge(d_final, 16)

        def half(src, c):
            return [src[:, k, c * HALF:(c + 1) * HALF] for k in range(KD)]

        jobs0 = []
        lat = xt_b
        for c in range(2):
            jobs0.append(([(wkvd[:, k, :], half(xt_a, c)[k]) for k in range(KD)],
                          lat[:, 0, c * HALF:(c + 1) * HALF], "copy"))
        for c in range(2):
            for m in range(KH):
                jobs0.append(([(wq0[:, k, m * P:(m + 1) * P], half(xt_a, c)[k]) for k in range(KD)],
                              qt[:, m, c * HALF:(c + 1) * HALF], "copy"))
            for m in range(KH):
                jobs0.append(([(wkvu[:, m * P:(m + 1) * P], lat[:, 0, c * HALF:(c + 1) * HALF])],
                              kt[:, m, c * HALF:(c + 1) * HALF], "copy"))
        for g in range(NG):
            for n in range(2):
                jobs0.append(([(lat[:, 0, g * TG:(g + 1) * TG], wkvu[:, HD + n * BANK:HD + (n + 1) * BANK])],
                              v[0:TG, g, n * BANK:(n + 1) * BANK], "copy"))
        jobs1 = []
        for c in range(2):
            for w, dst in ((wq1, qt), (wk1, kt)):
                for m in range(KH):
                    jobs1.append(([(w[:, k, m * P:(m + 1) * P], half(xt_b, c)[k]) for k in range(KD)],
                                  dst[:, m, c * HALF:(c + 1) * HALF], "phi"))
        for g in range(NG):
            for n in range(2):
                jobs1.append(([(xt_b[:, k, g * TG:(g + 1) * TG], wv1[:, k, n * BANK:(n + 1) * BANK])
                               for k in range(KD)], v[0:TG, g, n * BANK:(n + 1) * BANK], "copy"))
        PHI = sum(kind == "phi" for _, _, kind in jobs1)

        def place(n):
            return n % 2 * 4 + n // 2

        def job_result(j, dst):
            return ps[0:dst.shape[0], j % 8, 0:dst.shape[1]]

        @block.tensor
        def _(pe):
            def rows(r, tiles, product, src, step_lag=2):
                n = len(tiles)
                for s in range(n + step_lag):
                    if s < n:
                        if s >= 4:
                            pe.wait_ge(r.added, s - 3)
                        product(s, ps[0:tiles[s][1], s % 4, 0:D]).then_inc(r.made, 1)
                    if s >= step_lag:
                        i = s - step_lag
                        pe.wait_ge(r.normed, i + 1)
                        if i >= 2:
                            pe.wait_ge(r.xt, i - 1)
                        turn(src[0:tiles[i][1], i, :], tiles[i][1], 4 + i % 2).then_inc(r.turned, 1)

            def turn(src, size, bank):
                for k in range(KD):
                    last = nc.tensor.transpose(ps[:, bank, k * P:k * P + size], src[:, k * P:(k + 1) * P],
                                               ident[0:size, 0:size])
                return last

            def projections(a, jobs, deps):
                for j, (operands, _, _) in enumerate(jobs):
                    if j in deps:
                        for s, n in deps[j]:
                            pe.wait_ge(s, n)
                    if j >= 8:
                        pe.wait_ge((a.by_act, a.by_dve)[j % 2], (j - 8) // 2 + 1)
                    n = len(operands)
                    for k, (lhs, rhs) in enumerate(operands):
                        last = nc.tensor.matmul(job_bank(j, lhs, rhs), lhs, rhs, start=(k == 0), stop=(k == n - 1))
                    last.then_inc(a.made, 1)

            def job_bank(j, lhs, rhs):
                return ps[0:lhs.shape[1], j % 8, 0:rhs.shape[1]]

            def attention(a):
                for s in range(UNITS + LAG + 1):
                    if s < UNITS:
                        if s >= 2:
                            pe.wait_ge(a.masked, s - 1)
                        gs, hs = s * HU // HEADS, s * HU % HEADS
                        for n in range(HU):
                            m, r = (hs + n) // 2, (hs + n) % 2 * DH
                            cols = slice(gs * TG, (gs + 1) * TG)
                            last = nc.tensor.matmul(
                                ps[0:TG, 2 * (s % 2) + n % 2, n // 2 * TG:(n // 2 + 1) * TG],
                                qt[r:r + DH, m, cols], kt[r:r + DH, m, cols], start=True, stop=True)
                        last.then_inc(a.scored, 1)
                    u = s - LAG - 1
                    g, h0 = u * HU // HEADS, u * HU % HEADS
                    if u >= 0:
                        pe.wait_ge(a.pt, u + 1)
                        if u >= 1:
                            pe.wait_ge(a.y, u)
                        for n in range(HU):
                            r = n % 2 * DH
                            last = nc.tensor.matmul(
                                ps[r:r + DH, 6, n // 2 * TG:(n // 2 + 1) * TG],
                                v[0:TG, g, (h0 + n) * DH:(h0 + n + 1) * DH],
                                pt[0:TG, u % 2, place(n) * TG:(place(n) + 1) * TG], start=True, stop=True)
                        last.then_inc(a.y_made, 1)
                    u = s - LAG
                    if 0 <= u < UNITS:
                        pe.wait_ge(a.p, u + 1)
                        if u >= 1:
                            pe.wait_ge(a.pt, u)
                        for n in range(HU):
                            last = nc.tensor.transpose(
                                ps[0:TG, 4 + n // 4, (n % 4) * TG:(n % 4 + 1) * TG],
                                pm[0:TG, u % NPM, n * TG:(n + 1) * TG], ident[0:TG, 0:TG])
                        last.then_inc(a.pt_made, 1)

            def product_of(lhs, rhs, blocks, tiles):
                def product(s, dst):
                    t0, size = tiles[s]
                    for k in range(blocks):
                        last = nc.tensor.matmul(dst, lhs[:, k, t0:t0 + size], rhs[:, k, :],
                                                start=(k == 0), stop=(k == blocks - 1))
                    return last
                return product

            pe.wait_ge(d_tok, 16)

            def patch_rows(g, dst):
                c, t0 = divmod(GROUPS[g][0], HALF)
                if t0 == 0:
                    pe.wait_ge(d_pat[c], 16)
                if g == 2:
                    pe.wait_ge(d_const, 16)
                for k in range(KP):
                    last = nc.tensor.matmul(dst, pat[:, c, k, t0:t0 + TG], wtok[:, k, :],
                                            start=(k == 0), stop=(k == KP - 1))
                return last
            rows(r_tok, GROUPS, patch_rows, x)
            pe.wait_ge(r_tok.xt, NG)
            pe.wait_ge(d_qkv, 48)
            projections(a0, jobs0, {2: [(a0.by_act, 1), (a0.by_dve, 1)]})
            pe.wait_ge(a0.by_act, (len(jobs0) + 1) // 2)
            pe.wait_ge(a0.by_dve, len(jobs0) // 2)
            attention(a0)
            pe.wait_ge(a0.y, UNITS)
            pe.wait_ge(d_out0, 16)
            rows(r_out0, GROUPS, product_of(qt, wout, KH, GROUPS), x)

            pe.wait_ge(r_out0.xt, NG)
            pe.wait_ge(d_gw, 16)
            for g, (t0, size) in enumerate(GROUPS):
                for k in range(KD):
                    last = nc.tensor.matmul(ps[0:TG, 6, g * EXPERTS:(g + 1) * EXPERTS], xt_a[:, k, t0:t0 + size],
                                            gw[:, k, :], start=(k == 0), stop=(k == KD - 1))
            last.then_inc(logits0, 1)
            fresh = [True] * 3
            for g, (t0, size) in enumerate(GROUPS):
                for m in range(KD):
                    for bank, col, off, w in column_pieces(t0, size):
                        bk = bank(m)
                        last = nc.tensor.matmul(ps[:, bk, col(m):col(m) + w], h[0:TG, g, m * P:(m + 1) * P],
                                                ident[0:TG, off:off + w], start=fresh[bk], stop=False,
                                                skip_group_check=True)
                        fresh[bk] = False
            pe.wait_ge(apad_set, 1)
            for g in range(NG):
                last = nc.tensor.matmul(ps[:, 7, 0:SEQ], apad[0:TG, g * P:(g + 1) * P], const("fold", TG),
                                        start=(g == 0), stop=(g == NG - 1))
            last.then_inc(affinity_made, 1)
            pe.wait_ge(d_ready, 1)
            for n in range(2):
                last = nc.tensor.matmul(ps[0:TG, 4 + n, :], ones[:, 0:TG], d_idx[:, n * BANK:(n + 1) * BANK],
                                        start=True, stop=True)
            for n in range(2):
                last = nc.tensor.matmul(ps[:, 6, n * EXPERTS:(n + 1) * EXPERTS], d_pick[:, n, :],
                                        const("same_expert"), start=True, stop=True)
            last.then_inc(picks_made, 1)
            pe.wait_ge(onehot_set, 1)
            for g in range(NG):
                bank = 4 + g % 4
                if g >= 4:
                    pe.wait_ge((xin_act, xin_dve)[g % 2], (g - 4) // 2 + 1)
                for k in range(KD):
                    last = nc.tensor.matmul(ps[:, bank, k * P:(k + 1) * P], x[0:TG, g, k * P:(k + 1) * P],
                                            onehot[0:TG, g * P:(g + 1) * P], start=True, stop=True)
                last.then_inc(gathered, 1)
            pe.wait_ge(xin_act, NG // 2)
            pe.wait_ge(xin_dve, NG // 2)
            pe.wait_ge(spread_set, EXPERTS)

            def gate_up0(n, e, half, i=None):
                if e is None or e >= 1:
                    pe.wait_ge(hid0_set, 2 * (e if e is not None else i) + half - 1)
                for w in range(2):
                    for m in range(4):
                        for k in range(KD):
                            a = (w * KD + k) * I0 + (half * 4 + m) * P
                            rhs = (xin[:, k, e * P:(e + 1) * P] if e is not None
                                   else xin[:, k, bass.ds(i * P, P)])
                            last = nc.tensor.matmul(ps[:, 4 + 2 * half + w, m * P:(m + 1) * P],
                                                    slot0[n][:, a:a + P], rhs, start=(k == 0), stop=(k == KD - 1))
                last.then_inc(gu0, 1)

            def down_product0(n, done):
                pe.wait_ge(hid0_set, 2 * done)
                for k in range(K0):
                    a = 2 * KD * I0 + k * D
                    last = nc.tensor.matmul(ps[:, 3, 0:D], hid0[:, n, k, :], slot0[n][:, a:a + D],
                                            start=(k == 0), stop=(k == K0 - 1))
                last.then_inc(down0, 1)

            def combine0(e, done):
                pe.wait_ge(xe_set, done)
                for m in range(KD):
                    for bank, col, off, w in column_pieces(0, TOK):
                        rhs = spread[:, e, off:off + w] if isinstance(e, int) else \
                            spread[:].rearrange("p e t -> p (e t)")[:, bass.ds(e * TOK + off, w)]
                        last = nc.tensor.matmul(ps[:, bank(m), col(m):col(m) + w], xe[:, m * P:(m + 1) * P],
                                                rhs, start=False, stop=False, skip_group_check=True)
                last.then_inc(comb0, 1)

            pe.wait_ge(d_e0[0], 16)
            gate_up0(0, 0, 0)
            gate_up0(0, 0, 1)
            with pe.Fori(0, 2) as i:
                for n in (1, 2, 0):
                    e = 3 * i + (n if n else 3)
                    pe.wait_ge(d_e0[n], 16 * i + (16 if n else 32))
                    gate_up0(n, None, 0, e)
                    down_product0((n + 2) % 3, e)
                    gate_up0(n, None, 1, e)
                    combine0(e - 1, e)
            pe.wait_ge(d_e0[1], 16 * 3)
            gate_up0(1, EXPERTS - 1, 0)
            down_product0(0, EXPERTS - 1)
            gate_up0(1, EXPERTS - 1, 1)
            combine0(EXPERTS - 2, EXPERTS - 1)
            down_product0(1, EXPERTS)
            combine0(EXPERTS - 1, EXPERTS)

            def h2_rows(s, dst):
                if s == 0:
                    pe.wait_ge(h2t_set, 3)
                t0, size = TILES[s]
                for k in range(KD):
                    last = nc.tensor.transpose(dst[:, k * P:(k + 1) * P], xt_a[:, k, t0:t0 + size], ident)
                return last
            rows(r_mid, TILES, h2_rows, nrm)

            pe.wait_ge(r_mid.xt, NT)
            pe.wait_ge(d_l1, 64)
            projections(a1, jobs1, {})
            pe.wait_ge(a1.by_act, (len(jobs1) + 1) // 2)
            pe.wait_ge(a1.by_dve, len(jobs1) // 2)
            attention(a1)
            pe.wait_ge(a1.y, UNITS)
            rows(r_out1, TILES, product_of(qt, wo1, KH, TILES), nrm)

            pe.wait_ge(r_out1.xt, NT)
            pe.wait_ge(d_ffn, 32)
            for j in range(2 * KF):
                c, m = j // KF, j % KF
                if j >= 8:
                    pe.wait_ge(ffn_act, j - 7)
                for k in range(KD):
                    last = nc.tensor.matmul(ps[:, j % 8, 0:HALF], wf1[:, k, m * P:(m + 1) * P],
                                            xt_a[:, k, c * HALF:(c + 1) * HALF], start=(k == 0), stop=(k == KD - 1))
                last.then_inc(ffn_made, 1)
            pe.wait_ge(ffn_act, 2 * KF)
            rows(r_ffn, TILES, product_of(ft, wf2, KF, TILES), xn1)

            pe.wait_ge(r_ffn.added, NT)
            for i, (t0, size) in enumerate(TILES):
                pe.wait_ge(s_set, i + 1)
                if i == 4:
                    pe.wait_ge(st_set, 1)
                turn(s_sum[0:size, i, :], size, i % 4).then_inc(s_turned, 1)
            pe.wait_ge(r_ffn.xt, NT)
            pe.wait_ge(d_par, 32)
            for i, (t0, size) in enumerate(TILES):
                for k in range(KD):
                    last = nc.tensor.matmul(ps[0:size, 6, i * EXPERTS:(i + 1) * EXPERTS], xt_b[:, k, t0:t0 + size],
                                            rw[:, k, :], start=(k == 0), stop=(k == KD - 1))
            last.then_inc(logits1, 1)

            def gate_up1(n, e, c, m, i=None):
                j = c * K1 + m
                if e is None or 8 * e + j >= 2:
                    pe.wait_ge(ug_set, 8 * (e if e is not None else i) + j - 1)
                    pe.wait_ge(silu1, 8 * (e if e is not None else i) + j - 1)
                for w in range(2):
                    for k in range(KD):
                        a = k * 2 * I1 + w * I1 + m * P
                        last = nc.tensor.matmul(ps[:, 4 + 2 * (j % 2) + w, 0:HALF], slot1[n][:, a:a + P],
                                                xt_b[:, k, c * HALF:(c + 1) * HALF],
                                                start=(k == 0), stop=(k == KD - 1))
                last.then_inc(gu1, 1)

            def down_product1(n, done, first=False):
                pe.wait_ge(hid1_set, 8 * done)
                fresh = [first] * 3
                for m in range(KD):
                    for k in range(K1):
                        a = KD * 2 * I1 + k * D + m * P
                        for bank, col, off, w in column_pieces(0, TOK):
                            last = nc.tensor.matmul(ps[:, bank(m), col(m):col(m) + w], slot1[n][:, a:a + P],
                                                    hid1[:, n, k, off:off + w], start=fresh[bank(m)], stop=False,
                                                    skip_group_check=True)
                            fresh[bank(m)] = False
                last.then_inc(down1, 1)

            pe.wait_ge(gates_set, 1)
            for i, (t0, size) in enumerate(TILES):
                last = nc.tensor.transpose(ps[0:EXPERTS, 6 + i // 4, t0 % BANK:t0 % BANK + size],
                                           g_rows[0:size, 0, i * EXPERTS:(i + 1) * EXPERTS], ident[0:size, 0:size])
            last.then_inc(gt_made, 1)
            pe.wait_ge(gt_set, 2)
            pe.wait_ge(st_set, NT)
            for e in range(EXPERTS):
                if e >= 2:
                    pe.wait_ge(gbc_set, e - 1)
                sel = ident[0:EXPERTS, e:e + 1].broadcast_to([EXPERTS, P])
                for c in range(2):
                    last = nc.tensor.matmul(ps[:, 2 * (e % 2) + c, 0:HALF], sel,
                                            gt[0:EXPERTS, c * HALF:(c + 1) * HALF], start=True, stop=True)
                last.then_inc(gbc_made, 1)
            pe.wait_ge(gbc_set, EXPERTS)
            blocks = [(c, m) for c in range(2) for m in range(K1)]
            pe.wait_ge(d_e1[0], 16)
            for c, m in blocks:
                gate_up1(0, 0, c, m)
            pe.wait_ge(d_e1[1], 16)
            for c, m in blocks[0:4]:
                gate_up1(1, 1, c, m)
            down_product1(0, 1, first=True)
            for c, m in blocks[4:8]:
                gate_up1(1, 1, c, m)
            with pe.Fori(1, EXPERTS // 2) as i:
                for n in range(2):
                    e = 2 * i + n
                    pe.wait_ge(d_e1[n], 16 * i + 16)
                    for c, m in blocks[0:4]:
                        gate_up1(n, None, c, m, e)
                    down_product1(1 - n, e)
                    for c, m in blocks[4:8]:
                        gate_up1(n, None, c, m, e)
            down_product1(1, EXPERTS)

        @block.scalar
        def _(act):
            def turned(r, tiles, dst, gain=None, bias=None):
                for i, (t0, size) in enumerate(tiles):
                    act.wait_ge(r.turned, i + 1)
                    src = ps[:, 4 + i % 2, 0:KD * P].rearrange("p (k n) -> p k n", k=KD)[:, :, 0:size]
                    if gain is None:
                        last = nc.scalar.activation(dst[:, :, t0:t0 + size], src, ACT.Copy)
                    for k in range(KD if gain is not None else 0):
                        if bias is None:
                            last = nc.scalar.activation(dst[:, k, t0:t0 + size], src[:, k, :], ACT.Copy,
                                                        scale=par[:, k, gain:gain + 1])
                        else:
                            last = nc.scalar.activation(dst[:, k, t0:t0 + size], src[:, k, :], ACT.Identity,
                                                        scale=par[:, k, gain:gain + 1],
                                                        bias=par[:, k, bias:bias + 1])
                    last.then_inc(r.xt, 1)

            def attention(a, softmax):
                for s in range(UNITS + LAG + 1):
                    u = s - LAG - 1
                    if u >= 0:
                        g, m0 = u * HU // HEADS, u * HU % HEADS // 2
                        act.wait_ge(a.y_made, u + 1)
                        nc.scalar.activation(
                            qt[:, m0:m0 + HU // 2, g * TG:(g + 1) * TG],
                            ps[:, 6, 0:4 * TG].rearrange("p (m n) -> p m n", m=4), ACT.Copy).then_inc(a.y, 1)
                    if softmax and 1 <= s <= UNITS:
                        w = s - 1
                        act.wait_ge(a.shifted, w + 1)
                        nc.scalar.activation(pm[0:TG, w % NPM, :], pm[0:TG, w % NPM, :], ACT.Exp).then_inc(a.expd, 1)
                    u = s - LAG
                    if 0 <= u < UNITS:
                        act.wait_ge(a.pt_made, u + 1)
                        if u >= 2:
                            act.wait_ge(a.y_made, u - 1)
                        nc.scalar.activation(
                            pt[0:TG, u % 2, :].rearrange("p (b n) -> p b n", b=2),
                            ps[0:TG, 4:6, 0:4 * TG], ACT.Copy).then_inc(a.pt, 1)

            turned(r_tok, GROUPS, xt_a)
            for j in range(0, len(jobs0), 2):
                act.wait_ge(a0.made, j + 1)
                dst = jobs0[j][1]
                nc.scalar.activation(dst, job_result(j, dst), ACT.Copy).then_inc(a0.by_act, 1)
            attention(a0, True)
            turned(r_out0, GROUPS, xt_a)
            act.wait_ge(shifted0, 1)
            nc.scalar.activation(rsm[0:TG, 1, :], rsm[0:TG, 0, :], ACT.Exp).then_inc(exped0, 1)

            def xin_view(g, k):
                return xin[:, k, :].rearrange("p (e b j) -> p b e j", e=EXPERTS, b=IMAGES)[:, 2 * g:2 * g + 2]

            for g in range(0, NG, 2):
                act.wait_ge(gathered, g + 1)
                for k in range(KD):
                    last = nc.scalar.activation(
                        xin_view(g, k), ps[:, 4 + g % 4, k * P:(k + 1) * P].rearrange(
                            "p (b e j) -> p b e j", b=2, e=EXPERTS), ACT.Copy)
                last.then_inc(xin_act, 1)

            for half_ in range(2):
                act.wait_ge(gu0, half_ + 1)
                nc.scalar.activation(sg0[:, half_, :], ps[:, 4 + 2 * half_, :], ACT.Silu).then_inc(silu0, 1)
            with act.Fori(1, EXPERTS) as e:
                for half_ in range(2):
                    act.wait_ge(gu0, 2 * e + half_ + 1)
                    act.wait_ge(hid0_set, 2 * e + half_ - 1)
                    nc.scalar.activation(sg0[:, half_, :], ps[:, 4 + 2 * half_, :], ACT.Silu).then_inc(silu0, 1)

            act.wait_ge(comb0, EXPERTS)
            for n in range(2):
                nc.scalar.activation(xt_a[:, n, 0:BANK], ps[:, n, :], ACT.Copy).then_inc(h2t_set, 1)
            nc.scalar.activation(xt_a[:, :, BANK:TOK],
                                 ps[:, 2, 0:2 * (TOK - BANK)].rearrange("p (m n) -> p m n", m=2),
                                 ACT.Copy).then_inc(h2t_set, 1)
            act.wait_ge(d_par, 32)
            turned(r_mid, TILES, xt_b, GAIN1, BIAS1)

            for j in range(len(jobs1)):
                _, dst, kind = jobs1[j]
                if kind == "phi":
                    act.wait_ge(a1.made, j + 1)
                    if j >= 4:
                        act.wait_ge((a1.by_act, a1.by_dve)[j % 2], (j - 4) // 2 + 1)
                    nc.scalar.activation(phi[:, j % 4, 0, :], job_result(j, dst), ACT.Relu,
                                         scale=-1.0).then_inc(a1.relu, 1)
                    act.wait_ge(a1.relu, j + 1)
                    nc.scalar.activation(phi[:, j % 4, 1, :], phi[:, j % 4, 0, :], ACT.Exp,
                                         scale=-1.0).then_inc(a1.expd, 1)
                elif j % 2 == 0:
                    act.wait_ge(a1.made, j + 1)
                    if j == PHI:
                        act.wait_ge(a1.by_act, j // 2)
                    nc.scalar.activation(dst, job_result(j, dst), ACT.Copy).then_inc(a1.by_act, 1)
            attention(a1, False)
            turned(r_out1, TILES, xt_a, GAIN2, BIAS2)
            for j in range(2 * KF):
                c, m = j // KF, j % KF
                act.wait_ge(ffn_made, j + 1)
                nc.scalar.activation(ft[:, m, c * HALF:(c + 1) * HALF], ps[:, j % 8, 0:HALF],
                                     ACT.Gelu).then_inc(ffn_act, 1)
            turned(r_ffn, TILES, xt_b, NSCALE)
            for i, (t0, size) in enumerate(TILES):
                act.wait_ge(s_turned, i + 1)
                src = ps[:, i % 4, 0:KD * P].rearrange("p (k n) -> p k n", k=KD)[:, :, 0:size]
                nc.scalar.activation(st[:, :, t0:t0 + size], src, ACT.Copy).then_inc(st_set, 1)
            act.wait_ge(diff1, 1)
            nc.scalar.activation(picks[:, 3, 0:NT], picks[:, 2, 0:NT], ACT.Exp).then_inc(exped1, 1)
            for e in range(EXPERTS):
                act.wait_ge(gbc_made, e + 1)
                nc.scalar.activation(gbc[:, e, :].rearrange("p (c n) -> p c n", c=2),
                                     ps[:, 2 * (e % 2):2 * (e % 2) + 2, 0:HALF], ACT.Copy).then_inc(gbc_set, 1)

            def silus1(i, first):
                for j in range(8):
                    act.wait_ge(gu1, 8 * i + j + 1)
                    if not first or j >= 4:
                        act.wait_ge(hid1_set, 8 * i + j - 3)
                    nc.scalar.activation(sg1[:, j % 4, :], ps[:, 5 + 2 * (j % 2), 0:HALF],
                                         ACT.Silu).then_inc(silu1, 1)
            silus1(0, True)
            with act.Fori(1, EXPERTS) as i:
                silus1(i, False)

        @block.vector
        def _(dve):
            steps = [0]

            def link(ins):
                steps[0] += 1
                ins.then_inc(dve_step, 1)
                dve.wait_ge(dve_step, steps[0])

            def moments(src, size, s_, o=0, rms=False):
                link(nc.vector.bn_stats(s_[0:size, 0:6], src))
                link(nc.vector.bn_aggr(s_[0:size, 6:8], s_[0:size, 0:6]))
                if rms:
                    link(nc.vector.tensor_tensor(s_[0:size, 10:11], s_[0:size, 6:7], s_[0:size, 6:7], ALU.mult))
                    return nc.vector.scalar_tensor_tensor(s_[0:size, 8:9], s_[0:size, 7:8], EPS_RMS,
                                                          s_[0:size, 10:11], ALU.add, ALU.add)
                return nc.vector.tensor_scalar(s_[0:size, 8:9], s_[0:size, 7:8], EPS_LN, None, ALU.add)

            def normalise(dst, src, size, s_):
                return nc.vector.tensor_scalar(dst, src, s_[0:size, 6:7], s_[0:size, 9:10], ALU.subtract, ALU.mult)

            def rows(r, tiles, dst, addend, normed, s_):
                n = len(tiles)
                for s in range(n + 1):
                    if s < n:
                        size = tiles[s][1]
                        dve.wait_ge(r.made, s + 1)
                        nc.vector.tensor_tensor(dst[0:size, s, :], ps[0:size, s % 4, 0:D], addend(s, size),
                                                ALU.add).then_inc(r.added, 1)
                        dve.wait_ge(r.added, s + 1)
                        moments(dst[0:size, s, :], size, s_[:, s, :]).then_inc(r.var, 1)
                    if s >= 1:
                        i, size = s - 1, tiles[s - 1][1]
                        dve.wait_ge(r.rstd, i + 1)
                        normalise(normed[0:size, i, :], dst[0:size, i, :], size, s_[:, i, :]).then_inc(r.normed, 1)

            def attention(a, softmax):
                mask = const("addmask" if softmax else "mulmask", TG)
                for s in range(UNITS + 1):
                    if s < UNITS:
                        b = s % NPM
                        probs = pm[0:TG, b, :]
                        probs3 = probs.rearrange("p (h t) -> p h t", h=HU)
                        dve.wait_ge(a.scored, s + 1)
                        if s >= NPM:
                            dve.wait_ge(a.pt_made, s - NPM + 1)
                        for n in range(2):
                            dst = probs3[:, 4 * n:4 * n + 4, :]
                            src = ps[0:TG, 2 * (s % 2) + n, 0:4 * TG].rearrange("p (h t) -> p h t", h=4)
                            over = mask.unsqueeze(1).broadcast_to([TG, 4, TG])
                            if softmax:
                                last = nc.vector.scalar_tensor_tensor(dst, src, SCALE, over, ALU.mult, ALU.add)
                            else:
                                last = nc.vector.tensor_tensor(dst, src, over, ALU.mult)
                        last.then_inc(a.masked, 1)
                        dve.wait_ge(a.masked, s + 1)
                        if softmax:
                            nc.vector.tensor_reduce(att_small[0:TG, 0, b, 0, :], probs3, AXX, ALU.max)\
                                .then_inc(a.maxed, 1)
                        else:
                            link(nc.vector.tensor_reduce(att_small[0:TG, 1, b, 0, :], probs3, AXX, ALU.add))
                            link(nc.vector.tensor_scalar(att_small[0:TG, 1, b, 1, :], att_small[0:TG, 1, b, 0, :],
                                                         EPS_DEN, None, ALU.max))
                            nc.vector.reciprocal(att_small[0:TG, 1, b, 2, :], att_small[0:TG, 1, b, 1, :])\
                                .then_inc(a.summed, 1)
                    if softmax and s >= 1:
                        b = (s - 1) % NPM
                        dve.wait_ge(a.expd, s)
                        link(nc.vector.tensor_reduce(att_small[0:TG, 0, b, 1, :],
                                                     pm[0:TG, b, :].rearrange("p (h t) -> p h t", h=HU), AXX, ALU.add))
                        nc.vector.reciprocal(att_small[0:TG, 0, b, 2, :], att_small[0:TG, 0, b, 1, :])\
                            .then_inc(a.summed, 1)

            nc.vector.memset(ones[:], 1.0).then_inc(consts_set, 1)
            dve.wait_ge(d_add, 32)
            link(nc.vector.tensor_tensor(addp[0:TG, 0, :], addp[0:TG, 0, :], addp[0:TG, 1, :], ALU.add))
            rows(r_tok, GROUPS, h, lambda s, n: addp[0:TG, 0, :], x, stat[0])
            for j in range(1, len(jobs0), 2):
                dve.wait_ge(a0.made, j + 1)
                dst = jobs0[j][1]
                nc.vector.tensor_copy(dst, job_result(j, dst)).then_inc(a0.by_dve, 1)
            dve.wait_ge(d_const, 16)
            attention(a0, True)
            rows(r_out0, GROUPS, h, lambda s, n: h[0:n, s, :], x, stat[1])

            link(nc.vector.memset(apad[:], 0.0))
            dve.wait_ge(logits0, 1)
            lg = ps[0:TG, 6, 0:64].rearrange("p (g e) -> p g e", g=NG)
            r3 = [rsm[0:TG, n, :].rearrange("p (g e) -> p g e", g=NG) for n in range(4)]
            small = aff[0:TG, 0:8]
            small2 = aff[0:TG, 8:16]
            link(nc.vector.tensor_reduce(small, lg, AXX, ALU.max))
            nc.vector.tensor_tensor(r3[0], lg, small.unsqueeze(2).broadcast_to([TG, NG, EXPERTS]),
                                    ALU.subtract).then_inc(shifted0, 1)
            dve.wait_ge(exped0, 1)
            link(nc.vector.tensor_reduce(small, r3[1], AXX, ALU.add))
            link(nc.vector.reciprocal(small2, small))
            link(nc.vector.tensor_tensor(r3[2], r3[1], small2.unsqueeze(2).broadcast_to([TG, NG, EXPERTS]), ALU.mult))
            which = const("which", TG)
            diag = apad[0:TG, :].rearrange("p (g r) -> p g r", g=NG)[:, :, 0:2 * EXPERTS]
            for n in range(2):
                last = nc.vector.tensor_scalar(diag[:, :, n * EXPERTS:(n + 1) * EXPERTS], r3[2],
                                               which[:, n:n + 1], None, ALU.mult)
            last.then_inc(apad_set, 1)
            dve.wait_ge(affinity_made, 1)
            affs = aff[:, 16:16 + SEQ]
            top, idf = picks[:, 0, 0:PICKS], picks[:, 1, 0:PICKS]
            link(nc.vector.tensor_copy(affs, ps[:, 7, 0:SEQ]))
            link(nc.vector.max(top, affs))
            link(nc.vector.max_index(idx_u[:, 0, :], top, affs))
            link(nc.vector.tensor_copy(idf, idx_u[:, 0, :]))
            loc, glo = picks[:, 2, 0:PICKS], picks[:, 3, 0:PICKS]
            link(nc.vector.tensor_scalar(loc, idf, const("base_local"), None, ALU.add))
            link(nc.vector.tensor_scalar(glo, idf, const("base_global"), None, ALU.add))
            for n, val in enumerate((glo, top)):
                nc.vector.tensor_tensor(d_pick[:, n, :].rearrange("p (b j) -> p b j", b=IMAGES),
                                        const("same_image").unsqueeze(2).broadcast_to([P, IMAGES, PICKS]),
                                        val.unsqueeze(1).broadcast_to([P, IMAGES, PICKS]), ALU.mult)
            nc.vector.tensor_tensor(d_idx[:].rearrange("p (c j) -> p c j", c=P),
                                    ident.unsqueeze(2).broadcast_to([P, P, PICKS]),
                                    loc.unsqueeze(1).broadcast_to([P, P, PICKS]), ALU.mult).then_inc(d_ready, 1)
            dve.wait_ge(picks_made, 1)
            nc.vector.tensor_copy(picks[:, 4, 0:2 * EXPERTS], ps[:, 6, 0:2 * EXPERTS]).then_inc(pick_cols, 1)
            row = const("row", TG)
            nc.vector.tensor_scalar(onehot[0:TG, :].rearrange("p (b n) -> p b n", b=2), ps[0:TG, 4:6, :],
                                    row, None, ALU.is_equal).then_inc(onehot_set, 1)
            for g in range(1, NG, 2):
                dve.wait_ge(gathered, g + 1)
                for k in range(KD):
                    last = nc.vector.tensor_copy(
                        xin[:, k, :].rearrange("p (e b j) -> p b e j", e=EXPERTS, b=IMAGES)[:, 2 * g:2 * g + 2],
                        ps[:, 4 + g % 4, k * P:(k + 1) * P].rearrange("p (b e j) -> p b e j", b=2, e=EXPERTS))
                last.then_inc(xin_dve, 1)
            dve.wait_ge(pick_cols, 1)

            for e in range(EXPERTS + 1):
                for half_ in range(2):
                    if e < EXPERTS:
                        dve.wait_ge(silu0, 2 * e + half_ + 1)
                        if e >= 3:
                            dve.wait_ge(down0, e - 2)
                        nc.vector.tensor_tensor(
                            hid0[:, e % 3, 4 * half_:4 * half_ + 4, :].rearrange("p k t -> p (k t)"),
                            sg0[:, half_, :], ps[:, 5 + 2 * half_, :], ALU.mult).then_inc(hid0_set, 1)
                    if e >= 1 and half_ == 0:
                        dve.wait_ge(down0, e)
                        nc.vector.tensor_scalar(xe[:], ps[:, 3, 0:D],
                                                picks[:, 4, EXPERTS + e - 1:EXPERTS + e], None, ALU.mult)\
                            .then_inc(xe_set, 1)

            for s in range(NT + 2):
                if s < NT:
                    size = TILES[s][1]
                    dve.wait_ge(r_mid.made, s + 1)
                    nc.vector.tensor_copy(h2[0:size, s, :], ps[0:size, s % 4, 0:D]).then_inc(r_mid.added, 1)
                    dve.wait_ge(r_mid.added, s + 1)
                    moments(h2[0:size, s, :], size, stat[2][:, s, :]).then_inc(r_mid.var, 1)
                if 1 <= s <= NT:
                    i, size = s - 1, TILES[s - 1][1]
                    dve.wait_ge(r_mid.rstd, i + 1)
                    link(normalise(z[0:size, i, :], h2[0:size, i, :], size, stat[2][:, i, :]))
                    moments(z[0:size, i, :], size, stat[3][:, i, :]).then_inc(r_mid.var2, 1)
                if s >= 2:
                    i, size = s - 2, TILES[s - 2][1]
                    dve.wait_ge(r_mid.rstd2, i + 1)
                    normalise(nrm[0:size, i, :], z[0:size, i, :], size, stat[3][:, i, :]).then_inc(r_mid.normed, 1)
            for j, (_, dst, kind) in enumerate(jobs1):
                done = (a1.by_act, a1.by_dve)[j % 2]
                if kind == "phi":
                    dve.wait_ge(a1.expd, j + 1)
                    nc.vector.scalar_tensor_tensor(dst, job_result(j, dst), 1.0, phi[:, j % 4, 1, :],
                                                   ALU.add, ALU.max).then_inc(done, 1)
                elif j % 2 == 1:
                    dve.wait_ge(a1.made, j + 1)
                    nc.vector.tensor_copy(dst, job_result(j, dst)).then_inc(done, 1)
            attention(a1, False)
            rows(r_out1, TILES, z, lambda s, n: z[0:n, s, :], nrm, stat[4])
            for s in range(NT + 2):
                if s < NT:
                    size = TILES[s][1]
                    dve.wait_ge(r_ffn.made, s + 1)
                    nc.vector.tensor_tensor(z[0:size, s, :], ps[0:size, s % 4, 0:D], z[0:size, s, :],
                                            ALU.add).then_inc(r_ffn.added, 1)
                    dve.wait_ge(r_ffn.added, s + 1)
                    link(nc.vector.tensor_tensor(h2[0:size, s, :], z[0:size, s, :], h2[0:size, s, :], ALU.add))
                    moments(h2[0:size, s, :], size, stat[5][:, s, :]).then_inc(r_ffn.var, 1)
                if 1 <= s <= NT:
                    i, size = s - 1, TILES[s - 1][1]
                    dve.wait_ge(r_ffn.rstd, i + 1)
                    link(normalise(w_rows[0:size, i, :], h2[0:size, i, :], size, stat[5][:, i, :]))
                    nc.vector.tensor_tensor(s_sum[0:size, i, :], w_rows[0:size, i, :], h2[0:size, i, :],
                                            ALU.add).then_inc(s_set, 1)
                    moments(w_rows[0:size, i, :], size, stat[0][:, i, :], rms=True).then_inc(r_ffn.var2, 1)
                if s >= 2:
                    i, size = s - 2, TILES[s - 2][1]
                    dve.wait_ge(r_ffn.rstd2, i + 1)
                    nc.vector.tensor_scalar(xn1[0:size, i, :], w_rows[0:size, i, :], stat[0][0:size, i, 9:10],
                                            None, ALU.mult).then_inc(r_ffn.normed, 1)
            sc = g_rows[:, 1, :]
            link(nc.vector.memset(sc, 0.0))
            dve.wait_ge(logits1, 1)
            last_size = TILES[-1][1]
            nc.vector.tensor_copy(sc[:, 0:(NT - 1) * 8], ps[:, 6, 0:(NT - 1) * 8])
            link(nc.vector.tensor_copy(sc[0:last_size, (NT - 1) * 8:NT * 8], ps[0:last_size, 6, (NT - 1) * 8:NT * 8]))
            tops = picks[:, 0, :].rearrange("p (i n) -> p i n", i=NT)
            sc3 = sc.rearrange("p (i n) -> p i n", i=NT)
            for i in range(NT):
                last = nc.vector.max(tops[:, i, :], sc3[:, i, :])
            link(last)
            for i in range(NT):
                last = nc.vector.max_index(idx_u[:, i, :], tops[:, i, :], sc3[:, i, :])
            link(last)
            idf1 = picks[:, 1, :].rearrange("p (i n) -> p i n", i=NT)
            link(nc.vector.tensor_copy(idf1, idx_u[:]))
            nc.vector.tensor_tensor(picks[:, 2, 0:NT], tops[:, :, 1], tops[:, :, 0], ALU.subtract).then_inc(diff1, 1)
            dve.wait_ge(exped1, 1)
            link(nc.vector.tensor_scalar(picks[:, 4, 0:NT], picks[:, 3, 0:NT], 1.0, None, ALU.add))
            link(nc.vector.reciprocal(picks[:, 5, 0:NT], picks[:, 4, 0:NT]))
            link(nc.vector.tensor_tensor(picks[:, 5, 8:8 + NT], picks[:, 5, 0:NT], picks[:, 3, 0:NT], ALU.mult))
            shape = [P, NT, EXPERTS]
            ge = [g_rows[:, n, :].rearrange("p (i n) -> p i n", i=NT) for n in range(4)]
            for n in range(2):
                link(nc.vector.tensor_tensor(ge[2 + n], const("experts").unsqueeze(1).broadcast_to(shape),
                                             idf1[:, :, n:n + 1].broadcast_to(shape), ALU.is_equal))
                weight = picks[:, 5, 8 * n:8 * n + NT].unsqueeze(2).broadcast_to(shape)
                link(nc.vector.tensor_tensor(ge[2 + n], ge[2 + n], weight, ALU.mult))
            nc.vector.tensor_tensor(ge[0], ge[2], ge[3], ALU.add).then_inc(gates_set, 1)
            dve.wait_ge(gt_made, 1)
            nc.vector.tensor_copy(gt[0:EXPERTS, 0:BANK], ps[0:EXPERTS, 6, 0:BANK]).then_inc(gt_set, 1)
            nc.vector.tensor_copy(gt[0:EXPERTS, BANK:TOK], ps[0:EXPERTS, 7, 0:TOK - BANK]).then_inc(gt_set, 1)
            dve.wait_ge(gbc_set, EXPERTS)

            def gated_up(i, first):
                for j in range(8):
                    c = j // K1
                    dve.wait_ge(gu1, 8 * i + j + 1)
                    if not first or j >= 4:
                        dve.wait_ge(hid1_set, 8 * i + j - 3)
                    nc.vector.tensor_tensor(ug1[:, j % 4, :], ps[:, 4 + 2 * (j % 2), 0:HALF],
                                            gbc[:].rearrange("p e t -> p (e t)")[:, bass.ds(i * TOK + c * HALF, HALF)],
                                            ALU.mult).then_inc(ug_set, 1)
            gated_up(0, True)
            with dve.Fori(1, EXPERTS) as i:
                gated_up(i, False)
            dve.wait_ge(down1, EXPERTS)
            for m in range(KD):
                nc.vector.tensor_tensor(oute[:, m, 0:BANK], ps[:, m, :], st[:, m, 0:BANK], ALU.add)\
                    .then_inc(out_set, 1)
            nc.vector.tensor_tensor(oute[:, :, BANK:TOK],
                                    ps[:, 2, 0:2 * (TOK - BANK)].rearrange("p (m n) -> p m n", m=2),
                                    st[:, :, BANK:TOK], ALU.add).then_inc(out_set, 1)

        @block.gpsimd
        def _(pool):
            nc.gpsimd.memset(neg_half[:], -0.5).then_inc(consts_set, 1)
            pool.wait_ge(consts_set, 2)

            def roots(var, rstd, tiles, s_):
                for i, (_, size) in enumerate(tiles):
                    root(i, size, var, rstd, s_)

            def root(i, size, var, rstd, s_):
                pool.wait_ge(var, i + 1)
                nc.gpsimd.tensor_tensor(s_[0:size, i, 9:10], s_[0:size, i, 8:9], neg_half[0:size, :],
                                        ALU.pow).then_inc(rstd, 1)

            def attention(a, softmax):
                shape = [TG, HU, TG]
                for s in range(UNITS + 2):
                    if s >= 2:
                        b = (s - 2) % NPM
                        p3 = pm[0:TG, b, :].rearrange("p (h t) -> p h t", h=HU)
                        pool.wait_ge(a.summed, s - 1)
                        nc.gpsimd.tensor_tensor(p3, p3, att_small[0:TG, 0 if softmax else 1, b, 2, :].unsqueeze(2)
                                                .broadcast_to(shape), ALU.mult).then_inc(a.p, 1)
                    if softmax and s < UNITS:
                        p3 = pm[0:TG, s % NPM, :].rearrange("p (h t) -> p h t", h=HU)
                        pool.wait_ge(a.maxed, s + 1)
                        nc.gpsimd.tensor_tensor(p3, p3, att_small[0:TG, 0, s % NPM, 0, :].unsqueeze(2)
                                                .broadcast_to(shape), ALU.subtract).then_inc(a.shifted, 1)

            roots(r_tok.var, r_tok.rstd, GROUPS, stat[0])
            attention(a0, True)
            roots(r_out0.var, r_out0.rstd, GROUPS, stat[1])
            pool.wait_ge(pick_cols, 1)
            for e in range(EXPERTS):
                nc.gpsimd.tensor_scalar(spread[:, e, :], const("tokens"), picks[:, 4, e:e + 1], None,
                                        ALU.is_equal).then_inc(spread_set, 1)

            def two(r, s_a, s_b):
                for s in range(NT + 1):
                    if s < NT:
                        root(s, TILES[s][1], r.var, r.rstd, s_a)
                    if s >= 1:
                        root(s - 1, TILES[s - 1][1], r.var2, r.rstd2, s_b)
            two(r_mid, stat[2], stat[3])
            attention(a1, False)
            roots(r_out1.var, r_out1.rstd, TILES, stat[4])
            two(r_ffn, stat[5], stat[0])

            def hidden1(i, n, first=False):
                for j in range(8):
                    c, m = j // K1, j % K1
                    pool.wait_ge(silu1, 8 * i + j + 1)
                    pool.wait_ge(ug_set, 8 * i + j + 1)
                    if not first:
                        pool.wait_ge(down1, i - 1)
                    nc.gpsimd.tensor_tensor(hid1[:, n, m, c * HALF:(c + 1) * HALF], ug1[:, j % 4, :],
                                            sg1[:, j % 4, :], ALU.mult).then_inc(hid1_set, 1)
            hidden1(0, 0, True)
            hidden1(1, 1, True)
            with pool.Fori(1, EXPERTS // 2) as i:
                for n in range(2):
                    hidden1(2 * i + n, n)


def _constants():
    import numpy as np
    c = np.zeros((P, NCONST), np.float32)
    p = np.arange(P)

    def put(name, value):
        a, b = CONST[name]
        c[0:value.shape[0], a:b] = value
    t = np.arange(TG)
    seen = (t[:, None] // SEQ == t[None, :] // SEQ) & (t[None, :] <= t[:, None])
    put("ident", np.eye(P))
    put("addmask", np.where(seen, 0.0, MASKED))
    put("mulmask", np.where(seen, 1.0, 0.0))
    put("same_image", p[:, None] // EXPERTS == np.arange(IMAGES)[None, :])
    put("same_expert", p[:, None] % EXPERTS == np.arange(EXPERTS)[None, :])
    put("fold", t[:, None] % SEQ == np.arange(SEQ)[None, :])
    put("which", t[:, None] // SEQ == np.arange(2)[None, :])
    put("row", p[:, None])
    put("base_local", SEQ * (p[:, None] // EXPERTS % 2))
    put("base_global", SEQ * (p[:, None] // EXPERTS))
    put("tokens", np.broadcast_to(np.arange(TOK)[None, :], (P, TOK)))
    put("experts", np.broadcast_to(np.arange(EXPERTS)[None, :], (P, EXPERTS)))
    return c


def kernel(**inputs):
    import numpy as np
    import concourse.bacc as _bacc
    from concourse import mybir as _mybir
    from concourse.bass_utils import run_bass_kernel_spmd as _run

    a = {k: np.asarray(v) for k, v in inputs.items()}
    f = np.float32

    def blocks(w):
        return np.ascontiguousarray(w.reshape(-1, P, w.shape[-1]).transpose(1, 0, 2))

    n, c, hh, ww = a["x"].shape
    ph = 16
    side = hh // ph
    pt = a["x"].reshape(n, c, side, ph, side, ph).transpose(1, 3, 5, 0, 2, 4).reshape(PD, n, side * side)
    patches = np.zeros((PD, n, SEQ), a["x"].dtype)
    patches[:, :, 1:] = pt
    cls, pos = a["L0_tok_cls_token"][0], a["L0_tok_pos_embed"][0]
    add_a = np.concatenate([pos, pos], 0)
    one = np.concatenate([cls, np.broadcast_to(a["L0_tok_b"][None, :], (SEQ - 1, D))], 0)
    add_b = np.concatenate([one, one], 0)
    kvd = blocks(a["L0_attn_w_kv_down"])
    E = EXPERTS
    e0 = np.concatenate(
        [a["L0_ffn_w_gate"].transpose(0, 2, 1).reshape(E, KD, P, I0).transpose(0, 2, 1, 3).reshape(E, P, KD * I0),
         a["L0_ffn_w_up"].transpose(0, 2, 1).reshape(E, KD, P, I0).transpose(0, 2, 1, 3).reshape(E, P, KD * I0),
         a["L0_ffn_w_down"].transpose(0, 2, 1).reshape(E, K0, P, D).transpose(0, 2, 1, 3).reshape(E, P, K0 * D)], 2)
    e1 = np.concatenate(
        [a["L1_ffn_w_up"].transpose(0, 2, 1).reshape(E, KD, P, 2 * I1).transpose(0, 2, 1, 3).reshape(E, P, -1),
         a["L1_ffn_w_down"].transpose(0, 2, 1).reshape(E, K1, P, D).transpose(0, 2, 1, 3).reshape(E, P, K1 * D)], 2)
    params = np.stack([a["L1_attn_ln1_g"], a["L1_attn_ln1_b"], a["L1_attn_ln2_g"], a["L1_attn_ln2_b"],
                       a["L1_ffn_norm_scale"]], 1)
    arrays = {
        "patches": blocks(patches.reshape(PD, TOK)).reshape(P, KP, 2, HALF).transpose(2, 0, 1, 3), "tok_w": blocks(a["L0_tok_W"].T),
        "add_a": add_a, "add_b": add_b,
        "w_q": blocks(a["L0_attn_w_q"]), "w_kvd": kvd, "w_kvu": a["L0_attn_w_kv_up"],
        "w_out": blocks(a["L0_attn_w_out"]), "gate_w": blocks(a["L0_ffn_gate_w"].T), "w_e0": e0,
        "l1_wq": blocks(a["L1_attn_Wq"]), "l1_wk": blocks(a["L1_attn_Wk"]), "l1_wv": blocks(a["L1_attn_Wv"]),
        "l1_wo": blocks(a["L1_attn_Wo"]), "l1_wf1": blocks(a["L1_attn_Wf1"]), "l1_wf2": blocks(a["L1_attn_Wf2"]),
        "params": blocks(params), "router": blocks(a["L1_ffn_w_router"].T), "w_e1": e1,
        "consts": _constants(),
    }
    arrays = {k: np.ascontiguousarray(v) for k, v in arrays.items()}
    nc = _bacc.Bacc("TRN2", target_bir_lowering=False, num_devices=1)
    args = [nc.dram_tensor(k, v.shape, _mybir.dt.from_np(v.dtype), kind="ExternalInput").ap()
            for k, v in arrays.items()]
    args.append(nc.dram_tensor("out_t", (D, TOK), F32, kind="ExternalOutput").ap())
    vit_tower(nc, *args)
    r = _run(nc, [arrays], core_ids=[0])
    got = r.results[0]["out_t"]
    return np.ascontiguousarray(got.reshape(D, IMAGES, SEQ).transpose(1, 2, 0))
```

```python
from contextlib import ExitStack

import concourse.bass as bass
from concourse import mybir

ALU = mybir.AluOpType
ACT = mybir.ActivationFunctionType
AXX = mybir.AxisListType.X
F32 = mybir.dt.float32
U32 = mybir.dt.uint32

P = 128
IMAGES, D, SEQ = 16, 256, 37
TOK = IMAGES * SEQ
KD = D // P
NG, TG = IMAGES // 2, 2 * SEQ
GROUPS = [(TG * g, TG) for g in range(NG)]
TILES = [(t, min(P, TOK - t)) for t in range(0, TOK, P)]
NT = len(TILES)
HALF = TOK // 2
PD = 768
KP = PD // P
HEADS, DH = 16, 64
HD = HEADS * DH
KH = HD // P
RANK = 128
HU = 8
UNITS = NG * HEADS // HU
LAG = 3
NPM = LAG + 1
EXPERTS = 8
PICKS = SEQ // EXPERTS * 2
I0 = 1024
K0 = I0 // P
I1 = 512
K1 = I1 // P
DF = 1024
KF = DF // P
BLOCKS = (2 * TOK + EXPERTS * (P - 1)) // P
EPS_LN, EPS_RMS, EPS_DEN = 1e-5, 1e-6, 1e-6
SCALE = DH ** -0.5
MASKED = -1e30
W0 = 2 * KD * I0 + K0 * D
W1 = KD * 2 * I1 + K1 * D
BANK = 512

CONST = {}
_at = 0
for _name, _width in [("ident", P), ("addmask", TG), ("mulmask", TG), ("same_image", IMAGES),
                      ("same_expert", EXPERTS), ("fold", SEQ), ("which", 2), ("row", 1),
                      ("base_local", 1), ("base_global", 1), ("tokens", TOK), ("experts", EXPERTS),
                      ("before", P)]:
    CONST[_name] = (_at, _at + _width)
    _at += _width
NCONST = _at
GAIN1, BIAS1, GAIN2, BIAS2, NSCALE = range(5)


def column_pieces(t0, n):
    out = []
    if t0 < BANK:
        w = min(n, BANK - t0)
        out.append((lambda m: m, lambda m: t0, 0, w))
    if t0 + n > BANK:
        a = max(t0, BANK)
        out.append((lambda m: 2, lambda m: a - BANK + m * (TOK - BANK), a - t0, t0 + n - a))
    return out


def vit_tower(nc, patches, tok_w, add_a, add_b, w_q, w_kvd, w_kvu, w_out, gate_w, w_e0,
              l1_wq, l1_wk, l1_wv, l1_wo, l1_wf1, l1_wf2, params, router, w_e1, consts, out):
    with ExitStack() as ctx:
        base = (nc.sbuf_base + 31) // 32 * 32
        end = nc.sbuf_usable_end

        def put(name, shape, offset, dt=F32):
            size = 4
            for n in shape[1:]:
                size *= n
            return nc.alloc_sbuf_tensor_at(name, shape, dt, offset=offset), offset + (size + 31) // 32 * 32

        def sem(name):
            return ctx.enter_context(nc.semaphore(name))

        at = base
        cst, at = put("cst", [P, NCONST], at)
        ones, at = put("ones", [P, P], at)
        neg_half, at = put("neg_half", [P, 1], at)
        par, at = put("par", [P, KD, 5], at)
        gw, at = put("gw", [P, KD, EXPERTS], at)
        rw, at = put("rw", [P, KD, EXPERTS], at)
        stat = []
        for n in range(6):
            s_, at = put(f"stat{n}", [P, 8, 12], at)
            stat.append(s_)
        att_small, at = put("att_small", [P, 2, NPM, 3, HU], at)
        rsm, at = put("rsm", [P, 4, 8 * 8], at)
        idx_u, at = put("idx_u", [P, NT, 8], at, U32)
        picks, at = put("picks", [P, 6, NT * 8], at)
        g_rows, at = put("g_rows", [P, 4, NT * 8], at)
        rows_at = at
        h, at = put("h", [P, NG, D], at)
        x, at = put("x", [P, NG, D], at)
        h2, r_ = put("h2", [P, NT, D], rows_at)
        z, r_ = put("z", [P, NT, D], r_)
        nrm, r_ = put("nrm", [P, NT, D], r_)
        assert r_ <= at
        xt_a, at = put("xt_a", [P, KD, TOK], at)
        xt_b, at = put("xt_b", [P, KD, TOK], at)
        rank, at = put("rank", [P, 6, NT * EXPERTS], at)
        pos, at = put("pos", [P, 2, NT], at, U32)
        bounds, at = put("bounds", [P, 2, EXPERTS], at, mybir.dt.int32)
        B = at
        qt, at = put("qt", [P, KH, TOK], at)
        kt, at = put("kt", [P, KH, TOK], at)
        v, at = put("v", [P, NG, HD], at)
        pm, at = put("pm", [P, NPM, HU * TG], at)
        pt, at = put("pt", [P, 2, HU * TG], at)
        B_end = at
        b = B
        apad, b = put("apad", [P, NG * (P + 16)], b)
        d_idx, b = put("d_idx", [P, P * PICKS], b)
        onehot, b = put("onehot", [P, P * PICKS], b)
        d_pick, b = put("d_pick", [P, 2, P], b)
        aff, b = put("aff", [P, 64], b)
        xin, b = put("xin", [P, KD, EXPERTS * P], b)
        spread, b = put("spread", [P, EXPERTS, TOK], b)
        hid0, b = put("hid0", [P, 3, K0, P], b)
        sg0, b = put("sg0", [P, 2, BANK], b)
        xe, b = put("xe", [P, D], b)
        slot2_at = b
        assert b + W0 * 4 <= B_end, (b + W0 * 4, B_end)
        b = B
        xblk, b = put("xblk", [P, D], B + 32 * 1024)
        xbt, b = put("xbt", [P, KD, P], b)
        hid1, b = put("hid1", [P, K1, P], b)
        sg1, b = put("sg1", [P, 2, 2 * P], b)
        yblk, b = put("yblk", [P, D], b)
        picked, b = put("picked", [P, 2, NT, D], b)
        orow, b = put("orow", [P, NT, D], b)
        assert b <= B + 64 * 1024
        b = B + 64 * 1024
        s_sum, b = put("s_sum", [P, NT, D], b)
        xn1, b = put("xn1", [P, NT, D], b)
        w_rows, b = put("w_rows", [P, NT, D], b)
        assert b <= B_end
        ft, b = put("ft", [P, KF, TOK], B)
        zeros, _ = put("zeros", [P, BLOCKS + 2, D], B + KH * TOK * 2 * 4)
        phi, b = put("phi", [P, 4, 2, HALF], B + (KH * TOK * 2 + NG * HD) * 4)
        assert b <= B_end
        at = B_end
        C = at
        wq0, c_ = put("wq0", [P, KD, HD], C)
        wkvd, c_ = put("wkvd", [P, KD, RANK], c_)
        wkvu, c_ = put("wkvu", [P, 2 * HD], c_)
        wout, c_ = put("wout", [P, KH, D], c_)
        wq1, at = put("wq1", [P, KD, HD], C)
        wk1, at = put("wk1", [P, KD, HD], at)
        wv1, at = put("wv1", [P, KD, HD], at)
        wo1, at = put("wo1", [P, KH, D], at)
        at = max(at, c_)
        E = at
        slot0 = []
        for n in range(2):
            s_, at = put(f"slot0_{n}", [P, W0], at)
            slot0.append(s_)
        slot0.append(put("slot0_2", [P, W0], slot2_at)[0])
        E1 = E + W0 * 4
        assert at <= end, (at, end)
        pat, e_ = put("pat", [P, 2, KP, HALF], E1)
        wtok, e_ = put("wtok", [P, KP, D], e_)
        assert e_ <= at
        slot1 = []
        e_ = E
        for n in range(4):
            s_, e_ = put(f"slot1_{n}", [P, W1], e_)
            slot1.append(s_)
        assert e_ <= at and E + 2 * W1 * 4 == E1
        wf1, e_ = put("wf1", [P, KD, DF], E1)
        wf2, e_ = put("wf2", [P, KF, D], e_)
        assert e_ <= at
        addp, _ = put("addp", [P, 2, D], B)

        ps = ctx.enter_context(nc.psum_tensor("ps", [P, 8, BANK], F32))

        def const(name, rows=P):
            a, z_ = CONST[name]
            return cst[0:rows, a:z_]

        ident = const("ident")

        d_const, d_par = sem("d_const"), sem("d_par")
        d_add, d_tok, d_qkv, d_out0, d_gw = sem("d_add"), sem("d_tok"), sem("d_qkv"), sem("d_out0"), sem("d_gw")
        d_pat = [sem("d_pat_0"), sem("d_pat_1")]
        d_e0 = [sem(f"d_e0_{n}") for n in range(3)]
        d_e1 = [sem(f"d_e1_{n}") for n in range(4)]
        d_l1, d_ffn, d_final = sem("d_l1"), sem("d_ffn"), sem("d_final")
        consts_set = sem("consts_set")
        dve_step = sem("dve_step")

        class Rows:
            def __init__(self, name):
                self.made, self.added = sem(name + "_made"), sem(name + "_added")
                self.var, self.rstd = sem(name + "_var"), sem(name + "_rstd")
                self.var2, self.rstd2 = sem(name + "_var2"), sem(name + "_rstd2")
                self.normed, self.turned, self.xt = sem(name + "_normed"), sem(name + "_turned"), sem(name + "_xt")
        r_tok, r_out0, r_mid, r_out1, r_ffn = [Rows(n) for n in ("tok", "out0", "mid", "out1", "ffn")]

        class Att:
            def __init__(self, name):
                self.made = sem(name + "_proj")
                self.by_act, self.by_dve = sem(name + "_by_act"), sem(name + "_by_dve")
                self.relu = sem(name + "_relu")
                self.scored, self.masked, self.maxed = sem(name + "_scored"), sem(name + "_masked"), sem(name + "_maxed")
                self.shifted, self.expd, self.summed = sem(name + "_shifted"), sem(name + "_expd"), sem(name + "_summed")
                self.p, self.pt_made, self.pt = sem(name + "_p"), sem(name + "_pt_made"), sem(name + "_pt")
                self.y_made, self.y = sem(name + "_y_made"), sem(name + "_y")
                self.v_made, self.v = sem(name + "_v_made"), sem(name + "_v")
        a0, a1 = Att("a0"), Att("a1")

        logits0, shifted0, exped0 = sem("logits0"), sem("shifted0"), sem("exped0")
        apad_set, affinity_made, d_ready, picks_made, onehot_set = (
            sem("apad_set"), sem("affinity_made"), sem("d_ready"), sem("picks_made"), sem("onehot_set"))
        gathered, xin_act, xin_dve, pick_cols, spread_set = (
            sem("gathered"), sem("xin_act"), sem("xin_dve"), sem("pick_cols"), sem("spread_set"))
        gu0, silu0, hid0_set, down0, xe_set, comb0 = (
            sem("gu0"), sem("silu0"), sem("hid0_set"), sem("down0"), sem("xe_set"), sem("comb0"))
        h2t_set = sem("h2t_set")
        ffn_made, ffn_act = sem("hidden_made"), sem("hidden_act")
        s_set, zeros_set, d_zeroed = sem("s_set"), sem("zeros_set"), sem("d_zeroed")
        logits1, diff1, exped1, chosen_set, ranked, bounds_set = (
            sem("logits1"), sem("diff1"), sem("exped1"), sem("chosen_set"), sem("ranked"), sem("bounds_set"))
        d_sorted, d_xblk, x_turned, xbt_set = sem("d_sorted"), sem("d_xblk"), sem("x_turned"), sem("xbt_set")
        gu1, silu1, hid1_set, down1, y_set, d_y, pos_set, out_set = (
            sem("gu1"), sem("silu1"), sem("hid1_set"), sem("down1"), sem("y_set"), sem("d_y"), sem("pos_set"),
            sem("out_set"))
        stored = sem("stored")
        d_picked = [sem(f"d_picked_{i}") for i in range(NT)]
        xs = nc.dram_tensor("xs", ((BLOCKS + 2) * P, D), F32, kind="Internal").ap()

        block = ctx.enter_context(nc.Block())

        @block.sync
        def _(sp):
            def store_blocks(e, e_last):
                first = sp.value_load(bounds[0:1, 0, e:e + 1], min_val=0, max_val=BLOCKS)
                last = sp.value_load(bounds[0:1, 1, e_last:e_last + 1], min_val=1, max_val=BLOCKS)
                with sp.Fori(first, last) as b:
                    sp.wait_ge(y_set, b + 2)
                    sp.dma_start(xs[bass.ds(b * P, P), :], yblk[:]).then_inc(d_y, 16)
                return last

            sp.dma_start(pat[:, 0], patches[0]).then_inc(d_pat[0], 16)
            sp.dma_start(wtok[:], tok_w).then_inc(d_tok, 16)
            sp.dma_start(addp[0:TG, 0, :], add_a).then_inc(d_add, 16)
            sp.dma_start(addp[0:TG, 1, :], add_b).then_inc(d_add, 16)
            sp.dma_start(cst[:], consts).then_inc(d_const, 16)
            sp.dma_start(pat[:, 1], patches[1]).then_inc(d_pat[1], 16)
            sp.dma_start(wkvd[:], w_kvd).then_inc(d_qkv, 16)
            sp.dma_start(wq0[:], w_q).then_inc(d_qkv, 16)
            sp.dma_start(wkvu[:], w_kvu).then_inc(d_qkv, 16)
            sp.dma_start(wout[:], w_out).then_inc(d_out0, 16)
            sp.dma_start(gw[:], gate_w).then_inc(d_gw, 16)
            sp.dma_start(rw[:], router).then_inc(d_par, 16)
            sp.dma_start(par[:], params).then_inc(d_par, 16)
            sp.dma_start(slot0[0][:], w_e0[0]).then_inc(d_e0[0], 16)
            sp.wait_ge(zeros_set, 1)
            sp.dma_start(xs.rearrange("(n p) d -> p n d", p=P), zeros[:]).then_inc(d_zeroed, 16)
            sp.wait_ge(r_tok.made, NG)
            sp.dma_start(slot0[1][:], w_e0[1]).then_inc(d_e0[1], 16)
            sp.wait_ge(r_out0.made, NG)
            sp.dma_start(slot0[2][:], w_e0[2]).then_inc(d_e0[2], 16)
            for e in range(3, EXPERTS):
                sp.wait_ge(down0, e - 2)
                sp.dma_start(slot0[e % 3][:], w_e0[e]).then_inc(d_e0[e % 3], 16)
                if e == 4:
                    for dst, src in ((wq1, l1_wq), (wk1, l1_wk), (wv1, l1_wv), (wo1, l1_wo)):
                        sp.dma_start(dst[:], src).then_inc(d_l1, 16)
            sp.wait_ge(down0, EXPERTS)
            sp.dma_start(wf1[:], l1_wf1).then_inc(d_ffn, 16)
            sp.dma_start(wf2[:], l1_wf2).then_inc(d_ffn, 16)
            for n in range(2):
                sp.dma_start(slot1[n][:], w_e1[n]).then_inc(d_e1[n], 16)
            sp.wait_ge(r_ffn.made, NT)
            for n in range(2, 4):
                sp.dma_start(slot1[n][:], w_e1[n]).then_inc(d_e1[n], 16)
            sp.wait_ge(bounds_set, 1)
            for n in range(4):
                store_blocks(n, n)
                sp.dma_start(slot1[n][:], w_e1[n + 4]).then_inc(d_e1[n], 16)
            blocks_end = store_blocks(4, EXPERTS - 1)
            sp.wait_ge(d_y, 16 * blocks_end + 16)
            sp.sem_inc(stored, 1)
            for i in range(NT - 1):
                sp.wait_ge(out_set, i + 1)
                sp.dma_start(out[i * P:(i + 1) * P, :], orow[:, i, :]).then_inc(d_final, 16)
            sp.wait_ge(d_final, 16 * NT)

        def half(src, c):
            return [src[:, k, c * HALF:(c + 1) * HALF] for k in range(KD)]

        jobs0 = []
        lat = xt_b
        for c in range(2):
            jobs0.append(([(wkvd[:, k, :], half(xt_a, c)[k]) for k in range(KD)],
                          lat[:, 0, c * HALF:(c + 1) * HALF]))
        for c in range(2):
            for m in range(KH):
                jobs0.append(([(wq0[:, k, m * P:(m + 1) * P], half(xt_a, c)[k]) for k in range(KD)],
                              qt[:, m, c * HALF:(c + 1) * HALF]))
            for m in range(KH):
                jobs0.append(([(wkvu[:, m * P:(m + 1) * P], lat[:, 0, c * HALF:(c + 1) * HALF])],
                              kt[:, m, c * HALF:(c + 1) * HALF]))
        jobs1 = []
        for c in range(2):
            for w, dst in ((wq1, qt), (wk1, kt)):
                for m in range(KH):
                    jobs1.append(([(w[:, k, m * P:(m + 1) * P], half(xt_b, c)[k]) for k in range(KD)],
                                  dst[:, m, c * HALF:(c + 1) * HALF]))
        def values0(g, n):
            return [(lat[:, 0, g * TG:(g + 1) * TG], wkvu[:, HD + n * BANK:HD + (n + 1) * BANK])]

        def values1(g, n):
            return [(xt_b[:, k, g * TG:(g + 1) * TG], wv1[:, k, n * BANK:(n + 1) * BANK]) for k in range(KD)]

        def place(n):
            return n % 2 * 4 + n // 2

        def job_result(j, dst):
            return ps[0:dst.shape[0], j % 8, 0:dst.shape[1]]

        @block.tensor
        def _(pe):
            def rows(r, tiles, product, src, step_lag=2, first=0):
                n = len(tiles)
                for s in range(n + step_lag):
                    if first <= s < n:
                        if s >= 4:
                            pe.wait_ge(r.added, s - 3)
                        product(s, ps[0:tiles[s][1], s % 4, 0:D]).then_inc(r.made, 1)
                    if s >= step_lag:
                        i = s - step_lag
                        pe.wait_ge(r.normed, i + 1)
                        if i >= 2:
                            pe.wait_ge(r.xt, i - 1)
                        turn(src[0:tiles[i][1], i, :], tiles[i][1], 4 + i % 2).then_inc(r.turned, 1)

            def turn(src, size, bank):
                for k in range(KD):
                    last = nc.tensor.transpose(ps[:, bank, k * P:k * P + size], src[:, k * P:(k + 1) * P],
                                               ident[0:size, 0:size])
                return last

            def projections(a, jobs, deps):
                for j, (operands, _) in enumerate(jobs):
                    if j in deps:
                        for s, n in deps[j]:
                            pe.wait_ge(s, n)
                    if j >= 8:
                        pe.wait_ge((a.by_act, a.by_dve)[j % 2], (j - 8) // 2 + 1)
                    n = len(operands)
                    for k, (lhs, rhs) in enumerate(operands):
                        last = nc.tensor.matmul(job_bank(j, lhs, rhs), lhs, rhs, start=(k == 0), stop=(k == n - 1))
                    last.then_inc(a.made, 1)

            def job_bank(j, lhs, rhs):
                return ps[0:lhs.shape[1], j % 8, 0:rhs.shape[1]]

            def attention(a, values, out_rows, tiles, product):
                for s in range(UNITS + LAG + 1):
                    if s < UNITS:
                        if s >= 1:
                            pe.wait_ge(a.v, s)
                        operands = values(s * HU // HEADS, s * HU % HEADS // HU)
                        for k, (lhs, rhs) in enumerate(operands):
                            last = nc.tensor.matmul(ps[0:TG, 7, :], lhs, rhs, start=(k == 0),
                                                    stop=(k == len(operands) - 1))
                        last.then_inc(a.v_made, 1)
                        if s >= 2:
                            pe.wait_ge(a.masked, s - 1)
                        gs, hs = s * HU // HEADS, s * HU % HEADS
                        for n in range(HU):
                            m, r = (hs + n) // 2, (hs + n) % 2 * DH
                            cols = slice(gs * TG, (gs + 1) * TG)
                            last = nc.tensor.matmul(
                                ps[0:TG, 2 * (s % 2) + n % 2, n // 2 * TG:(n // 2 + 1) * TG],
                                qt[r:r + DH, m, cols], kt[r:r + DH, m, cols], start=True, stop=True)
                        last.then_inc(a.scored, 1)
                    u = s - LAG - 1
                    g, h0 = u * HU // HEADS, u * HU % HEADS
                    if u >= 0:
                        pe.wait_ge(a.pt, u + 1)
                        pe.wait_ge(a.v, 2 * g + 2)
                        if u >= 1:
                            pe.wait_ge(a.y, u)
                        for n in range(HU):
                            r = n % 2 * DH
                            last = nc.tensor.matmul(
                                ps[r:r + DH, 6, n // 2 * TG:(n // 2 + 1) * TG],
                                v[0:TG, g, (h0 + n) * DH:(h0 + n + 1) * DH],
                                pt[0:TG, u % 2, place(n) * TG:(place(n) + 1) * TG], start=True, stop=True)
                        last.then_inc(a.y_made, 1)
                    u = s - LAG
                    if 0 <= u < UNITS:
                        pe.wait_ge(a.p, u + 1)
                        if u >= 1:
                            pe.wait_ge(a.pt, u)
                        for n in range(HU):
                            last = nc.tensor.transpose(
                                ps[0:TG, 4 + n // 4, (n % 4) * TG:(n % 4 + 1) * TG],
                                pm[0:TG, u % NPM, n * TG:(n + 1) * TG], ident[0:TG, 0:TG])
                        last.then_inc(a.pt_made, 1)
                    i = s - UNITS
                    if i >= 0:
                        pe.wait_ge(a.masked, UNITS - 1 + i // 2 if i < 2 else UNITS)
                        pe.wait_ge(a.y, units_before(sum(tiles[i])))
                        product(i, ps[0:tiles[i][1], i, 0:D]).then_inc(out_rows.made, 1)

            def units_before(token):
                return -(-token // TG) * (HEADS // HU)

            def product_of(lhs, rhs, blocks, tiles):
                def product(s, dst):
                    t0, size = tiles[s]
                    for k in range(blocks):
                        last = nc.tensor.matmul(dst, lhs[:, k, t0:t0 + size], rhs[:, k, :],
                                                start=(k == 0), stop=(k == blocks - 1))
                    return last
                return product

            pe.wait_ge(d_tok, 16)

            def patch_rows(g, dst):
                c, t0 = divmod(GROUPS[g][0], HALF)
                if t0 == 0:
                    pe.wait_ge(d_pat[c], 16)
                if g == 2:
                    pe.wait_ge(d_const, 16)
                for k in range(KP):
                    last = nc.tensor.matmul(dst, pat[:, c, k, t0:t0 + TG], wtok[:, k, :],
                                            start=(k == 0), stop=(k == KP - 1))
                return last
            rows(r_tok, GROUPS, patch_rows, x)
            pe.wait_ge(r_tok.xt, NG)
            pe.wait_ge(d_qkv, 48)
            projections(a0, jobs0, {2: [(a0.by_act, 1), (a0.by_dve, 1)]})
            pe.wait_ge(a0.by_act, (len(jobs0) + 1) // 2)
            pe.wait_ge(a0.by_dve, len(jobs0) // 2)
            pe.wait_ge(d_out0, 16)
            product = product_of(qt, wout, KH, GROUPS)
            attention(a0, values0, r_out0, GROUPS, product)
            pe.wait_ge(a0.y, UNITS)
            rows(r_out0, GROUPS, product, x, first=LAG + 1)

            pe.wait_ge(r_out0.xt, NG)
            pe.wait_ge(d_gw, 16)
            for g, (t0, size) in enumerate(GROUPS):
                for k in range(KD):
                    last = nc.tensor.matmul(ps[0:TG, 6, g * EXPERTS:(g + 1) * EXPERTS], xt_a[:, k, t0:t0 + size],
                                            gw[:, k, :], start=(k == 0), stop=(k == KD - 1))
            last.then_inc(logits0, 1)
            fresh = [True] * 3
            for g, (t0, size) in enumerate(GROUPS):
                for m in range(KD):
                    for bank, col, off, w in column_pieces(t0, size):
                        bk = bank(m)
                        last = nc.tensor.matmul(ps[:, bk, col(m):col(m) + w], h[0:TG, g, m * P:(m + 1) * P],
                                                ident[0:TG, off:off + w], start=fresh[bk], stop=False,
                                                skip_group_check=True)
                        fresh[bk] = False
            pe.wait_ge(apad_set, 1)
            for g in range(NG):
                last = nc.tensor.matmul(ps[:, 7, 0:SEQ], apad[0:TG, g * P:(g + 1) * P], const("fold", TG),
                                        start=(g == 0), stop=(g == NG - 1))
            last.then_inc(affinity_made, 1)
            pe.wait_ge(d_ready, 1)
            for n in range(2):
                last = nc.tensor.matmul(ps[0:TG, 4 + n, :], ones[:, 0:TG], d_idx[:, n * BANK:(n + 1) * BANK],
                                        start=True, stop=True)
            for n in range(2):
                last = nc.tensor.matmul(ps[:, 6, n * EXPERTS:(n + 1) * EXPERTS], d_pick[:, n, :],
                                        const("same_expert"), start=True, stop=True)
            last.then_inc(picks_made, 1)
            pe.wait_ge(onehot_set, 1)
            for g in range(NG):
                bank = 4 + g % 4
                if g >= 4:
                    pe.wait_ge((xin_act, xin_dve)[g % 2], (g - 4) // 2 + 1)
                for k in range(KD):
                    last = nc.tensor.matmul(ps[:, bank, k * P:(k + 1) * P], x[0:TG, g, k * P:(k + 1) * P],
                                            onehot[0:TG, g * P:(g + 1) * P], start=True, stop=True)
                last.then_inc(gathered, 1)
            pe.wait_ge(xin_act, NG // 2)
            pe.wait_ge(xin_dve, NG // 2)

            def gate_up0(n, e, half, i=None):
                if e is None or e >= 1:
                    pe.wait_ge(hid0_set, 2 * (e if e is not None else i) + half - 1)
                for w in range(2):
                    for m in range(4):
                        for k in range(KD):
                            a = (w * KD + k) * I0 + (half * 4 + m) * P
                            rhs = (xin[:, k, e * P:(e + 1) * P] if e is not None
                                   else xin[:, k, bass.ds(i * P, P)])
                            last = nc.tensor.matmul(ps[:, 4 + 2 * half + w, m * P:(m + 1) * P],
                                                    slot0[n][:, a:a + P], rhs, start=(k == 0), stop=(k == KD - 1))
                last.then_inc(gu0, 1)

            def down_product0(n, done):
                pe.wait_ge(hid0_set, 2 * done)
                for k in range(K0):
                    a = 2 * KD * I0 + k * D
                    last = nc.tensor.matmul(ps[:, 3, 0:D], hid0[:, n, k, :], slot0[n][:, a:a + D],
                                            start=(k == 0), stop=(k == K0 - 1))
                last.then_inc(down0, 1)

            def combine0(e, done):
                pe.wait_ge(xe_set, done)
                for m in range(KD):
                    for bank, col, off, w in column_pieces(0, TOK):
                        rhs = spread[:, e, off:off + w] if isinstance(e, int) else \
                            spread[:].rearrange("p e t -> p (e t)")[:, bass.ds(e * TOK + off, w)]
                        last = nc.tensor.matmul(ps[:, bank(m), col(m):col(m) + w], xe[:, m * P:(m + 1) * P],
                                                rhs, start=False, stop=False, skip_group_check=True)
                last.then_inc(comb0, 1)

            pe.wait_ge(d_e0[0], 16)
            gate_up0(0, 0, 0)
            gate_up0(0, 0, 1)
            pe.wait_ge(spread_set, EXPERTS)
            with pe.Fori(0, 2) as i:
                for n in (1, 2, 0):
                    e = 3 * i + (n if n else 3)
                    pe.wait_ge(d_e0[n], 16 * i + (16 if n else 32))
                    gate_up0(n, None, 0, e)
                    down_product0((n + 2) % 3, e)
                    gate_up0(n, None, 1, e)
                    combine0(e - 1, e)
            pe.wait_ge(d_e0[1], 16 * 3)
            gate_up0(1, EXPERTS - 1, 0)
            down_product0(0, EXPERTS - 1)
            gate_up0(1, EXPERTS - 1, 1)
            combine0(EXPERTS - 2, EXPERTS - 1)
            down_product0(1, EXPERTS)
            combine0(EXPERTS - 1, EXPERTS)

            def h2_rows(s, dst):
                if s == 0:
                    pe.wait_ge(h2t_set, 3)
                t0, size = TILES[s]
                for k in range(KD):
                    last = nc.tensor.transpose(dst[:, k * P:(k + 1) * P], xt_a[:, k, t0:t0 + size], ident)
                return last
            rows(r_mid, TILES, h2_rows, nrm)

            pe.wait_ge(r_mid.xt, NT)
            pe.wait_ge(d_l1, 64)
            projections(a1, jobs1, {})
            pe.wait_ge(a1.by_act, (len(jobs1) + 1) // 2)
            pe.wait_ge(a1.by_dve, len(jobs1) // 2)
            product = product_of(qt, wo1, KH, TILES)
            attention(a1, values1, r_out1, TILES, product)
            pe.wait_ge(a1.y, UNITS)
            rows(r_out1, TILES, product, nrm, first=LAG + 1)

            pe.wait_ge(r_out1.xt, NT)
            pe.wait_ge(d_ffn, 32)
            for j in range(2 * KF):
                c, m = j // KF, j % KF
                if j >= 8:
                    pe.wait_ge(ffn_act, j - 7)
                for k in range(KD):
                    last = nc.tensor.matmul(ps[:, j % 8, 0:HALF], wf1[:, k, m * P:(m + 1) * P],
                                            xt_a[:, k, c * HALF:(c + 1) * HALF], start=(k == 0), stop=(k == KD - 1))
                last.then_inc(ffn_made, 1)
            pe.wait_ge(ffn_act, 2 * KF)
            rows(r_ffn, TILES, product_of(ft, wf2, KF, TILES), xn1)

            pe.wait_ge(r_ffn.xt, NT)
            pe.wait_ge(d_par, 32)
            for i, (t0, size) in enumerate(TILES):
                for k in range(KD):
                    last = nc.tensor.matmul(ps[0:size, 6, i * EXPERTS:(i + 1) * EXPERTS], xt_b[:, k, t0:t0 + size],
                                            rw[:, k, :], start=(k == 0), stop=(k == KD - 1))
            last.then_inc(logits1, 1)

            pe.wait_ge(chosen_set, 1)
            for i in range(NT):
                for f in range(i + 1):
                    k = TILES[f][1]
                    last = nc.tensor.matmul(ps[:, 4, i * EXPERTS:(i + 1) * EXPERTS],
                                            (const("before") if f == i else ones)[0:k, :],
                                            rank[0:k, 2, f * EXPERTS:(f + 1) * EXPERTS], start=(f == 0), stop=(f == i))
            for f in range(NT):
                k = TILES[f][1]
                last = nc.tensor.matmul(ps[:, 5, 0:EXPERTS], ones[0:k, :], rank[0:k, 2, f * EXPERTS:(f + 1) * EXPERTS],
                                        start=(f == 0), stop=(f == NT - 1))
            last.then_inc(ranked, 1)

            def turn_block(landed):
                pe.wait_ge(d_xblk, landed)
                turn(xblk, P, 2).then_inc(x_turned, 1)

            pe.wait_ge(bounds_set, 1)
            turn_block(16)
            with pe.Fori(0, EXPERTS // 4) as i:
                for n in range(4):
                    first = pe.value_load(bounds[0:1, 0, bass.ds(4 * i + n, 1)], min_val=0, max_val=BLOCKS)
                    end = pe.value_load(bounds[0:1, 1, bass.ds(4 * i + n, 1)], min_val=1, max_val=BLOCKS)
                    with pe.Fori(first, end) as b:
                        pe.wait_ge(d_e1[n], 16 * i + 16)
                        pe.wait_ge(xbt_set, b + 1)
                        for half_ in range(2):
                            for w in range(2):
                                for m in range(2):
                                    for k in range(KD):
                                        a = k * 2 * I1 + w * I1 + (2 * half_ + m) * P
                                        last = nc.tensor.matmul(ps[:, 4 + 2 * half_ + w, m * P:(m + 1) * P],
                                                                slot1[n][:, a:a + P], xbt[:, k, :],
                                                                start=(k == 0), stop=(k == KD - 1))
                            last.then_inc(gu1, 1)
                        turn_block(16 * b + 32)
                        pe.wait_ge(y_set, b + 1)
                        for k in range(K1):
                            if k % 2 == 0:
                                pe.wait_ge(hid1_set, 2 * b + 1 + k // 2)
                            a = KD * 2 * I1 + k * D
                            last = nc.tensor.matmul(ps[:, 0, 0:D], hid1[:, k, :], slot1[n][:, a:a + D],
                                                    start=(k == 0), stop=(k == K1 - 1))
                        last.then_inc(down1, 1)

        @block.scalar
        def _(act):
            def turned(r, tiles, dst, gain=None, bias=None):
                for i, (t0, size) in enumerate(tiles):
                    act.wait_ge(r.turned, i + 1)
                    src = ps[:, 4 + i % 2, 0:KD * P].rearrange("p (k n) -> p k n", k=KD)[:, :, 0:size]
                    if gain is None:
                        last = nc.scalar.activation(dst[:, :, t0:t0 + size], src, ACT.Copy)
                    for k in range(KD if gain is not None else 0):
                        if bias is None:
                            last = nc.scalar.activation(dst[:, k, t0:t0 + size], src[:, k, :], ACT.Copy,
                                                        scale=par[:, k, gain:gain + 1])
                        else:
                            last = nc.scalar.activation(dst[:, k, t0:t0 + size], src[:, k, :], ACT.Identity,
                                                        scale=par[:, k, gain:gain + 1],
                                                        bias=par[:, k, bias:bias + 1])
                    last.then_inc(r.xt, 1)

            def attention(a, softmax):
                for s in range(UNITS + LAG + 1):
                    if s < UNITS:
                        g, n = s * HU // HEADS, s * HU % HEADS // HU
                        act.wait_ge(a.v_made, s + 1)
                        nc.scalar.activation(v[0:TG, g, n * BANK:(n + 1) * BANK], ps[0:TG, 7, :],
                                             ACT.Copy).then_inc(a.v, 1)
                    u = s - LAG - 1
                    if u >= 0:
                        g, m0 = u * HU // HEADS, u * HU % HEADS // 2
                        act.wait_ge(a.y_made, u + 1)
                        nc.scalar.activation(
                            qt[:, m0:m0 + HU // 2, g * TG:(g + 1) * TG],
                            ps[:, 6, 0:4 * TG].rearrange("p (m n) -> p m n", m=4), ACT.Copy).then_inc(a.y, 1)
                    if softmax and 1 <= s <= UNITS:
                        w = s - 1
                        act.wait_ge(a.shifted, w + 1)
                        nc.scalar.activation(pm[0:TG, w % NPM, :], pm[0:TG, w % NPM, :], ACT.Exp).then_inc(a.expd, 1)
                    u = s - LAG
                    if 0 <= u < UNITS:
                        act.wait_ge(a.pt_made, u + 1)
                        if u >= 2:
                            act.wait_ge(a.y_made, u - 1)
                        nc.scalar.activation(
                            pt[0:TG, u % 2, :].rearrange("p (b n) -> p b n", b=2),
                            ps[0:TG, 4:6, 0:4 * TG], ACT.Copy).then_inc(a.pt, 1)

            turned(r_tok, GROUPS, xt_a)
            act.wait_ge(d_zeroed, 16)
            for j in range(0, len(jobs0), 2):
                act.wait_ge(a0.made, j + 1)
                dst = jobs0[j][1]
                nc.scalar.activation(dst, job_result(j, dst), ACT.Copy).then_inc(a0.by_act, 1)
            attention(a0, True)
            turned(r_out0, GROUPS, xt_a)
            act.wait_ge(shifted0, 1)
            nc.scalar.activation(rsm[0:TG, 1, :], rsm[0:TG, 0, :], ACT.Exp).then_inc(exped0, 1)

            def xin_view(g, k):
                return xin[:, k, :].rearrange("p (e b j) -> p b e j", e=EXPERTS, b=IMAGES)[:, 2 * g:2 * g + 2]

            for g in range(0, NG, 2):
                act.wait_ge(gathered, g + 1)
                for k in range(KD):
                    last = nc.scalar.activation(
                        xin_view(g, k), ps[:, 4 + g % 4, k * P:(k + 1) * P].rearrange(
                            "p (b e j) -> p b e j", b=2, e=EXPERTS), ACT.Copy)
                last.then_inc(xin_act, 1)

            for half_ in range(2):
                act.wait_ge(gu0, half_ + 1)
                nc.scalar.activation(sg0[:, half_, :], ps[:, 4 + 2 * half_, :], ACT.Silu).then_inc(silu0, 1)
            with act.Fori(1, EXPERTS) as e:
                for half_ in range(2):
                    act.wait_ge(gu0, 2 * e + half_ + 1)
                    act.wait_ge(hid0_set, 2 * e + half_ - 1)
                    nc.scalar.activation(sg0[:, half_, :], ps[:, 4 + 2 * half_, :], ACT.Silu).then_inc(silu0, 1)

            act.wait_ge(comb0, EXPERTS)
            for n in range(2):
                nc.scalar.activation(xt_a[:, n, 0:BANK], ps[:, n, :], ACT.Copy).then_inc(h2t_set, 1)
            nc.scalar.activation(xt_a[:, :, BANK:TOK],
                                 ps[:, 2, 0:2 * (TOK - BANK)].rearrange("p (m n) -> p m n", m=2),
                                 ACT.Copy).then_inc(h2t_set, 1)
            act.wait_ge(d_par, 32)
            turned(r_mid, TILES, xt_b, GAIN1, BIAS1)

            for j in range(len(jobs1)):
                act.wait_ge(a1.made, j + 1)
                if j >= 4:
                    act.wait_ge((a1.by_act, a1.by_dve)[j % 2], (j - 4) // 2 + 1)
                nc.scalar.activation(phi[:, j % 4, 0, :], job_result(j, jobs1[j][1]), ACT.Relu,
                                     scale=-1.0).then_inc(a1.relu, 1)
                act.wait_ge(a1.relu, j + 1)
                nc.scalar.activation(phi[:, j % 4, 1, :], phi[:, j % 4, 0, :], ACT.Exp,
                                     scale=-1.0).then_inc(a1.expd, 1)
            attention(a1, False)
            turned(r_out1, TILES, xt_a, GAIN2, BIAS2)
            for j in range(2 * KF):
                c, m = j // KF, j % KF
                act.wait_ge(ffn_made, j + 1)
                nc.scalar.activation(ft[:, m, c * HALF:(c + 1) * HALF], ps[:, j % 8, 0:HALF],
                                     ACT.Gelu).then_inc(ffn_act, 1)
            turned(r_ffn, TILES, xt_b, NSCALE)
            act.wait_ge(diff1, 1)
            nc.scalar.activation(picks[:, 3, 0:NT], picks[:, 2, 0:NT], ACT.Exp).then_inc(exped1, 1)

            def load_block(row):
                src = xs[bass.ds(row, P), :] if not isinstance(row, int) else xs[row:row + P, :]
                act.dma_start(xblk[:], src).then_inc(d_xblk, 16)

            def scaled_block():
                for k in range(KD):
                    last = nc.scalar.activation(xbt[:, k, :], ps[:, 2, k * P:(k + 1) * P], ACT.Copy,
                                                scale=par[:, k, NSCALE:NSCALE + 1])
                last.then_inc(xbt_set, 1)

            act.wait_ge(bounds_set, 1)
            act.wait_ge(d_sorted, 32 * NT)
            load_block(0)
            act.wait_ge(x_turned, 1)
            scaled_block()
            load_block(P)
            blocks_end = act.value_load(bounds[0:1, 1, EXPERTS - 1:EXPERTS], min_val=1, max_val=BLOCKS)
            with act.Fori(0, blocks_end) as b:
                for half_ in range(2):
                    act.wait_ge(gu1, 2 * b + half_ + 1)
                    nc.scalar.activation(sg1[:, half_, :], ps[:, 5 + 2 * half_, 0:2 * P], ACT.Silu).then_inc(silu1, 1)
                act.wait_ge(x_turned, b + 2)
                scaled_block()
                load_block((b + 2) * P)
            act.wait_ge(d_xblk, 16 * blocks_end + 32)
            full = (NT - 1) * P
            act.wait_ge(out_set, NT)
            act.dma_start(out[full:TOK, :], orow[0:TOK - full, NT - 1, :]).then_inc(d_final, 16)

        @block.vector
        def _(dve):
            steps = [0]

            def link(ins):
                steps[0] += 1
                ins.then_inc(dve_step, 1)
                dve.wait_ge(dve_step, steps[0])

            def moments(src, size, s_, o=0, rms=False):
                link(nc.vector.bn_stats(s_[0:size, 0:6], src))
                link(nc.vector.bn_aggr(s_[0:size, 6:8], s_[0:size, 0:6]))
                if rms:
                    link(nc.vector.tensor_tensor(s_[0:size, 10:11], s_[0:size, 6:7], s_[0:size, 6:7], ALU.mult))
                    return nc.vector.scalar_tensor_tensor(s_[0:size, 8:9], s_[0:size, 7:8], EPS_RMS,
                                                          s_[0:size, 10:11], ALU.add, ALU.add)
                return nc.vector.tensor_scalar(s_[0:size, 8:9], s_[0:size, 7:8], EPS_LN, None, ALU.add)

            def normalise(dst, src, size, s_):
                return nc.vector.tensor_scalar(dst, src, s_[0:size, 6:7], s_[0:size, 9:10], ALU.subtract, ALU.mult)

            def rows(r, tiles, dst, addend, normed, s_):
                n = len(tiles)
                for s in range(n + 1):
                    if s < n:
                        size = tiles[s][1]
                        dve.wait_ge(r.made, s + 1)
                        nc.vector.tensor_tensor(dst[0:size, s, :], ps[0:size, s % 4, 0:D], addend(s, size),
                                                ALU.add).then_inc(r.added, 1)
                        dve.wait_ge(r.added, s + 1)
                        moments(dst[0:size, s, :], size, s_[:, s, :]).then_inc(r.var, 1)
                    if s >= 1:
                        i, size = s - 1, tiles[s - 1][1]
                        dve.wait_ge(r.rstd, i + 1)
                        normalise(normed[0:size, i, :], dst[0:size, i, :], size, s_[:, i, :]).then_inc(r.normed, 1)

            def attention(a, softmax):
                mask = const("addmask" if softmax else "mulmask", TG)
                for s in range(UNITS + 1):
                    if s < UNITS:
                        b = s % NPM
                        probs = pm[0:TG, b, :]
                        probs3 = probs.rearrange("p (h t) -> p h t", h=HU)
                        dve.wait_ge(a.scored, s + 1)
                        if s >= NPM:
                            dve.wait_ge(a.pt_made, s - NPM + 1)
                        for n in range(2):
                            dst = probs3[:, 4 * n:4 * n + 4, :]
                            src = ps[0:TG, 2 * (s % 2) + n, 0:4 * TG].rearrange("p (h t) -> p h t", h=4)
                            over = mask.unsqueeze(1).broadcast_to([TG, 4, TG])
                            if softmax:
                                last = nc.vector.scalar_tensor_tensor(dst, src, SCALE, over, ALU.mult, ALU.add)
                            else:
                                last = nc.vector.tensor_tensor(dst, src, over, ALU.mult)
                        last.then_inc(a.masked, 1)
                        dve.wait_ge(a.masked, s + 1)
                        if softmax:
                            nc.vector.tensor_reduce(att_small[0:TG, 0, b, 0, :], probs3, AXX, ALU.max)\
                                .then_inc(a.maxed, 1)
                        else:
                            link(nc.vector.tensor_reduce(att_small[0:TG, 1, b, 0, :], probs3, AXX, ALU.add))
                            link(nc.vector.tensor_scalar(att_small[0:TG, 1, b, 1, :], att_small[0:TG, 1, b, 0, :],
                                                         EPS_DEN, None, ALU.max))
                            nc.vector.reciprocal(att_small[0:TG, 1, b, 2, :], att_small[0:TG, 1, b, 1, :])\
                                .then_inc(a.summed, 1)
                    if softmax and s >= 1:
                        b = (s - 1) % NPM
                        dve.wait_ge(a.expd, s)
                        link(nc.vector.tensor_reduce(att_small[0:TG, 0, b, 1, :],
                                                     pm[0:TG, b, :].rearrange("p (h t) -> p h t", h=HU), AXX, ALU.add))
                        nc.vector.reciprocal(att_small[0:TG, 0, b, 2, :], att_small[0:TG, 0, b, 1, :])\
                            .then_inc(a.summed, 1)

            nc.vector.memset(ones[:], 1.0).then_inc(consts_set, 1)
            nc.vector.memset(zeros[:], 0.0).then_inc(zeros_set, 1)
            dve.wait_ge(d_add, 32)
            link(nc.vector.tensor_tensor(addp[0:TG, 0, :], addp[0:TG, 0, :], addp[0:TG, 1, :], ALU.add))
            rows(r_tok, GROUPS, h, lambda s, n: addp[0:TG, 0, :], x, stat[0])
            dve.wait_ge(d_zeroed, 16)
            for j in range(1, len(jobs0), 2):
                dve.wait_ge(a0.made, j + 1)
                dst = jobs0[j][1]
                nc.vector.tensor_copy(dst, job_result(j, dst)).then_inc(a0.by_dve, 1)
            dve.wait_ge(d_const, 16)
            attention(a0, True)
            rows(r_out0, GROUPS, h, lambda s, n: h[0:n, s, :], x, stat[1])

            link(nc.vector.memset(apad[:], 0.0))
            dve.wait_ge(logits0, 1)
            lg = ps[0:TG, 6, 0:64].rearrange("p (g e) -> p g e", g=NG)
            r3 = [rsm[0:TG, n, :].rearrange("p (g e) -> p g e", g=NG) for n in range(4)]
            small = aff[0:TG, 0:8]
            small2 = aff[0:TG, 8:16]
            link(nc.vector.tensor_reduce(small, lg, AXX, ALU.max))
            nc.vector.tensor_tensor(r3[0], lg, small.unsqueeze(2).broadcast_to([TG, NG, EXPERTS]),
                                    ALU.subtract).then_inc(shifted0, 1)
            dve.wait_ge(exped0, 1)
            link(nc.vector.tensor_reduce(small, r3[1], AXX, ALU.add))
            link(nc.vector.reciprocal(small2, small))
            link(nc.vector.tensor_tensor(r3[2], r3[1], small2.unsqueeze(2).broadcast_to([TG, NG, EXPERTS]), ALU.mult))
            which = const("which", TG)
            diag = apad[0:TG, :].rearrange("p (g r) -> p g r", g=NG)[:, :, 0:2 * EXPERTS]
            for n in range(2):
                last = nc.vector.tensor_scalar(diag[:, :, n * EXPERTS:(n + 1) * EXPERTS], r3[2],
                                               which[:, n:n + 1], None, ALU.mult)
            last.then_inc(apad_set, 1)
            dve.wait_ge(affinity_made, 1)
            affs = aff[:, 16:16 + SEQ]
            top, idf = picks[:, 0, 0:PICKS], picks[:, 1, 0:PICKS]
            link(nc.vector.tensor_copy(affs, ps[:, 7, 0:SEQ]))
            link(nc.vector.max(top, affs))
            link(nc.vector.max_index(idx_u[:, 0, :], top, affs))
            link(nc.vector.tensor_copy(idf, idx_u[:, 0, :]))
            loc, glo = picks[:, 2, 0:PICKS], picks[:, 3, 0:PICKS]
            link(nc.vector.tensor_scalar(loc, idf, const("base_local"), None, ALU.add))
            link(nc.vector.tensor_scalar(glo, idf, const("base_global"), None, ALU.add))
            for n, val in enumerate((glo, top)):
                nc.vector.tensor_tensor(d_pick[:, n, :].rearrange("p (b j) -> p b j", b=IMAGES),
                                        const("same_image").unsqueeze(2).broadcast_to([P, IMAGES, PICKS]),
                                        val.unsqueeze(1).broadcast_to([P, IMAGES, PICKS]), ALU.mult)
            nc.vector.tensor_tensor(d_idx[:].rearrange("p (c j) -> p c j", c=P),
                                    ident.unsqueeze(2).broadcast_to([P, P, PICKS]),
                                    loc.unsqueeze(1).broadcast_to([P, P, PICKS]), ALU.mult).then_inc(d_ready, 1)
            dve.wait_ge(picks_made, 1)
            nc.vector.tensor_copy(picks[:, 4, 0:2 * EXPERTS], ps[:, 6, 0:2 * EXPERTS]).then_inc(pick_cols, 1)
            row = const("row", TG)
            nc.vector.tensor_scalar(onehot[0:TG, :].rearrange("p (b n) -> p b n", b=2), ps[0:TG, 4:6, :],
                                    row, None, ALU.is_equal).then_inc(onehot_set, 1)
            for g in range(1, NG, 2):
                dve.wait_ge(gathered, g + 1)
                for k in range(KD):
                    last = nc.vector.tensor_copy(
                        xin[:, k, :].rearrange("p (e b j) -> p b e j", e=EXPERTS, b=IMAGES)[:, 2 * g:2 * g + 2],
                        ps[:, 4 + g % 4, k * P:(k + 1) * P].rearrange("p (b e j) -> p b e j", b=2, e=EXPERTS))
                last.then_inc(xin_dve, 1)
            dve.wait_ge(pick_cols, 1)
            for e in range(EXPERTS):
                nc.vector.tensor_scalar(spread[:, e, :], const("tokens"), picks[:, 4, e:e + 1], None,
                                        ALU.is_equal).then_inc(spread_set, 1)

            for e in range(EXPERTS + 1):
                for half_ in range(2):
                    if e < EXPERTS:
                        dve.wait_ge(silu0, 2 * e + half_ + 1)
                        if e >= 3:
                            dve.wait_ge(down0, e - 2)
                        nc.vector.tensor_tensor(
                            hid0[:, e % 3, 4 * half_:4 * half_ + 4, :].rearrange("p k t -> p (k t)"),
                            sg0[:, half_, :], ps[:, 5 + 2 * half_, :], ALU.mult).then_inc(hid0_set, 1)
                    if e >= 1 and half_ == 0:
                        dve.wait_ge(down0, e)
                        nc.vector.tensor_scalar(xe[:], ps[:, 3, 0:D],
                                                picks[:, 4, EXPERTS + e - 1:EXPERTS + e], None, ALU.mult)\
                            .then_inc(xe_set, 1)

            for s in range(NT + 2):
                if s < NT:
                    size = TILES[s][1]
                    dve.wait_ge(r_mid.made, s + 1)
                    nc.vector.tensor_copy(h2[0:size, s, :], ps[0:size, s % 4, 0:D]).then_inc(r_mid.added, 1)
                    dve.wait_ge(r_mid.added, s + 1)
                    moments(h2[0:size, s, :], size, stat[2][:, s, :]).then_inc(r_mid.var, 1)
                if 1 <= s <= NT:
                    i, size = s - 1, TILES[s - 1][1]
                    dve.wait_ge(r_mid.rstd, i + 1)
                    link(normalise(z[0:size, i, :], h2[0:size, i, :], size, stat[2][:, i, :]))
                    moments(z[0:size, i, :], size, stat[3][:, i, :]).then_inc(r_mid.var2, 1)
                if s >= 2:
                    i, size = s - 2, TILES[s - 2][1]
                    dve.wait_ge(r_mid.rstd2, i + 1)
                    normalise(nrm[0:size, i, :], z[0:size, i, :], size, stat[3][:, i, :]).then_inc(r_mid.normed, 1)
            for j, (_, dst) in enumerate(jobs1):
                done = (a1.by_act, a1.by_dve)[j % 2]
                dve.wait_ge(a1.expd, j + 1)
                nc.vector.scalar_tensor_tensor(dst, job_result(j, dst), 1.0, phi[:, j % 4, 1, :],
                                               ALU.add, ALU.max).then_inc(done, 1)
            attention(a1, False)
            rows(r_out1, TILES, z, lambda s, n: z[0:n, s, :], nrm, stat[4])
            for s in range(NT + 2):
                if s < NT:
                    size = TILES[s][1]
                    dve.wait_ge(r_ffn.made, s + 1)
                    nc.vector.tensor_tensor(z[0:size, s, :], ps[0:size, s % 4, 0:D], z[0:size, s, :],
                                            ALU.add).then_inc(r_ffn.added, 1)
                    dve.wait_ge(r_ffn.added, s + 1)
                    link(nc.vector.tensor_tensor(h2[0:size, s, :], z[0:size, s, :], h2[0:size, s, :], ALU.add))
                    moments(h2[0:size, s, :], size, stat[5][:, s, :]).then_inc(r_ffn.var, 1)
                if 1 <= s <= NT:
                    i, size = s - 1, TILES[s - 1][1]
                    dve.wait_ge(r_ffn.rstd, i + 1)
                    link(normalise(w_rows[0:size, i, :], h2[0:size, i, :], size, stat[5][:, i, :]))
                    nc.vector.tensor_tensor(s_sum[0:size, i, :], w_rows[0:size, i, :], h2[0:size, i, :],
                                            ALU.add).then_inc(s_set, 1)
                    moments(w_rows[0:size, i, :], size, stat[0][:, i, :], rms=True).then_inc(r_ffn.var2, 1)
                if s >= 2:
                    i, size = s - 2, TILES[s - 2][1]
                    dve.wait_ge(r_ffn.rstd2, i + 1)
                    nc.vector.tensor_scalar(xn1[0:size, i, :], w_rows[0:size, i, :], stat[0][0:size, i, 9:10],
                                            None, ALU.mult).then_inc(r_ffn.normed, 1)
            sc = g_rows[:, 1, :]
            link(nc.vector.memset(sc, 0.0))
            dve.wait_ge(logits1, 1)
            last_size = TILES[-1][1]
            nc.vector.tensor_copy(sc[:, 0:(NT - 1) * 8], ps[:, 6, 0:(NT - 1) * 8])
            link(nc.vector.tensor_copy(sc[0:last_size, (NT - 1) * 8:NT * 8], ps[0:last_size, 6, (NT - 1) * 8:NT * 8]))
            tops = picks[:, 0, :].rearrange("p (i n) -> p i n", i=NT)
            sc3 = sc.rearrange("p (i n) -> p i n", i=NT)
            for i in range(NT):
                last = nc.vector.max(tops[:, i, :], sc3[:, i, :])
            link(last)
            for i in range(NT):
                last = nc.vector.max_index(idx_u[:, i, :], tops[:, i, :], sc3[:, i, :])
            link(last)
            idf1 = picks[:, 1, :].rearrange("p (i n) -> p i n", i=NT)
            link(nc.vector.tensor_copy(idf1, idx_u[:]))
            shape = [P, NT, EXPERTS]
            rk = [rank[:, n, :].rearrange("p (i n) -> p i n", i=NT) for n in range(6)]
            for n in range(2):
                last = nc.vector.tensor_tensor(rk[n], const("experts").unsqueeze(1).broadcast_to(shape),
                                               idf1[:, :, n:n + 1].broadcast_to(shape), ALU.is_equal)
            link(last)
            nc.vector.tensor_tensor(rk[2], rk[0], rk[1], ALU.add).then_inc(chosen_set, 1)
            nc.vector.tensor_tensor(picks[:, 2, 0:NT], tops[:, :, 1], tops[:, :, 0], ALU.subtract).then_inc(diff1, 1)
            dve.wait_ge(ranked, 1)
            count, used, last_block, first_block, base_row = [g_rows[:, n, 0:EXPERTS] for n in range(4)] + [
                g_rows[:, 0, EXPERTS:2 * EXPERTS]]
            link(nc.vector.tensor_copy(count, ps[:, 5, 0:EXPERTS]))
            link(nc.vector.memset(used, 1.0))
            for full in range(P, TOK, P):
                link(nc.vector.scalar_tensor_tensor(used, count, float(full), used, ALU.is_gt, ALU.add))
            link(nc.vector.tensor_tensor_scan(last_block, ones[:, 0:EXPERTS], used, 0.0, ALU.mult, ALU.add))
            link(nc.vector.tensor_tensor(first_block, last_block, used, ALU.subtract))
            nc.vector.tensor_copy(bounds[:, 0, :], first_block)
            nc.vector.tensor_copy(bounds[:, 1, :], last_block).then_inc(bounds_set, 1)
            link(nc.vector.tensor_scalar(base_row, first_block, float(P), None, ALU.mult))
            link(nc.vector.tensor_tensor(rk[3], ps[:, 4, 0:NT * EXPERTS].rearrange("p (i n) -> p i n", i=NT),
                                         base_row.unsqueeze(1).broadcast_to(shape), ALU.add))
            for n in range(2):
                link(nc.vector.tensor_tensor(rk[4], rk[3], rk[n], ALU.mult))
                link(nc.vector.tensor_reduce(picks[:, 4, n * NT:(n + 1) * NT], rk[4], AXX, ALU.add))
            nc.vector.tensor_copy(pos[:].rearrange("p n i -> p (n i)"), picks[:, 4, 0:2 * NT]).then_inc(pos_set, 1)
            dve.wait_ge(exped1, 1)
            link(nc.vector.tensor_scalar(picks[:, 0, 0:NT], picks[:, 3, 0:NT], 1.0, None, ALU.add))
            link(nc.vector.reciprocal(picks[:, 5, 0:NT], picks[:, 0, 0:NT]))
            link(nc.vector.tensor_tensor(picks[:, 5, NT:2 * NT], picks[:, 5, 0:NT], picks[:, 3, 0:NT], ALU.mult))

            dve.sem_inc(y_set, 1)
            blocks_end = dve.value_load(bounds[0:1, 1, EXPERTS - 1:EXPERTS], min_val=1, max_val=BLOCKS)
            with dve.Fori(0, blocks_end) as b:
                for half_ in range(2):
                    dve.wait_ge(silu1, 2 * b + half_ + 1)
                    nc.vector.tensor_tensor(hid1[:, 2 * half_:2 * half_ + 2, :].rearrange("p k t -> p (k t)"),
                                            sg1[:, half_, :], ps[:, 4 + 2 * half_, 0:2 * P], ALU.mult)\
                        .then_inc(hid1_set, 1)
                dve.wait_ge(down1, b + 1)
                dve.wait_ge(d_y, 16 * b + 16)
                nc.vector.tensor_copy(yblk[:], ps[:, 0, 0:D]).then_inc(y_set, 1)
            dve.wait_ge(s_set, NT)
            for i, (_, size) in enumerate(TILES):
                dve.wait_ge(d_picked[i], 32)
                for n in range(2):
                    last = nc.vector.scalar_tensor_tensor(
                        orow[0:size, i, :] if n else s_sum[0:size, i, :], picked[0:size, n, i, :],
                        picks[0:size, 5, n * NT + i:n * NT + i + 1], s_sum[0:size, i, :], ALU.mult, ALU.add)
                    if n == 0:
                        link(last)
                last.then_inc(out_set, 1)

        @block.gpsimd
        def _(pool):
            nc.gpsimd.memset(neg_half[:], -0.5).then_inc(consts_set, 1)
            pool.wait_ge(consts_set, 2)

            def roots(var, rstd, tiles, s_):
                for i, (_, size) in enumerate(tiles):
                    root(i, size, var, rstd, s_)

            def root(i, size, var, rstd, s_):
                pool.wait_ge(var, i + 1)
                nc.gpsimd.tensor_tensor(s_[0:size, i, 9:10], s_[0:size, i, 8:9], neg_half[0:size, :],
                                        ALU.pow).then_inc(rstd, 1)

            def attention(a, softmax):
                shape = [TG, HU, TG]
                for s in range(UNITS + 2):
                    if s >= 2:
                        b = (s - 2) % NPM
                        p3 = pm[0:TG, b, :].rearrange("p (h t) -> p h t", h=HU)
                        pool.wait_ge(a.summed, s - 1)
                        nc.gpsimd.tensor_tensor(p3, p3, att_small[0:TG, 0 if softmax else 1, b, 2, :].unsqueeze(2)
                                                .broadcast_to(shape), ALU.mult).then_inc(a.p, 1)
                    if softmax and s < UNITS:
                        p3 = pm[0:TG, s % NPM, :].rearrange("p (h t) -> p h t", h=HU)
                        pool.wait_ge(a.maxed, s + 1)
                        nc.gpsimd.tensor_tensor(p3, p3, att_small[0:TG, 0, s % NPM, 0, :].unsqueeze(2)
                                                .broadcast_to(shape), ALU.subtract).then_inc(a.shifted, 1)

            roots(r_tok.var, r_tok.rstd, GROUPS, stat[0])
            attention(a0, True)
            roots(r_out0.var, r_out0.rstd, GROUPS, stat[1])

            def two(r, s_a, s_b):
                for s in range(NT + 1):
                    if s < NT:
                        root(s, TILES[s][1], r.var, r.rstd, s_a)
                    if s >= 1:
                        root(s - 1, TILES[s - 1][1], r.var2, r.rstd2, s_b)
            two(r_mid, stat[2], stat[3])
            attention(a1, False)
            roots(r_out1.var, r_out1.rstd, TILES, stat[4])
            two(r_ffn, stat[5], stat[0])

            pool.wait_ge(d_zeroed, 16)
            pool.wait_ge(pos_set, 1)
            for i, (_, size) in enumerate(TILES):
                for n in range(2):
                    nc.gpsimd.indirect_dma_start(
                        out=xs, out_offset=bass.IndirectOffsetOnAxis(ap=pos[0:size, n, i:i + 1], axis=0),
                        in_=xn1[0:size, i, :], in_offset=None).then_inc(d_sorted, 16)
            pool.sem_inc(d_y, 16)
            pool.wait_ge(stored, 1)
            for i, (_, size) in enumerate(TILES):
                for n in range(2):
                    nc.gpsimd.indirect_dma_start(
                        out=picked[0:size, n, i, :], out_offset=None, in_=xs,
                        in_offset=bass.IndirectOffsetOnAxis(ap=pos[0:size, n, i:i + 1], axis=0))\
                        .then_inc(d_picked[i], 16)


def _constants():
    import numpy as np
    c = np.zeros((P, NCONST), np.float32)
    p = np.arange(P)

    def put(name, value):
        a, b = CONST[name]
        c[0:value.shape[0], a:b] = value
    t = np.arange(TG)
    seen = (t[:, None] // SEQ == t[None, :] // SEQ) & (t[None, :] <= t[:, None])
    put("ident", np.eye(P))
    put("addmask", np.where(seen, 0.0, MASKED))
    put("mulmask", np.where(seen, 1.0, 0.0))
    put("same_image", p[:, None] // EXPERTS == np.arange(IMAGES)[None, :])
    put("same_expert", p[:, None] % EXPERTS == np.arange(EXPERTS)[None, :])
    put("fold", t[:, None] % SEQ == np.arange(SEQ)[None, :])
    put("which", t[:, None] // SEQ == np.arange(2)[None, :])
    put("row", p[:, None])
    put("base_local", SEQ * (p[:, None] // EXPERTS % 2))
    put("base_global", SEQ * (p[:, None] // EXPERTS))
    put("tokens", np.broadcast_to(np.arange(TOK)[None, :], (P, TOK)))
    put("before", p[:, None] < p[None, :])
    put("experts", np.broadcast_to(np.arange(EXPERTS)[None, :], (P, EXPERTS)))
    return c


def kernel(**inputs):
    import numpy as np
    import concourse.bacc as _bacc
    from concourse import mybir as _mybir
    from concourse.bass_utils import run_bass_kernel_spmd as _run

    a = {k: np.asarray(v) for k, v in inputs.items()}
    f = np.float32

    def blocks(w):
        return np.ascontiguousarray(w.reshape(-1, P, w.shape[-1]).transpose(1, 0, 2))

    n, c, hh, ww = a["x"].shape
    ph = 16
    side = hh // ph
    pt = a["x"].reshape(n, c, side, ph, side, ph).transpose(1, 3, 5, 0, 2, 4).reshape(PD, n, side * side)
    patches = np.zeros((PD, n, SEQ), a["x"].dtype)
    patches[:, :, 1:] = pt
    cls, pos = a["L0_tok_cls_token"][0], a["L0_tok_pos_embed"][0]
    add_a = np.concatenate([pos, pos], 0)
    one = np.concatenate([cls, np.broadcast_to(a["L0_tok_b"][None, :], (SEQ - 1, D))], 0)
    add_b = np.concatenate([one, one], 0)
    kvd = blocks(a["L0_attn_w_kv_down"])
    E = EXPERTS
    e0 = np.concatenate(
        [a["L0_ffn_w_gate"].transpose(0, 2, 1).reshape(E, KD, P, I0).transpose(0, 2, 1, 3).reshape(E, P, KD * I0),
         a["L0_ffn_w_up"].transpose(0, 2, 1).reshape(E, KD, P, I0).transpose(0, 2, 1, 3).reshape(E, P, KD * I0),
         a["L0_ffn_w_down"].transpose(0, 2, 1).reshape(E, K0, P, D).transpose(0, 2, 1, 3).reshape(E, P, K0 * D)], 2)
    e1 = np.concatenate(
        [a["L1_ffn_w_up"].transpose(0, 2, 1).reshape(E, KD, P, 2 * I1).transpose(0, 2, 1, 3).reshape(E, P, -1),
         a["L1_ffn_w_down"].transpose(0, 2, 1).reshape(E, K1, P, D).transpose(0, 2, 1, 3).reshape(E, P, K1 * D)], 2)
    params = np.stack([a["L1_attn_ln1_g"], a["L1_attn_ln1_b"], a["L1_attn_ln2_g"], a["L1_attn_ln2_b"],
                       a["L1_ffn_norm_scale"]], 1)
    arrays = {
        "patches": blocks(patches.reshape(PD, TOK)).reshape(P, KP, 2, HALF).transpose(2, 0, 1, 3), "tok_w": blocks(a["L0_tok_W"].T),
        "add_a": add_a, "add_b": add_b,
        "w_q": blocks(a["L0_attn_w_q"]), "w_kvd": kvd, "w_kvu": a["L0_attn_w_kv_up"],
        "w_out": blocks(a["L0_attn_w_out"]), "gate_w": blocks(a["L0_ffn_gate_w"].T), "w_e0": e0,
        "l1_wq": blocks(a["L1_attn_Wq"]), "l1_wk": blocks(a["L1_attn_Wk"]), "l1_wv": blocks(a["L1_attn_Wv"]),
        "l1_wo": blocks(a["L1_attn_Wo"]), "l1_wf1": blocks(a["L1_attn_Wf1"]), "l1_wf2": blocks(a["L1_attn_Wf2"]),
        "params": blocks(params), "router": blocks(a["L1_ffn_w_router"].T), "w_e1": e1,
        "consts": _constants(),
    }
    arrays = {k: np.ascontiguousarray(v) for k, v in arrays.items()}
    nc = _bacc.Bacc("TRN2", target_bir_lowering=False, num_devices=1)
    args = [nc.dram_tensor(k, v.shape, _mybir.dt.from_np(v.dtype), kind="ExternalInput").ap()
            for k, v in arrays.items()]
    args.append(nc.dram_tensor("out_rows", (TOK, D), F32, kind="ExternalOutput").ap())
    vit_tower(nc, *args)
    r = _run(nc, [arrays], core_ids=[0])
    return np.ascontiguousarray(r.results[0]["out_rows"].reshape(IMAGES, SEQ, D))
```

```python
from contextlib import ExitStack

import concourse.bass as bass
from concourse import mybir

ALU = mybir.AluOpType
ACT = mybir.ActivationFunctionType
AXX = mybir.AxisListType.X
F32 = mybir.dt.float32
F32R = mybir.dt.float32r
BF16 = mybir.dt.bfloat16
U32 = mybir.dt.uint32

P = 128
IMAGES, D, SEQ = 16, 256, 37
TOK = IMAGES * SEQ
KD = D // P
NG, TG = IMAGES // 2, 2 * SEQ
GROUPS = [(TG * g, TG) for g in range(NG)]
TILES = [(t, min(P, TOK - t)) for t in range(0, TOK, P)]
NT = len(TILES)
EARLY = 2 * P
MEETS = [(t0 // TG, (t0 + size - 1) // TG) for t0, size in TILES]
PARTS = [sum(b - a + 1 for a, b in MEETS[:i]) for i in range(NT + 1)]
HALF = TOK // 2
PD = 768
KP = PD // P
HEADS, DH = 16, 64
HD = HEADS * DH
KH = HD // P
RANK = 128
HU = 8
UNITS = NG * HEADS // HU
LAG = 3
NPM = LAG + 1
EXPERTS = 8
GE = NG * EXPERTS
PICKS = SEQ // EXPERTS * 2
I0 = 1024
K0 = I0 // P
I1 = 512
K1 = I1 // P
DF = 1024
KF = DF // P
BLOCKS = (2 * TOK + EXPERTS * (P - 1)) // P
LEVELS = -(-TOK // P)
EPS_LN, EPS_RMS, EPS_DEN = 1e-5, 1e-6, 1e-6
SCALE = DH ** -0.5
MASKED = -1e30
W0 = 2 * KD * I0 + K0 * D
W1 = KD * 2 * I1 + K1 * D
BANK = 512

CONST = {}
_at = 0
for _name, _width in [("ident", P), ("addmask", TG), ("mulmask", TG), ("same_group", NG),
                      ("same_expert", EXPERTS), ("token_of_row", NT), ("image_start", 2),
                      ("tokens", TOK), ("experts", EXPERTS), ("filled", LEVELS),
                      ("before", P)]:
    CONST[_name] = (_at, _at + _width)
    _at += _width
NCONST = _at
GAIN1, BIAS1, GAIN2, BIAS2, NSCALE = range(5)


VALUE_PIECES = [sum(PARTS[f + 1] - PARTS[f] for f in range(i % 2, i + 1, 2)) for i in range(NT)]


def tiles_of(g):
    return [i for i in range(NT) if MEETS[i][0] <= g <= MEETS[i][1]]


PAIRS = [range(i, min(i + 2, NT)) for i in range(0, NT, 2)]
SINGLES = [range(0, 2)] + [range(i, i + 1) for i in range(2, NT)]


def column_pieces(t0, n):
    out = []
    if t0 < BANK:
        w = min(n, BANK - t0)
        out.append((lambda m: m, lambda m: t0, 0, w))
    if t0 + n > BANK:
        a = max(t0, BANK)
        out.append((lambda m: 2, lambda m: a - BANK + m * (TOK - BANK), a - t0, t0 + n - a))
    return out


def vit_tower(nc, patches_a, patches_b, tok_w, places, add_a, add_b, w_q, w_kvd, w_kvu, w_out, gate_w, w_e0,
              l1_wq, l1_wk, l1_wv, l1_wo, l1_wf1, l1_wf2, params, router, w_e1, consts, out):
    with ExitStack() as ctx:
        base = (nc.sbuf_base + 31) // 32 * 32
        end = nc.sbuf_usable_end

        def put(name, shape, offset, dt=F32):
            size = 4
            for n in shape[1:]:
                size *= n
            return nc.alloc_sbuf_tensor_at(name, shape, dt, offset=offset), offset + (size + 31) // 32 * 32

        def sem(name):
            return ctx.enter_context(nc.semaphore(name))

        at = base
        cst, at = put("cst", [P, NCONST], at)
        ones, at = put("ones", [P, P], at)
        ones_r, at = put("ones_r", [P, P], at, F32R)
        ones_bf, at = put("ones_bf", [P, P], at, BF16)
        before_bf, at = put("before_bf", [P, P], at, BF16)
        chosen, at = put("chosen", [P, NT * EXPERTS], at, BF16)
        neg_half, at = put("neg_half", [P, 1], at)
        par, at = put("par", [P, KD, 5], at)
        gw, at = put("gw", [P, KD, EXPERTS], at)
        rw, at = put("rw", [P, KD, EXPERTS], at)
        stat = []
        for n in range(6):
            s_, at = put(f"stat{n}", [P, 8, 12], at)
            stat.append(s_)
        att_small, at = put("att_small", [P, 2, NPM, 3, HU], at)
        rsm, at = put("rsm", [P, 4, 8 * 8], at)
        idx_u, at = put("idx_u", [P, NT, 8], at, U32)
        picks, at = put("picks", [P, 6, NT * 8], at)
        g_rows, at = put("g_rows", [P, 4, NT * 8], at)
        rows_at = at
        h, r_ = put("h", [P, NT, D], at)
        x, r_ = put("x", [P, NT, D], r_)
        h2, r_ = put("h2", [P, NT, D], rows_at)
        z, r_ = put("z", [P, NT, D], r_)
        x_hi, _ = put("x_hi", [P, NT, D], r_, F32R)
        x_lo, _ = put("x_lo", [P, NT, D], r_ - NT * D * 4, F32R)
        xa_hi, _ = put("xa_hi", [P, KD, TOK], r_, F32R)
        nrm, at = put("nrm", [P, NT, D], r_)
        xt_a, at = put("xt_a", [P, KD, TOK], at)
        xt_b, at = put("xt_b", [P, KD, TOK], at)
        xb_hi, _ = put("xb_hi", [P, KD, TOK], at - 2 * ((KD * TOK * 4 + 31) // 32 * 32), F32R)
        xa_lo, _ = put("xa_lo", [P, KD, TOK], at - 2 * ((KD * TOK * 4 + 31) // 32 * 32), F32R)
        lat_hi, lat_at = put("lat_hi", [P, 1, TOK], at - (KD * TOK * 4 + 31) // 32 * 32, F32R)
        lat_lo, _ = put("lat_lo", [P, 1, TOK], lat_at, F32R)
        xb_lo, _ = put("xb_lo", [P, KD, TOK], at - (KD * TOK * 4 + 31) // 32 * 32, F32R)
        rank, at = put("rank", [P, 6, NT * EXPERTS], at)
        pos, at = put("pos", [P, 2, NT], at, U32)
        bounds, at = put("bounds", [P, 2, EXPERTS], at, mybir.dt.int32)
        B = at
        qt, at = put("qt", [P, KH, TOK], at)
        kt, at = put("kt", [P, KH, TOK], at)
        v, at = put("v", [P, NG, HD], at)
        pm, at = put("pm", [P, NPM, HU * TG], at)
        pt, at = put("pt", [P, 2, HU * TG], at)
        B_end = at
        b = B
        d_idx, b = put("d_idx", [P, P * PICKS], b, F32R)
        xe, _ = put("xe", [P, D], b)
        onehot, b = put("onehot", [P, PARTS[NT], P], b, F32R)
        d_pick, b = put("d_pick", [P, 2, P], b)
        aff, b = put("aff", [P, 96], b)
        xin, b = put("xin", [P, KD, EXPERTS * P], b)
        spread, b = put("spread", [P, EXPERTS, TOK], b, F32R)
        hid0, b = put("hid0", [P, 3, K0, P], b)
        sg0, b = put("sg0", [P, 2, BANK], b)
        xe_hi, b = put("xe_hi", [P, D], b, F32R)
        xe_lo, b = put("xe_lo", [P, D], b, F32R)
        slot2_at = b
        assert b + W0 * 4 <= B_end, (b + W0 * 4, B_end)
        b = B
        xblk, b = put("xblk", [P, D], B + 32 * 1024)
        xbt, b = put("xbt", [P, KD, P], b)
        hid1, b = put("hid1", [P, K1, P], b)
        sg1, b = put("sg1", [P, 2, 2 * P], b)
        yblk, b = put("yblk", [P, D], b)
        picked, b = put("picked", [P, 2, NT, D], b)
        orow, b = put("orow", [P, NT, D], b)
        assert b <= B + 64 * 1024
        b = B + 64 * 1024
        s_sum, b = put("s_sum", [P, NT, D], b)
        xn1, b = put("xn1", [P, NT, D], b)
        w_rows, b = put("w_rows", [P, NT, D], b)
        assert b <= B_end
        ft, b = put("ft", [P, KF, TOK], B)
        ft_lo, b = put("ft_lo", [P, KF, TOK], B, F32R)
        ft_hi, b = put("ft_hi", [P, KF, TOK], b, F32R)
        zeros, _ = put("zeros", [P, BLOCKS + 2, D], B + KH * TOK * 2 * 4)
        phi, b = put("phi", [P, 4, 2, HALF], B + (KH * TOK * 2 + NG * HD) * 4)
        assert b <= B_end
        at = B_end
        C = at
        wq0, c_ = put("wq0", [P, KD, HD], C)
        wkvd, c_ = put("wkvd", [P, KD, RANK], c_)
        wkvu, c_ = put("wkvu", [P, 1, 2 * HD], c_)
        wout, c_ = put("wout", [P, KH, D], c_)
        wq0_lo, _ = put("wq0_lo", [P, KD, HD], C, F32R)
        wkvd_lo, l_ = put("wkvd_lo", [P, KD, RANK], _, F32R)
        wkvu_lo, l_ = put("wkvu_lo", [P, 1, 2 * HD], l_, F32R)
        wq1, at = put("wq1", [P, KD, HD], C)
        wk1, at = put("wk1", [P, KD, HD], at)
        wv1, at = put("wv1", [P, KD, HD], at)
        wo1, at = put("wo1", [P, KH, D], at)
        at = max(at, c_)
        wq1_lo, c_ = put("wq1_lo", [P, KD, HD], C, F32R)
        wk1_lo, c_ = put("wk1_lo", [P, KD, HD], c_, F32R)
        wv1_lo, c_ = put("wv1_lo", [P, KD, HD], c_, F32R)
        E = at
        v_rows, _ = put("v_rows", [P, 2, HD], E)
        wq0_hi, e_ = put("wq0_hi", [P, KD, HD], E, F32R)
        wkvd_hi, e_ = put("wkvd_hi", [P, KD, RANK], e_, F32R)
        wkvu_hi, e_ = put("wkvu_hi", [P, 1, 2 * HD], e_, F32R)
        assert e_ <= E + W0 * 4
        parts0 = ((wkvd, wkvd_hi, wkvd_lo), (wq0, wq0_hi, wq0_lo), (wkvu, wkvu_hi, wkvu_lo))
        slot0 = []
        for n in range(2):
            s_, at = put(f"slot0_{n}", [P, W0], at)
            slot0.append(s_)
        slot0.append(put("slot0_2", [P, W0], slot2_at)[0])
        E1 = E + W0 * 4
        assert at <= end, (at, end)
        pat_a, e_ = put("pat_a", [P, KP, EARLY], E1)
        pat_b, e_ = put("pat_b", [P, KP, TOK - EARLY], e_)
        wtok, e_ = put("wtok", [P, KP, D], e_)
        place_of, e_ = put("place_of", [SEQ, TOK], e_)
        assert e_ <= at
        slot1 = []
        e_ = E
        for n in range(4):
            s_, e_ = put(f"slot1_{n}", [P, W1], e_)
            slot1.append(s_)
        assert e_ <= at and E + 2 * W1 * 4 == E1
        wq1_hi, b = put("wq1_hi", [P, KD, HD], slot2_at, F32R)
        assert b <= B + (KH * TOK * 2 + NG * HD) * 4 and slot2_at >= B + KH * TOK * 2 * 4
        wk1_hi, e_ = put("wk1_hi", [P, KD, HD], E, F32R)
        wv1_hi, e_ = put("wv1_hi", [P, KD, HD], e_, F32R)
        assert e_ <= E1
        parts1 = ((wq1, wq1_hi, wq1_lo), (wk1, wk1_hi, wk1_lo), (wv1, wv1_hi, wv1_lo))
        wf1, e_ = put("wf1", [P, KD, DF], E1)
        wf2, e_ = put("wf2", [P, 1, KF * D], e_)
        assert e_ <= at
        wf1_hi, c_ = put("wf1_hi", [P, KD, DF], C, F32R)
        wf2_hi, c_ = put("wf2_hi", [P, 1, KF * D], c_, F32R)
        assert c_ <= C + 2 * KD * HD * 4
        wf1_lo, e_ = put("wf1_lo", [P, KD, DF], E1, F32R)
        wf2_lo, e_ = put("wf2_lo", [P, 1, KF * D], e_, F32R)
        parts_f = ((wf1, wf1_hi, wf1_lo), (wf2, wf2_hi, wf2_lo))
        addp, _ = put("addp", [SEQ, 2, D], B)

        ps = ctx.enter_context(nc.psum_tensor("ps", [P, 8, BANK], F32))

        def const(name, rows=P):
            a, z_ = CONST[name]
            return cst[0:rows, a:z_]

        ident = const("ident")

        d_const, d_par = sem("d_const"), sem("d_par")
        d_add, d_tok, d_qkv = sem("d_add"), sem("d_tok"), sem("d_qkv")
        d_pat = [sem("d_pat_0"), sem("d_pat_1")]
        d_e0 = [sem(f"d_e0_{n}") for n in range(3)]
        d_e1 = [sem(f"d_e1_{n}") for n in range(4)]
        d_l1, d_ffn, d_final = sem("d_l1"), sem("d_ffn"), sem("d_final")
        stats_set, addp_set = sem("stats_set"), sem("addp_set")
        dve_step = sem("dve_step")

        class Rows:
            def __init__(self, name, two=False):
                self.made, self.added = sem(name + "_made"), sem(name + "_added")
                self.var, self.rstd = sem(name + "_var"), sem(name + "_rstd")
                if two:
                    self.var2, self.rstd2 = sem(name + "_var2"), sem(name + "_rstd2")
                self.normed, self.turned, self.xt = sem(name + "_normed"), sem(name + "_turned"), sem(name + "_xt")
        r_tok, r_out0, r_mid, r_out1, r_ffn = [Rows(n, n in ("mid", "ffn"))
                                               for n in ("tok", "out0", "mid", "out1", "ffn")]

        class Att:
            def __init__(self, name, softmax):
                self.made = sem(name + "_proj")
                self.by_act, self.by_dve = sem(name + "_by_act"), sem(name + "_by_dve")
                self.scored, self.masked = sem(name + "_scored"), sem(name + "_masked")
                self.expd, self.summed = sem(name + "_expd"), sem(name + "_summed")
                if softmax:
                    self.maxed, self.shifted = sem(name + "_maxed"), sem(name + "_shifted")
                else:
                    self.relu = sem(name + "_relu")
                self.p, self.pt_made, self.pt = sem(name + "_p"), sem(name + "_pt_made"), sem(name + "_pt")
                self.y_made, self.y = sem(name + "_y_made"), sem(name + "_y")
                self.v_made, self.v = sem(name + "_v_made"), sem(name + "_v")
                self.d_v = [sem(name + "_d_v_0"), sem(name + "_d_v_1")]
        a0, a1 = Att("a0", True), Att("a1", False)

        logits0, shifted0, exped0 = sem("logits0"), sem("shifted0"), sem("exped0")
        affinity_set, affinity_made, d_ready, picks_made, onehot_set = (
            sem("affinity_set"), sem("affinity_made"), sem("d_ready"), sem("picks_made"), sem("onehot_set"))
        gathered, xin_act, xin_dve, spread_set = (
            sem("gathered"), sem("xin_act"), sem("xin_dve"), sem("spread_set"))
        gu0, silu0, hid0_set, down0, xe_set, comb0 = (
            sem("gu0"), sem("silu0"), sem("hid0_set"), sem("down0"), sem("xe_set"), sem("comb0"))
        h2t_set, h2_set = sem("h2t_set"), sem("h2_set")
        ffn_made, ffn_act = sem("hidden_made"), sem("hidden_act")
        zeros_set, d_zeroed = sem("zeros_set"), sem("d_zeroed")
        logits1, diff1, exped1, chosen_set, ranked, bounds_set = (
            sem("logits1"), sem("diff1"), sem("exped1"), sem("chosen_set"), sem("ranked"), sem("bounds_set"))
        d_sorted = [sem("d_sorted_low"), sem("d_sorted_high")]
        d_xblk, x_turned, xbt_set = sem("d_xblk"), sem("x_turned"), sem("xbt_set")
        gu1, silu1, hid1_set, down1, y_set, d_y, pos_set, out_set = (
            sem("gu1"), sem("silu1"), sem("hid1_set"), sem("down1"), sem("y_set"), sem("d_y"), sem("pos_set"),
            sem("out_set"))
        w0_high, w0_split, w0_split_up, x0_high, lat_high = (
            sem("w0_high"), sem("w0_split"), sem("w0_split_up"), sem("x0_high"), sem("lat_high"))
        wf_split, ft_split, xg_high, xg_split = sem("wf_split"), sem("ft_split"), sem("xg_high"), sem("xg_split")
        w_high, w_split, x_split = sem("w_high"), sem("w_split"), sem("x_split")
        stored = sem("stored")
        d_low, d_high = sem("d_low"), [sem(f"d_high_{i}") for i in range(NT)]
        xs = nc.dram_tensor("xs", ((BLOCKS + 2) * P, D), F32, kind="Internal").ap()

        block = ctx.enter_context(nc.Block())

        @block.sync
        def _(sp):
            def store_blocks(e, e_last):
                first = sp.value_load(bounds[0:1, 0, e:e + 1], min_val=0, max_val=BLOCKS)
                last = sp.value_load(bounds[0:1, 1, e_last:e_last + 1], min_val=1, max_val=BLOCKS)
                with sp.Fori(first, last) as b:
                    sp.wait_ge(y_set, b + 2)
                    sp.dma_start(xs[bass.ds(b * P, P), :], yblk[:]).then_inc(d_y, 16)
                return last

            def place_values(a):
                for i, (t0, size) in enumerate(TILES):
                    sp.wait_ge(a.v, 2 * i + 2)
                    for g in range(MEETS[i][0], MEETS[i][1] + 1):
                        first, last = max(t0, g * TG), min(t0 + size, (g + 1) * TG)
                        sp.dma_start(v[first - g * TG:last - g * TG, g, :], v_rows[first - t0:last - t0, i % 2, :])\
                            .then_inc(a.d_v[i % 2], 16)
                for i in range(NT - 2, NT):
                    sp.wait_ge(a.d_v[i % 2], 16 * VALUE_PIECES[i])

            for done, k in ((d_tok, slice(0, KP // 2)), (d_pat[0], slice(KP // 2, KP))):
                sp.dma_start(pat_a[:, k, :], patches_a[:, k, :]).then_inc(done, 16)
                sp.dma_start(wtok[:, k, :], tok_w[:, k, :]).then_inc(done, 16)
            sp.dma_start(addp[:, 0, :], add_a).then_inc(d_add, 16)
            sp.dma_start(addp[:, 1, :], add_b).then_inc(d_add, 16)
            sp.dma_start(place_of[:], places).then_inc(d_add, 16)
            sp.dma_start(pat_b[:], patches_b).then_inc(d_pat[1], 16)
            sp.dma_start(cst[:], consts).then_inc(d_const, 16)
            sp.dma_start(wkvd[:], w_kvd).then_inc(d_qkv, 16)
            sp.dma_start(wq0[:], w_q).then_inc(d_qkv, 16)
            sp.dma_start(wkvu[:, 0, :], w_kvu).then_inc(d_qkv, 16)
            sp.dma_start(wout[:], w_out).then_inc(d_par, 16)
            sp.dma_start(gw[:], gate_w).then_inc(d_par, 16)
            sp.dma_start(rw[:], router).then_inc(d_par, 16)
            sp.dma_start(par[:], params).then_inc(d_par, 16)
            sp.wait_ge(zeros_set, 1)
            sp.dma_start(xs.rearrange("(n p) d -> p n d", p=P), zeros[:]).then_inc(d_zeroed, 16)
            sp.wait_ge(r_tok.made, NT)
            sp.dma_start(slot0[1][:], w_e0[1]).then_inc(d_e0[1], 16)
            sp.wait_ge(d_zeroed, 16)
            place_values(a0)
            sp.dma_start(slot0[0][:], w_e0[0]).then_inc(d_e0[0], 16)
            sp.wait_ge(r_out0.made, NT)
            sp.dma_start(slot0[2][:], w_e0[2]).then_inc(d_e0[2], 16)
            for e in range(3, EXPERTS):
                sp.wait_ge(down0, e - 2)
                sp.dma_start(slot0[e % 3][:], w_e0[e]).then_inc(d_e0[e % 3], 16)
            for dst, src in ((wq1, l1_wq), (wk1, l1_wk), (wv1, l1_wv), (wo1, l1_wo)):
                sp.dma_start(dst[:], src).then_inc(d_l1, 16)
            sp.wait_ge(down0, EXPERTS)
            sp.dma_start(wf1[:], l1_wf1).then_inc(d_ffn, 16)
            sp.dma_start(wf2[:, 0, :], l1_wf2.rearrange("p k n -> p (k n)")).then_inc(d_ffn, 16)
            place_values(a1)
            for n in range(2):
                sp.dma_start(slot1[n][:], w_e1[n]).then_inc(d_e1[n], 16)
            sp.wait_ge(r_ffn.made, NT)
            for n in range(2, 4):
                sp.dma_start(slot1[n][:], w_e1[n]).then_inc(d_e1[n], 16)
            sp.wait_ge(bounds_set, 1)
            for n in range(4):
                store_blocks(n, n)
                sp.dma_start(slot1[n][:], w_e1[n + 4]).then_inc(d_e1[n], 16)
            for e, e_last in ((4, EXPERTS - 2), (EXPERTS - 1, EXPERTS - 1)):
                blocks_end = store_blocks(e, e_last)
                sp.wait_ge(d_y, 16 * blocks_end + 16)
                sp.sem_inc(stored, 1)
            for i in range(NT - 1):
                sp.wait_ge(out_set, i + 1)
                sp.dma_start(out[i * P:(i + 1) * P, :], orow[:, i, :]).then_inc(d_final, 16)
            sp.wait_ge(d_final, 16 * NT)

        MID_BANKS = [0, 1, 2, 3, 6]

        GATHER_BANKS = [[7, 6], [4, 5]]

        def xin_half(c, k):
            return xin[:, k, :].rearrange("p (e b j) -> p b e j", e=EXPERTS, b=IMAGES)[:, c * NG:(c + 1) * NG]

        def gathered_half(c, k):
            return ps[:, GATHER_BANKS[c][k], :].rearrange("p (b e j) -> p b e j", b=NG, e=EXPERTS)

        def half(c):
            return slice(c * HALF, (c + 1) * HALF)

        def chunks(w):
            width = w.shape[2]
            return [(k, slice(c, min(c + BANK, width))) for k in range(w.shape[1]) for c in range(0, width, BANK)]

        def in_parts(w, x, blocks, cols, tokens, x_first=False):
            pairs = [(wp[:, k, cols], xp[:, k, tokens]) for k in range(blocks)
                     for wp, xp in ((w[0], x[0]), (w[0], x[1]), (w[1], x[0]))]
            return [(b, a) for a, b in pairs] if x_first else pairs

        def turned_tile(i, size):
            return ps[:, 4 + i % 2, 0:KD * P].rearrange("p (k n) -> p k n", k=KD)[:, :, 0:size]

        WF_CHUNKS = sum(len(chunks(w)) for w, _, _ in parts_f)
        wf_chunks = [(part, k, cols) for part in parts_f for k, cols in chunks(part[0])]

        jobs0 = []
        for c in range(2):
            jobs0.append((in_parts(parts0[0][1:], (xa_hi, xa_lo), KD, slice(0, RANK), half(c)), lat_hi[:, 0, half(c)]))
        for c in range(2):
            for m in range(KH):
                jobs0.append((in_parts(parts0[1][1:], (xa_hi, xa_lo), KD, slice(m * P, (m + 1) * P), half(c)),
                              qt[:, m, half(c)]))
            for m in range(KH):
                jobs0.append((in_parts(parts0[2][1:], (lat_hi, lat_lo), 1, slice(m * P, (m + 1) * P), half(c)),
                              kt[:, m, half(c)]))
        jobs1 = []
        for c in range(2):
            for part, dst in ((parts1[0], qt), (parts1[1], kt)):
                for m in range(KH):
                    jobs1.append((in_parts(part[1:], (xb_hi, xb_lo), KD, slice(m * P, (m + 1) * P), half(c)),
                                  dst[:, m, half(c)]))

        def values0(i, n):
            return in_parts(parts0[2][1:], (lat_hi, lat_lo), 1, slice(HD + n * BANK, HD + (n + 1) * BANK),
                            slice(TILES[i][0], sum(TILES[i])), x_first=True)

        def values1(i, n):
            return in_parts(parts1[2][1:], (xb_hi, xb_lo), KD, slice(n * BANK, (n + 1) * BANK),
                            slice(TILES[i][0], sum(TILES[i])), x_first=True)

        def place(n):
            return n % 2 * 4 + n // 2

        def job_result(j, dst):
            return ps[0:dst.shape[0], j % 8, 0:dst.shape[1]]

        @block.tensor
        def _(pe):
            def rows(r, tiles, product, src, step_lag=4, first=0, scores=None, ring=range(4)):
                n = len(tiles)
                for s in range(n + step_lag):
                    if first <= s < n:
                        if s >= len(ring):
                            pe.wait_ge(r.added, s - len(ring) + 1)
                        product(s, ps[0:tiles[s][1], ring[s % len(ring)], 0:D]).then_inc(r.made, 1)
                    if s >= step_lag:
                        i = s - step_lag
                        pe.wait_ge(r.normed, i + 1)
                        if i >= 2:
                            pe.wait_ge(r.xt, i - 1)
                        turn(src[0:tiles[i][1], i, :], tiles[i][1], 4 + i % 2).then_inc(r.turned, 1)
                        if scores is not None and i >= 1:
                            pe.wait_ge(r.xt, i)
                            scores(i - 1)
                if scores is not None:
                    pe.wait_ge(r.xt, n)
                    scores(n - 1)

            def router_scores(xt, weights, spans, made):
                def scores(i):
                    for n, (t0, size) in enumerate(spans):
                        if sum(TILES[i]) - TILES[i][1] < t0 + size <= sum(TILES[i]):
                            for k in range(KD):
                                last = nc.tensor.matmul(ps[0:size, 6, n * EXPERTS:(n + 1) * EXPERTS],
                                                        xt[:, k, t0:t0 + size], weights[:, k, :],
                                                        start=(k == 0), stop=(k == KD - 1))
                            last.then_inc(made, 1)
                return scores

            def turn(src, size, bank):
                for k in range(KD):
                    last = nc.tensor.transpose(ps[:, bank, k * P:k * P + size], src[:, k * P:(k + 1) * P],
                                               ident[0:size, 0:size])
                return last

            def projections(a, jobs, deps):
                for j, (operands, _) in enumerate(jobs):
                    if j in deps:
                        for s, n in deps[j]:
                            pe.wait_ge(s, n)
                    if j >= 8:
                        pe.wait_ge((a.by_act, a.by_dve)[j % 2], (j - 8) // 2 + 1)
                    n = len(operands)
                    for k, (lhs, rhs) in enumerate(operands):
                        last = nc.tensor.matmul(job_bank(j, lhs, rhs), lhs, rhs, start=(k == 0), stop=(k == n - 1))
                    last.then_inc(a.made, 1)

            def job_bank(j, lhs, rhs):
                return ps[0:lhs.shape[1], j % 8, 0:rhs.shape[1]]

            def attention(a, values, out_rows, tiles, product):
                for s in range(UNITS + LAG + 1):
                    if s < 2 * NT:
                        if s >= 1:
                            pe.wait_ge(a.v, s)
                        operands = values(s // 2, s % 2)
                        for k, (lhs, rhs) in enumerate(operands):
                            last = nc.tensor.matmul(ps[0:TILES[s // 2][1], 7, :], lhs, rhs, start=(k == 0),
                                                    stop=(k == len(operands) - 1))
                        last.then_inc(a.v_made, 1)
                    if s < UNITS:
                        if s >= 2:
                            pe.wait_ge(a.masked, s - 1)
                        gs, hs = s * HU // HEADS, s * HU % HEADS
                        for n in range(HU):
                            m, r = (hs + n) // 2, (hs + n) % 2 * DH
                            cols = slice(gs * TG, (gs + 1) * TG)
                            last = nc.tensor.matmul(
                                ps[0:TG, 2 * (s % 2) + n % 2, n // 2 * TG:(n // 2 + 1) * TG],
                                qt[r:r + DH, m, cols], kt[r:r + DH, m, cols], start=True, stop=True)
                        last.then_inc(a.scored, 1)
                    u = s - LAG - 1
                    g, h0 = u * HU // HEADS, u * HU % HEADS
                    if u >= 0:
                        pe.wait_ge(a.pt, u + 1)
                        for i in tiles_of(g):
                            pe.wait_ge(a.d_v[i % 2], 16 * VALUE_PIECES[i])
                        if u >= 1:
                            pe.wait_ge(a.y, u)
                        for n in range(HU):
                            r = n % 2 * DH
                            last = nc.tensor.matmul(
                                ps[r:r + DH, 6, n // 2 * TG:(n // 2 + 1) * TG],
                                v[0:TG, g, (h0 + n) * DH:(h0 + n + 1) * DH],
                                pt[0:TG, u % 2, place(n) * TG:(place(n) + 1) * TG], start=True, stop=True)
                        last.then_inc(a.y_made, 1)
                    u = s - LAG
                    if 0 <= u < UNITS:
                        pe.wait_ge(a.p, u + 1)
                        if u >= 1:
                            pe.wait_ge(a.pt, u)
                        for n in range(HU):
                            last = nc.tensor.transpose(
                                ps[0:TG, 4 + n // 4, (n % 4) * TG:(n % 4 + 1) * TG],
                                pm[0:TG, u % NPM, n * TG:(n + 1) * TG], ident[0:TG, 0:TG])
                        last.then_inc(a.pt_made, 1)
                    i = s - UNITS
                    if i >= 0:
                        pe.wait_ge(a.masked, UNITS - 1 + i // 2 if i < 2 else UNITS)
                        pe.wait_ge(a.y, units_before(sum(tiles[i])))
                        product(i, ps[0:tiles[i][1], i, 0:D]).then_inc(out_rows.made, 1)

            def units_before(token):
                return -(-token // TG) * (HEADS // HU)

            def product_of(lhs, rhs, blocks, tiles):
                def product(s, dst):
                    t0, size = tiles[s]
                    for k in range(blocks):
                        last = nc.tensor.matmul(dst, lhs[:, k, t0:t0 + size], rhs[:, k, :],
                                                start=(k == 0), stop=(k == blocks - 1))
                    return last
                return product

            pe.wait_ge(d_tok, 32)

            def patch_rows(i, dst):
                t0, size = TILES[i]
                if t0 == EARLY:
                    pe.wait_ge(d_pat[1], 16)
                if i == NT - 1:
                    pe.wait_ge(d_const, 16)
                src, t = (pat_a, t0) if t0 < EARLY else (pat_b, t0 - EARLY)
                for k in range(KP):
                    if i == 0 and k == KP // 2:
                        pe.wait_ge(d_pat[0], 32)
                    nc.tensor.matmul(dst, src[:, k, t:t + size], wtok[:, k, :], start=(k == 0), stop=False)
                if i == 0:
                    pe.wait_ge(addp_set, 1)
                return nc.tensor.matmul(dst, place_of[:, t0:t0 + size], addp[:, 0, :], start=False, stop=True)
            rows(r_tok, TILES, patch_rows, x)
            projections(a0, jobs0, {0: [(w0_split, len(chunks(wkvd)) + len(chunks(wq0))), (r_tok.xt, 3)],
                                    1: [(r_tok.xt, NT)],
                                    2 + KH: [(a0.by_act, 1), (a0.by_dve, 1), (w0_split_up, len(chunks(wkvu)))]})
            pe.wait_ge(a0.by_act, (len(jobs0) + 1) // 2)
            pe.wait_ge(a0.by_dve, len(jobs0) // 2)
            pe.wait_ge(d_par, 64)
            product = product_of(qt, wout, KH, TILES)
            attention(a0, values0, r_out0, TILES, product)
            pe.wait_ge(a0.y, UNITS)
            rows(r_out0, TILES, product, x, step_lag=3, first=LAG + 1, scores=router_scores(xt_a, gw, GROUPS, logits0))

            fresh = [True] * 3

            def residual(tiles):
                for i in tiles:
                    t0, size = TILES[i]
                    for m in range(KD):
                        for bank, col, off, w in column_pieces(t0, size):
                            bk = bank(m)
                            nc.tensor.matmul(ps[:, bk, col(m):col(m) + w], h[0:size, i, m * P:(m + 1) * P],
                                             ident[0:size, off:off + w], start=fresh[bk], stop=False,
                                             skip_group_check=True)
                            fresh[bk] = False
            residual(range(0, 2))
            pe.wait_ge(affinity_set, 1)
            nc.tensor.transpose(ps[0:GE, 7, 0:TG], rsm[0:TG, 2, :], ident[0:TG, 0:TG]).then_inc(affinity_made, 1)
            residual(range(2, 4))
            pe.wait_ge(d_ready, 1)
            for n in range(2):
                nc.tensor.matmul(ps[:, 4 + n, :], ones_r[0:GE, :], d_idx[0:GE, n * BANK:(n + 1) * BANK],
                                 start=True, stop=True)
            for n in range(2):
                last = nc.tensor.matmul(ps[:, 6, n * EXPERTS:(n + 1) * EXPERTS], d_pick[0:GE, n, :],
                                        const("same_expert", GE), start=True, stop=True)
            last.then_inc(picks_made, 1)
            residual(range(4, NT))
            pe.wait_ge(xg_split, NT)
            for c in range(2):
                for k in range(KD):
                    fresh_bank = True
                    for i, (_, size) in enumerate(TILES):
                        first, last_g = max(MEETS[i][0], c * NG // 2), min(MEETS[i][1], (c + 1) * NG // 2 - 1)
                        if first > last_g:
                            continue
                        pe.wait_ge(onehot_set, NT if c else i + 1)
                        for part in (x_hi, x_lo):
                            last = nc.tensor.matmul(
                                ps[:, GATHER_BANKS[c][k],
                                   (first - c * NG // 2) * P:(last_g + 1 - c * NG // 2) * P],
                                part[0:size, i, k * P:(k + 1) * P],
                                onehot[0:size, PARTS[i] + first - MEETS[i][0]:PARTS[i] + last_g + 1 - MEETS[i][0], :]
                                .rearrange("p n c -> p (n c)"), start=fresh_bank, stop=False,
                                skip_group_check=True)
                            fresh_bank = False
                    last.then_inc(gathered, 1)
            pe.wait_ge(xin_act, 2)
            pe.wait_ge(xin_dve, 2)

            def gate_up0(n, e, half, i=None):
                if e is None or e >= 1:
                    pe.wait_ge(hid0_set, 2 * (e if e is not None else i) + half - 1)
                for w in range(2):
                    for m in range(4):
                        for k in range(KD):
                            a = (w * KD + k) * I0 + (half * 4 + m) * P
                            rhs = (xin[:, k, e * P:(e + 1) * P] if e is not None
                                   else xin[:, k, bass.ds(i * P, P)])
                            last = nc.tensor.matmul(ps[:, 4 + 2 * half + w, m * P:(m + 1) * P],
                                                    slot0[n][:, a:a + P], rhs, start=(k == 0), stop=(k == KD - 1))
                last.then_inc(gu0, 1)

            def down_product0(n, done):
                pe.wait_ge(hid0_set, 2 * done)
                for k in range(K0):
                    a = 2 * KD * I0 + k * D
                    last = nc.tensor.matmul(ps[:, 3, 0:D], hid0[:, n, k, :], slot0[n][:, a:a + D],
                                            start=(k == 0), stop=(k == K0 - 1))
                last.then_inc(down0, 1)

            def combine0(e, done):
                pe.wait_ge(xe_set, done)
                for m in range(KD):
                    for bank, col, off, w in column_pieces(0, TOK):
                        rhs = spread[:].rearrange("p e t -> p (e t)")[:, bass.ds(e * TOK + off, w)]
                        for part in (xe_hi, xe_lo):
                            last = nc.tensor.matmul(ps[:, bank(m), col(m):col(m) + w], part[:, m * P:(m + 1) * P],
                                                    rhs, start=False, stop=False, skip_group_check=True)
                last.then_inc(comb0, 1)

            pe.wait_ge(d_e0[0], 16)
            gate_up0(0, 0, 0)
            gate_up0(0, 0, 1)
            pe.wait_ge(spread_set, EXPERTS)
            with pe.Fori(0, 2) as i:
                for n in (1, 2, 0):
                    e = 3 * i + (n if n else 3)
                    pe.wait_ge(d_e0[n], 16 * i + (16 if n else 32))
                    gate_up0(n, None, 0, e)
                    down_product0((n + 2) % 3, e)
                    gate_up0(n, None, 1, e)
                    combine0(e - 1, e)
            pe.wait_ge(d_e0[1], 16 * 3)
            gate_up0(1, EXPERTS - 1, 0)
            down_product0(0, EXPERTS - 1)
            gate_up0(1, EXPERTS - 1, 1)
            combine0(EXPERTS - 2, EXPERTS - 1)
            down_product0(1, EXPERTS)
            combine0(EXPERTS - 1, EXPERTS)

            def h2_rows(s, dst):
                if s == 0:
                    pe.wait_ge(h2t_set, 3)
                t0, size = TILES[s]
                for k in range(KD):
                    last = nc.tensor.transpose(dst[:, k * P:(k + 1) * P], xt_a[:, k, t0:t0 + size], ident)
                return last
            rows(r_mid, TILES, h2_rows, nrm, ring=MID_BANKS)

            projections(a1, jobs1, {0: [(w_split, 2 * KD), (x_split, 3), (h2_set, NT)],
                                    4: [(r_mid.xt, NT)],
                                    KH: [(w_split, 4 * KD)],
                                    len(jobs1) // 2: [(x_split, NT)]})
            pe.wait_ge(w_split, 6 * KD)
            pe.wait_ge(a1.by_act, (len(jobs1) + 1) // 2)
            pe.wait_ge(a1.by_dve, len(jobs1) // 2)
            product = product_of(qt, wo1, KH, TILES)
            attention(a1, values1, r_out1, TILES, product)
            pe.wait_ge(a1.y, UNITS)
            rows(r_out1, TILES, product, nrm, first=LAG + 1)

            pe.wait_ge(wf_split, WF_CHUNKS)
            for j in range(2 * KF):
                c, m = j // KF, j % KF
                if j % KF == 0:
                    pe.wait_ge(x_split, NT + (NT if c else 3))
                if j == 4:
                    pe.wait_ge(r_out1.xt, NT)
                if j >= 8:
                    pe.wait_ge(ffn_act, j - 7)
                operands = in_parts((wf1_hi, wf1_lo), (xb_hi, xb_lo), KD, slice(m * P, (m + 1) * P), half(c))
                for k, (lhs, rhs) in enumerate(operands):
                    last = nc.tensor.matmul(ps[:, j % 8, 0:HALF], lhs, rhs, start=(k == 0),
                                            stop=(k == len(operands) - 1))
                last.then_inc(ffn_made, 1)

            def ffn_rows(i, dst):
                t0, size = TILES[i]
                pe.wait_ge(ffn_act, 2 * KF if i == NT - 1 else KF + 1 + i)
                pe.wait_ge(ft_split, KF if t0 + size <= HALF else 2 * KF)
                pairs = [(fp[:, k, t0:t0 + size], wp[:, 0, k * D:(k + 1) * D]) for k in range(KF)
                         for fp, wp in ((ft_hi, wf2_hi), (ft_lo, wf2_hi), (ft_hi, wf2_lo))]
                for k, (lhs, rhs) in enumerate(pairs):
                    last = nc.tensor.matmul(dst, lhs, rhs, start=(k == 0), stop=(k == len(pairs) - 1))
                return last
            rows(r_ffn, TILES, ffn_rows, xn1, scores=router_scores(xt_b, rw, TILES, logits1))

            pe.wait_ge(chosen_set, 1)
            for f in range(NT):
                nc.tensor.matmul(ps[:, 4, (f + 1) * EXPERTS:(NT + 1) * EXPERTS].rearrange("p (i e) -> p i e", e=EXPERTS),
                                 ones_bf[:], chosen[:, f * EXPERTS:(f + 1) * EXPERTS].unsqueeze(1)
                                 .broadcast_to([P, NT - f, EXPERTS]), start=(f == 0), stop=False,
                                 skip_group_check=True)
            nc.tensor.matmul(ps[:, 4, 0:NT * EXPERTS], before_bf[:], chosen[:], start=False, stop=True,
                             skip_group_check=True).then_inc(ranked, 1)

            def turn_block(landed):
                pe.wait_ge(d_xblk, landed)
                turn(xblk, P, 2).then_inc(x_turned, 1)

            pe.wait_ge(bounds_set, 1)
            ends = [pe.value_load(bounds[0:1, 1, e:e + 1], min_val=1, max_val=BLOCKS) for e in range(EXPERTS)]
            turn_block(16)
            for e in range(EXPERTS):
                n = e % 4
                pe.wait_ge(d_e1[n], 16 * (e // 4) + 16)
                with pe.Fori(0 if e == 0 else ends[e - 1], ends[e]) as b:
                    pe.wait_ge(xbt_set, b + 1)
                    for half_ in range(2):
                        for w in range(2):
                            for m in range(2):
                                for k in range(KD):
                                    a = k * 2 * I1 + w * I1 + (2 * half_ + m) * P
                                    last = nc.tensor.matmul(ps[:, 4 + 2 * half_ + w, m * P:(m + 1) * P],
                                                            slot1[n][:, a:a + P], xbt[:, k, :],
                                                            start=(k == 0), stop=(k == KD - 1))
                        last.then_inc(gu1, 1)
                    turn_block(16 * b + 32)
                    pe.wait_ge(y_set, b + 1)
                    for k in range(K1):
                        if k % 2 == 0:
                            pe.wait_ge(hid1_set, 2 * b + 1 + k // 2)
                        a = KD * 2 * I1 + k * D
                        last = nc.tensor.matmul(ps[:, 0, 0:D], hid1[:, k, :], slot1[n][:, a:a + D],
                                                start=(k == 0), stop=(k == K1 - 1))
                    last.then_inc(down1, 1)

        @block.scalar
        def _(act):
            def turned(r, dst, gain=None, bias=None, tiles=range(NT)):
                for i in tiles:
                    t0, size = TILES[i]
                    act.wait_ge(r.turned, i + 1)
                    src = ps[:, 4 + i % 2, 0:KD * P].rearrange("p (k n) -> p k n", k=KD)[:, :, 0:size]
                    if gain is None:
                        last = nc.scalar.activation(dst[:, :, t0:t0 + size], src, ACT.Copy)
                    for k in range(KD if gain is not None else 0):
                        if bias is None:
                            last = nc.scalar.activation(dst[:, k, t0:t0 + size], src[:, k, :], ACT.Copy,
                                                        scale=par[:, k, gain:gain + 1])
                        else:
                            last = nc.scalar.activation(dst[:, k, t0:t0 + size], src[:, k, :], ACT.Identity,
                                                        scale=par[:, k, gain:gain + 1],
                                                        bias=par[:, k, bias:bias + 1])
                    last.then_inc(r.xt, 1)

            def attention(a, softmax):
                for s in range(UNITS + LAG + 1):
                    if s < 2 * NT:
                        i, n = s // 2, s % 2
                        act.wait_ge(a.v_made, s + 1)
                        if i >= 2 and n == 0:
                            act.wait_ge(a.d_v[i % 2], 16 * VALUE_PIECES[i - 2])
                        nc.scalar.activation(v_rows[0:TILES[i][1], i % 2, n * BANK:(n + 1) * BANK],
                                             ps[0:TILES[i][1], 7, :], ACT.Copy).then_inc(a.v, 1)
                    if s < UNITS:
                        if not softmax and s % 2 == 1:
                            if s == 1:
                                act.wait_ge(d_ffn, 32)
                            (w, hi, _), k, cols = wf_chunks[s // 2]
                            nc.scalar.activation(hi[:, k, cols], w[:, k, cols], ACT.Copy).then_inc(w_high, 1)
                    u = s - LAG - 1
                    if u >= 0:
                        g, m0 = u * HU // HEADS, u * HU % HEADS // 2
                        act.wait_ge(a.y_made, u + 1)
                        nc.scalar.activation(
                            qt[:, m0:m0 + HU // 2, g * TG:(g + 1) * TG],
                            ps[:, 6, 0:4 * TG].rearrange("p (m n) -> p m n", m=4), ACT.Copy).then_inc(a.y, 1)
                    if softmax and 1 <= s <= UNITS:
                        w = s - 1
                        act.wait_ge(a.shifted, w + 1)
                        nc.scalar.activation(pm[0:TG, w % NPM, :], pm[0:TG, w % NPM, :], ACT.Exp).then_inc(a.expd, 1)
                    u = s - LAG
                    if 0 <= u < UNITS:
                        act.wait_ge(a.pt_made, u + 1)
                        if u >= 2:
                            act.wait_ge(a.y_made, u - 1)
                        nc.scalar.activation(
                            pt[0:TG, u % 2, :].rearrange("p (b n) -> p b n", b=2),
                            ps[0:TG, 4:6, 0:4 * TG], ACT.Copy).then_inc(a.pt, 1)

            def high_parts(part, done):
                w, hi, _ = part
                for k, cols in chunks(w):
                    nc.scalar.activation(hi[:, k, cols], w[:, k, cols], ACT.Copy).then_inc(done, 1)

            act.wait_ge(d_qkv, 48)
            for part in parts0:
                high_parts(part, w0_high)
            for i, (t0, size) in enumerate(TILES):
                act.wait_ge(r_tok.turned, i + 1)
                nc.scalar.activation(xa_hi[:, :, t0:t0 + size], turned_tile(i, size), ACT.Copy).then_inc(x0_high, 1)
            for j in range(2):
                act.wait_ge(a0.made, j + 1)
                dst = jobs0[j][1]
                nc.scalar.activation(dst, job_result(j, dst), ACT.Copy).then_inc(lat_high, 1)
            act.wait_ge(a0.by_act, 1)
            for j in range(2, len(jobs0), 2):
                act.wait_ge(a0.made, j + 1)
                dst = jobs0[j][1]
                nc.scalar.activation(dst, job_result(j, dst), ACT.Copy).then_inc(a0.by_act, 1)
            attention(a0, True)
            turned(r_out0, xt_a)
            for i, (_, size) in enumerate(TILES):
                act.wait_ge(r_out0.normed, i + 1)
                nc.scalar.activation(x_hi[0:size, i, :], x[0:size, i, :], ACT.Copy).then_inc(xg_high, 1)
            act.wait_ge(shifted0, 1)
            nc.scalar.activation(rsm[0:TG, 1, :], rsm[0:TG, 0, :], ACT.Exp).then_inc(exped0, 1)

            for c in range(2):
                act.wait_ge(gathered, 2 * c + 1)
                nc.scalar.activation(xin_half(c, 0), gathered_half(c, 0), ACT.Copy).then_inc(xin_act, 1)

            for half_ in range(2):
                act.wait_ge(gu0, half_ + 1)
                nc.scalar.activation(sg0[:, half_, :], ps[:, 4 + 2 * half_, :], ACT.Silu).then_inc(silu0, 1)
            def silus(e):
                for half_ in range(2):
                    act.wait_ge(gu0, 2 * e + half_ + 1)
                    act.wait_ge(hid0_set, 2 * e + half_ - 1)
                    nc.scalar.activation(sg0[:, half_, :], ps[:, 4 + 2 * half_, :], ACT.Silu).then_inc(silu0, 1)
            with act.Fori(1, EXPERTS - 1) as e:
                silus(e)
            act.wait_ge(d_l1, 64)
            act.wait_ge(down0, EXPERTS - 2)
            high_parts(parts1[0], w_high)
            silus(EXPERTS - 1)
            act.wait_ge(down0, EXPERTS - 1)
            for part in parts1[1:]:
                high_parts(part, w_high)
            act.wait_ge(comb0, EXPERTS)
            nc.scalar.activation(xt_a[:, 0, 0:BANK], ps[:, 0, :], ACT.Copy).then_inc(h2t_set, 1)
            nc.scalar.activation(xt_a[:, :, BANK:TOK],
                                 ps[:, 2, 0:2 * (TOK - BANK)].rearrange("p (m n) -> p m n", m=2),
                                 ACT.Copy).then_inc(h2t_set, 1)
            act.wait_ge(d_par, 64)
            for i, (_, size) in enumerate(TILES):
                act.wait_ge(r_mid.made, i + 1)
                nc.scalar.activation(h2[0:size, i, :], ps[0:size, MID_BANKS[i], 0:D], ACT.Copy).then_inc(h2_set, 1)
            turned(r_mid, xt_b, GAIN1, BIAS1)

            for j in range(len(jobs1)):
                act.wait_ge(a1.made, j + 1)
                if j >= 4:
                    act.wait_ge((a1.by_act, a1.by_dve)[j % 2], (j - 4) // 2 + 1)
                nc.scalar.activation(phi[:, j % 4, 0, :], job_result(j, jobs1[j][1]), ACT.Relu,
                                     scale=-1.0).then_inc(a1.relu, 1)
                act.wait_ge(a1.relu, j + 1)
                nc.scalar.activation(phi[:, j % 4, 1, :], phi[:, j % 4, 0, :], ACT.Exp,
                                     scale=-1.0).then_inc(a1.expd, 1)
            attention(a1, False)
            turned(r_out1, xt_b, GAIN2, BIAS2)
            for j in range(2 * KF):
                c, m = j // KF, j % KF
                act.wait_ge(ffn_made, j + 1)
                nc.scalar.activation(ft[:, m, c * HALF:(c + 1) * HALF], ps[:, j % 8, 0:HALF],
                                     ACT.Gelu).then_inc(ffn_act, 1)
            for n, tiles in enumerate(SINGLES):
                act.wait_ge(r_ffn.rstd2, n + 1)
                for i in tiles:
                    size = TILES[i][1]
                    nc.scalar.activation(xn1[0:size, i, :], w_rows[0:size, i, :], ACT.Copy,
                                         scale=stat[0][0:size, i, 9:10]).then_inc(r_ffn.normed, 1)
                turned(r_ffn, xt_b, NSCALE, tiles=tiles)
            act.wait_ge(diff1, 1)
            nc.scalar.activation(picks[:, 3, 0:NT], picks[:, 2, 0:NT], ACT.Exp).then_inc(exped1, 1)

            def load_block(row):
                src = xs[bass.ds(row, P), :] if not isinstance(row, int) else xs[row:row + P, :]
                act.dma_start(xblk[:], src).then_inc(d_xblk, 16)

            def scaled_block():
                for k in range(KD):
                    last = nc.scalar.activation(xbt[:, k, :], ps[:, 2, k * P:(k + 1) * P], ACT.Copy,
                                                scale=par[:, k, NSCALE:NSCALE + 1])
                last.then_inc(xbt_set, 1)

            act.wait_ge(bounds_set, 1)
            act.wait_ge(d_sorted[0], 16 * NT)
            load_block(0)
            act.wait_ge(x_turned, 1)
            scaled_block()
            act.wait_ge(d_sorted[1], 16 * NT)
            load_block(P)
            blocks_end = act.value_load(bounds[0:1, 1, EXPERTS - 1:EXPERTS], min_val=1, max_val=BLOCKS)
            with act.Fori(0, blocks_end) as b:
                for half_ in range(2):
                    act.wait_ge(gu1, 2 * b + half_ + 1)
                    nc.scalar.activation(sg1[:, half_, :], ps[:, 5 + 2 * half_, 0:2 * P], ACT.Silu).then_inc(silu1, 1)
                act.wait_ge(x_turned, b + 2)
                scaled_block()
                load_block((b + 2) * P)
            act.wait_ge(d_xblk, 16 * blocks_end + 32)
            full = (NT - 1) * P
            act.wait_ge(out_set, NT)
            act.dma_start(out[full:TOK, :], orow[0:TOK - full, NT - 1, :]).then_inc(d_final, 16)

        @block.vector
        def _(dve):
            steps = [0]

            def link(ins):
                steps[0] += 1
                ins.then_inc(dve_step, 1)
                dve.wait_ge(dve_step, steps[0])

            def split_x(r):
                for i, (t0, size) in enumerate(TILES):
                    dve.wait_ge(r.xt, i + 1)
                    link(nc.vector.tensor_copy(xb_hi[:, :, t0:t0 + size], xt_b[:, :, t0:t0 + size]))
                    nc.vector.tensor_tensor(xb_lo[:, :, t0:t0 + size], xt_b[:, :, t0:t0 + size],
                                            xb_hi[:, :, t0:t0 + size].bitcast(F32), ALU.subtract).then_inc(x_split, 1)

            def moments(src, tiles, batch, s_, rms=False):
                for i in batch:
                    size = tiles[i][1]
                    last = nc.vector.bn_stats(s_[0:size, i, 0:6], src[0:size, i, :])
                link(last)
                for i in batch:
                    size = tiles[i][1]
                    last = nc.vector.bn_aggr(s_[0:size, i, 6:8], s_[0:size, i, 0:6])
                link(last)
                col = [s_[:, batch[0]:batch[-1] + 1, n] for n in range(12)]
                if rms:
                    link(nc.vector.tensor_tensor(col[10], col[6], col[6], ALU.mult))
                    return nc.vector.scalar_tensor_tensor(col[8], col[7], EPS_RMS, col[10], ALU.add, ALU.add)
                return nc.vector.tensor_scalar(col[8], col[7], EPS_LN, None, ALU.add)

            def normalise(dst, src, tiles, i, s_):
                size = tiles[i][1]
                return nc.vector.tensor_scalar(dst[0:size, i, :], src[0:size, i, :], s_[0:size, i, 6:7],
                                               s_[0:size, i, 9:10], ALU.subtract, ALU.mult)

            def rows(r, parts, tiles, dst, addend, normed, s_, meanwhile=None):
                for s in range(len(parts) + 1):
                    if s < len(parts):
                        for i in parts[s]:
                            size = tiles[i][1]
                            if meanwhile is not None and i == len(tiles) - 2:
                                meanwhile()
                            dve.wait_ge(r.made, i + 1)
                            if addend is None:
                                last = nc.vector.tensor_copy(dst[0:size, i, :], ps[0:size, i % 4, 0:D])
                            else:
                                last = nc.vector.tensor_tensor(dst[0:size, i, :], ps[0:size, i % 4, 0:D],
                                                               addend(i, size), ALU.add)
                            last.then_inc(r.added, 1)
                        dve.wait_ge(r.added, parts[s][-1] + 1)
                        moments(dst, tiles, parts[s], s_).then_inc(r.var, 1)
                    if s >= 1:
                        dve.wait_ge(r.rstd, s)
                        for i in parts[s - 1]:
                            normalise(normed, dst, tiles, i, s_).then_inc(r.normed, 1)

            def attention(a, softmax):
                mask = const("addmask" if softmax else "mulmask", TG)
                for s in range(UNITS + 1):
                    if s < UNITS:
                        b = s % NPM
                        probs = pm[0:TG, b, :]
                        probs3 = probs.rearrange("p (h t) -> p h t", h=HU)
                        dve.wait_ge(a.scored, s + 1)
                        if s >= NPM:
                            dve.wait_ge(a.pt_made, s - NPM + 1)
                        for n in range(2):
                            dst = probs3[:, 4 * n:4 * n + 4, :]
                            src = ps[0:TG, 2 * (s % 2) + n, 0:4 * TG].rearrange("p (h t) -> p h t", h=4)
                            over = mask.unsqueeze(1).broadcast_to([TG, 4, TG])
                            if softmax:
                                last = nc.vector.scalar_tensor_tensor(dst, src, SCALE, over, ALU.mult, ALU.add)
                            else:
                                last = nc.vector.tensor_tensor(dst, src, over, ALU.mult)
                        last.then_inc(a.masked, 1)
                        dve.wait_ge(a.masked, s + 1)
                        if softmax:
                            nc.vector.tensor_reduce(att_small[0:TG, 0, b, 0, :], probs3, AXX, ALU.max)\
                                .then_inc(a.maxed, 1)
                        else:
                            link(nc.vector.tensor_reduce(att_small[0:TG, 1, b, 0, :], probs3, AXX, ALU.add))
                            link(nc.vector.tensor_scalar(att_small[0:TG, 1, b, 1, :], att_small[0:TG, 1, b, 0, :],
                                                         EPS_DEN, None, ALU.max))
                            nc.vector.reciprocal(att_small[0:TG, 1, b, 2, :], att_small[0:TG, 1, b, 1, :])\
                                .then_inc(a.summed, 1)
                    if softmax and s >= 1:
                        b = (s - 1) % NPM
                        dve.wait_ge(a.expd, s)
                        link(nc.vector.tensor_reduce(att_small[0:TG, 0, b, 1, :],
                                                     pm[0:TG, b, :].rearrange("p (h t) -> p h t", h=HU), AXX, ALU.add))
                        nc.vector.reciprocal(att_small[0:TG, 0, b, 2, :], att_small[0:TG, 0, b, 1, :])\
                            .then_inc(a.summed, 1)

            nc.vector.memset(ones_bf[:], 1.0)
            link(nc.vector.memset(ones[:], 1.0))
            link(nc.vector.tensor_copy(ones_r[:], ones[:]))
            nc.vector.memset(zeros[:], 0.0).then_inc(zeros_set, 1)
            dve.wait_ge(stats_set, len(stat) + 1)
            dve.wait_ge(d_add, 48)
            nc.vector.tensor_tensor(addp[:, 0, :], addp[:, 0, :], addp[:, 1, :], ALU.add).then_inc(addp_set, 1)
            def low_parts0():
                n = 0
                for w, hi, lo in parts0[:2]:
                    for k, cols in chunks(w):
                        n += 1
                        dve.wait_ge(w0_high, n)
                        nc.vector.tensor_tensor(lo[:, k, cols], w[:, k, cols], hi[:, k, cols].bitcast(F32),
                                                ALU.subtract).then_inc(w0_split, 1)
            rows(r_tok, PAIRS, TILES, h, None, x, stat[0], low_parts0)
            for i, (t0, size) in enumerate(TILES):
                dve.wait_ge(x0_high, i + 1)
                nc.vector.tensor_tensor(xa_lo[:, :, t0:t0 + size], turned_tile(i, size),
                                        xa_hi[:, :, t0:t0 + size].bitcast(F32), ALU.subtract).then_inc(r_tok.xt, 1)
            for j in range(2):
                dve.wait_ge(lat_high, j + 1)
                nc.vector.tensor_tensor(lat_lo[:, 0, half(j)], job_result(j, jobs0[j][1]),
                                        lat_hi[:, 0, half(j)].bitcast(F32), ALU.subtract)\
                    .then_inc((a0.by_act, a0.by_dve)[j], 1)
            for j in range(3, len(jobs0), 2):
                dve.wait_ge(a0.made, j + 1)
                dst = jobs0[j][1]
                nc.vector.tensor_copy(dst, job_result(j, dst)).then_inc(a0.by_dve, 1)
            dve.wait_ge(d_const, 16)
            nc.vector.memset(chosen[:], 0.0)
            nc.vector.tensor_copy(before_bf[:], const("before"))
            attention(a0, True)
            rows(r_out0, SINGLES, TILES, h, lambda s, n: h[0:n, s, :], x, stat[1])

            dve.wait_ge(logits0, NG)
            lg = ps[0:TG, 6, 0:GE].rearrange("p (g e) -> p g e", g=NG)
            r3 = [rsm[0:TG, n, :].rearrange("p (g e) -> p g e", g=NG) for n in range(4)]
            small = aff[0:TG, 0:8]
            small2 = aff[0:TG, 8:16]
            link(nc.vector.tensor_reduce(small, lg, AXX, ALU.max))
            nc.vector.tensor_tensor(r3[0], lg, small.unsqueeze(2).broadcast_to([TG, NG, EXPERTS]),
                                    ALU.subtract).then_inc(shifted0, 1)
            dve.wait_ge(exped0, 1)
            link(nc.vector.tensor_reduce(small, r3[1], AXX, ALU.add))
            link(nc.vector.reciprocal(small2, small))
            nc.vector.tensor_tensor(r3[2], r3[1], small2.unsqueeze(2).broadcast_to([TG, NG, EXPERTS]),
                                    ALU.mult).then_inc(affinity_set, 1)
            dve.wait_ge(affinity_made, 1)
            affs = aff[0:GE, 16:16 + TG]
            top, idf = picks[0:GE, 0, 0:2 * PICKS], picks[0:GE, 1, 0:2 * PICKS]
            link(nc.vector.tensor_copy(affs, ps[0:GE, 7, 0:TG]))
            for n in range(2):
                last = nc.vector.max(top[:, n * PICKS:(n + 1) * PICKS], affs[:, n * SEQ:(n + 1) * SEQ])
            link(last)
            for n in range(2):
                last = nc.vector.max_index(idx_u[0:GE, n, :], top[:, n * PICKS:(n + 1) * PICKS],
                                           affs[:, n * SEQ:(n + 1) * SEQ])
            link(last)
            link(nc.vector.tensor_copy(idf.rearrange("p (a j) -> p a j", a=2), idx_u[0:GE, 0:2, :]))
            tokens = picks[0:GE, 2, 0:2 * PICKS]
            link(nc.vector.tensor_tensor(tokens.rearrange("p (a j) -> p a j", a=2),
                                         idf.rearrange("p (a j) -> p a j", a=2),
                                         const("image_start", GE).unsqueeze(2).broadcast_to([GE, 2, PICKS]), ALU.add))
            for n, val in enumerate((tokens, top)):
                nc.vector.tensor_tensor(d_pick[0:GE, n, :].rearrange("p (g q) -> p g q", g=NG),
                                        const("same_group", GE).unsqueeze(2).broadcast_to([GE, NG, 2 * PICKS]),
                                        val.unsqueeze(1).broadcast_to([GE, NG, 2 * PICKS]), ALU.mult)
            for n in range(2):
                shape = [GE, NG, EXPERTS, PICKS]
                last = nc.vector.tensor_tensor(
                    d_idx[0:GE, :].rearrange("p (g a e j) -> p g a e j", g=NG, a=2, e=EXPERTS)[:, :, n],
                    ident[0:GE, 0:GE].rearrange("p (g e) -> p g e", g=NG).unsqueeze(3).broadcast_to(shape),
                    tokens[:, n * PICKS:(n + 1) * PICKS].unsqueeze(1).unsqueeze(1).broadcast_to(shape), ALU.mult)
            last.then_inc(d_ready, 1)
            dve.wait_ge(picks_made, 1)
            link(nc.vector.tensor_copy(picks[:, 4, 0:2 * EXPERTS], ps[:, 6, 0:2 * EXPERTS]))
            for i, (_, size) in enumerate(TILES):
                a, b = MEETS[i]
                nc.vector.tensor_scalar(
                    onehot[0:size, PARTS[i]:PARTS[i + 1], :].rearrange("p n c -> p (n c)"),
                    ps[0:size, 4:6, :].rearrange("p b n -> p (b n)")[:, a * P:(b + 1) * P],
                    const("token_of_row", size)[:, i:i + 1], None, ALU.is_equal).then_inc(onehot_set, 1)
            for c in range(2):
                dve.wait_ge(gathered, 2 * c + 2)
                nc.vector.tensor_copy(xin_half(c, 1), gathered_half(c, 1)).then_inc(xin_dve, 1)
            for e in range(EXPERTS):
                nc.vector.tensor_scalar(spread[:, e, :], const("tokens"), picks[:, 4, e:e + 1], None,
                                        ALU.is_equal).then_inc(spread_set, 1)

            for e in range(EXPERTS + 1):
                for half_ in range(2):
                    if e < EXPERTS:
                        dve.wait_ge(silu0, 2 * e + half_ + 1)
                        if e >= 3:
                            dve.wait_ge(down0, e - 2)
                        nc.vector.tensor_tensor(
                            hid0[:, e % 3, 4 * half_:4 * half_ + 4, :].rearrange("p k t -> p (k t)"),
                            sg0[:, half_, :], ps[:, 5 + 2 * half_, :], ALU.mult).then_inc(hid0_set, 1)
                    if e >= 1 and half_ == 0:
                        dve.wait_ge(down0, e)
                        gate = picks[:, 4, EXPERTS + e - 1:EXPERTS + e]
                        nc.vector.tensor_scalar(xe[:], ps[:, 3, 0:D], gate, None, ALU.mult)
                        if e >= 2:
                            dve.wait_ge(comb0, e - 1)
                        link(nc.vector.tensor_scalar(xe_hi[:], ps[:, 3, 0:D], gate, None, ALU.mult))
                        nc.vector.tensor_tensor(xe_lo[:], xe[:], xe_hi[:].bitcast(F32), ALU.subtract)\
                            .then_inc(xe_set, 1)

            dve.wait_ge(comb0, EXPERTS)
            nc.vector.tensor_copy(xt_a[:, 1, 0:BANK], ps[:, 1, :]).then_inc(h2t_set, 1)
            for s in range(len(PAIRS) + 2):
                if s < len(PAIRS):
                    dve.wait_ge(h2_set, PAIRS[s][-1] + 1)
                    moments(h2, TILES, PAIRS[s], stat[2]).then_inc(r_mid.var, 1)
                if 1 <= s <= len(PAIRS):
                    dve.wait_ge(r_mid.rstd, s)
                    for i in PAIRS[s - 1]:
                        last = normalise(z, h2, TILES, i, stat[2])
                    link(last)
                    moments(z, TILES, PAIRS[s - 1], stat[3]).then_inc(r_mid.var2, 1)
                if s >= 2:
                    dve.wait_ge(r_mid.rstd2, s - 1)
                    for i in PAIRS[s - 2]:
                        normalise(nrm, z, TILES, i, stat[3]).then_inc(r_mid.normed, 1)
            split_x(r_mid)
            for j, (_, dst) in enumerate(jobs1):
                done = (a1.by_act, a1.by_dve)[j % 2]
                dve.wait_ge(a1.expd, j + 1)
                nc.vector.scalar_tensor_tensor(dst, job_result(j, dst), 1.0, phi[:, j % 4, 1, :],
                                               ALU.add, ALU.max).then_inc(done, 1)
            attention(a1, False)
            rows(r_out1, PAIRS, TILES, z, lambda s, n: z[0:n, s, :], nrm, stat[4])
            split_x(r_out1)
            for i, (_, size) in enumerate(TILES):
                last = nc.vector.tensor_tensor(h2[0:size, i, :], z[0:size, i, :], h2[0:size, i, :], ALU.add)
            link(last)
            for j in range(2 * KF):
                cols, m = half(j // KF), j % KF
                dve.wait_ge(ffn_act, j + 1)
                link(nc.vector.tensor_copy(ft_hi[:, m, cols], ft[:, m, cols]))
                nc.vector.tensor_tensor(ft_lo[:, m, cols], ft[:, m, cols], ft_hi[:, m, cols].bitcast(F32),
                                        ALU.subtract).then_inc(ft_split, 1)
            for s in range(len(SINGLES) + 1):
                if s < len(SINGLES):
                    for i in SINGLES[s]:
                        size = TILES[i][1]
                        dve.wait_ge(r_ffn.made, i + 1)
                        nc.vector.tensor_tensor(h2[0:size, i, :], ps[0:size, i % 4, 0:D], h2[0:size, i, :],
                                                ALU.add).then_inc(r_ffn.added, 1)
                    dve.wait_ge(r_ffn.added, SINGLES[s][-1] + 1)
                    moments(h2, TILES, SINGLES[s], stat[5]).then_inc(r_ffn.var, 1)
                if s >= 1:
                    dve.wait_ge(r_ffn.rstd, s)
                    for i in SINGLES[s - 1]:
                        last = normalise(w_rows, h2, TILES, i, stat[5])
                    link(last)
                    moments(w_rows, TILES, SINGLES[s - 1], stat[0], rms=True).then_inc(r_ffn.var2, 1)
            sc = g_rows[:, 1, :]
            link(nc.vector.memset(sc, 0.0))
            dve.wait_ge(logits1, NT)
            last_size = TILES[-1][1]
            nc.vector.tensor_copy(sc[:, 0:(NT - 1) * 8], ps[:, 6, 0:(NT - 1) * 8])
            link(nc.vector.tensor_copy(sc[0:last_size, (NT - 1) * 8:NT * 8], ps[0:last_size, 6, (NT - 1) * 8:NT * 8]))
            tops = picks[:, 0, :].rearrange("p (i n) -> p i n", i=NT)
            sc3 = sc.rearrange("p (i n) -> p i n", i=NT)
            for i in range(NT):
                last = nc.vector.max(tops[:, i, :], sc3[:, i, :])
            link(last)
            for i in range(NT):
                last = nc.vector.max_index(idx_u[:, i, :], tops[:, i, :], sc3[:, i, :])
            link(last)
            idf1 = picks[:, 1, :].rearrange("p (i n) -> p i n", i=NT)
            link(nc.vector.tensor_copy(idf1, idx_u[:]))
            shape = [P, NT, EXPERTS]
            rk = [rank[:, n, :].rearrange("p (i n) -> p i n", i=NT) for n in range(6)]
            full = (NT - 1) * EXPERTS
            for n in range(2):
                last = nc.vector.tensor_tensor(rk[n], const("experts").unsqueeze(1).broadcast_to(shape),
                                               idf1[:, :, n:n + 1].broadcast_to(shape), ALU.is_equal)
            link(last)
            nc.vector.tensor_tensor(chosen[:, 0:full], rank[:, 0, 0:full], rank[:, 1, 0:full], ALU.add)
            nc.vector.tensor_tensor(chosen[0:last_size, full:], rank[0:last_size, 0, full:],
                                    rank[0:last_size, 1, full:], ALU.add).then_inc(chosen_set, 1)
            nc.vector.tensor_tensor(picks[:, 2, 0:NT], tops[:, :, 1], tops[:, :, 0], ALU.subtract).then_inc(diff1, 1)
            dve.wait_ge(ranked, 1)
            used, last_block, first_block = [g_rows[:, n, 0:EXPERTS] for n in range(3)]
            shape_l = [P, EXPERTS, LEVELS]
            more = rank[:, 2, :].rearrange("p (e l) -> p e l", e=EXPERTS)
            link(nc.vector.tensor_tensor(more, ps[:, 4, NT * EXPERTS:(NT + 1) * EXPERTS].unsqueeze(2)
                                         .broadcast_to(shape_l), const("filled").unsqueeze(1).broadcast_to(shape_l),
                                         ALU.is_gt))
            link(nc.vector.tensor_reduce(used, more, AXX, ALU.add))
            link(nc.vector.tensor_tensor_scan(last_block, ones[:, 0:EXPERTS], used, 0.0, ALU.mult, ALU.add))
            link(nc.vector.tensor_tensor(first_block, last_block, used, ALU.subtract))
            nc.vector.tensor_copy(bounds[:, 0, :], first_block)
            nc.vector.tensor_copy(bounds[:, 1, :], last_block).then_inc(bounds_set, 1)
            link(nc.vector.scalar_tensor_tensor(
                rk[3], first_block.unsqueeze(1).broadcast_to(shape), float(P),
                ps[:, 4, 0:NT * EXPERTS].rearrange("p (i n) -> p i n", i=NT), ALU.mult, ALU.add))
            for n in range(2):
                last = nc.vector.tensor_tensor(rk[4 + n], rk[3], rk[n], ALU.mult)
            link(last)
            for n in range(2):
                last = nc.vector.tensor_reduce(picks[:, 4, n * NT:(n + 1) * NT], rk[4 + n], AXX, ALU.add)
            link(last)
            place_a, place_b = picks[:, 4, 0:NT], picks[:, 4, NT:2 * NT]
            nc.vector.tensor_tensor(pos[:, 0, :], place_a, place_b, ALU.min)
            nc.vector.tensor_tensor(pos[:, 1, :], place_a, place_b, ALU.max).then_inc(pos_set, 1)
            dve.wait_ge(exped1, 1)
            a_low, b_low, total = picks[:, 1, 0:NT], picks[:, 1, NT:2 * NT], picks[:, 0, 0:NT]
            weight_a, weight_b = picks[:, 2, 0:NT], picks[:, 2, NT:2 * NT]
            nc.vector.tensor_tensor(a_low, place_a, place_b, ALU.is_lt)
            nc.vector.tensor_tensor(b_low, place_a, place_b, ALU.is_gt)
            link(nc.vector.tensor_scalar(total, picks[:, 3, 0:NT], 1.0, None, ALU.add))
            link(nc.vector.reciprocal(weight_a, total))
            link(nc.vector.tensor_tensor(weight_b, weight_a, picks[:, 3, 0:NT], ALU.mult))
            for n, (of_a, of_b) in enumerate(((a_low, b_low), (b_low, a_low))):
                nc.vector.tensor_tensor(picks[:, 3, n * NT:(n + 1) * NT], weight_a, of_a, ALU.mult)
                link(nc.vector.tensor_tensor(picks[:, 0, n * NT:(n + 1) * NT], weight_b, of_b, ALU.mult))
            nc.vector.tensor_tensor(picks[:, 5, 0:2 * NT], picks[:, 3, 0:2 * NT], picks[:, 0, 0:2 * NT], ALU.add)
            for i, (_, size) in enumerate(TILES):
                last = nc.vector.tensor_tensor(s_sum[0:size, i, :], w_rows[0:size, i, :], h2[0:size, i, :], ALU.add)
            link(last)

            dve.sem_inc(y_set, 1)
            blocks_end = dve.value_load(bounds[0:1, 1, EXPERTS - 1:EXPERTS], min_val=1, max_val=BLOCKS)
            with dve.Fori(0, blocks_end) as b:
                for half_ in range(2):
                    dve.wait_ge(silu1, 2 * b + half_ + 1)
                    nc.vector.tensor_tensor(hid1[:, 2 * half_:2 * half_ + 2, :].rearrange("p k t -> p (k t)"),
                                            sg1[:, half_, :], ps[:, 4 + 2 * half_, 0:2 * P], ALU.mult)\
                        .then_inc(hid1_set, 1)
                dve.wait_ge(down1, b + 1)
                dve.wait_ge(d_y, 16 * b + 16)
                nc.vector.tensor_copy(yblk[:], ps[:, 0, 0:D]).then_inc(y_set, 1)
            dve.wait_ge(d_low, 16 * NT)
            for i, (_, size) in enumerate(TILES):
                last = nc.vector.scalar_tensor_tensor(
                    s_sum[0:size, i, :], picked[0:size, 0, i, :], picks[0:size, 5, i:i + 1],
                    s_sum[0:size, i, :], ALU.mult, ALU.add)
            link(last)
            for i, (_, size) in enumerate(TILES):
                dve.wait_ge(d_high[i], 16)
                nc.vector.scalar_tensor_tensor(
                    orow[0:size, i, :], picked[0:size, 1, i, :], picks[0:size, 5, NT + i:NT + i + 1],
                    s_sum[0:size, i, :], ALU.mult, ALU.add).then_inc(out_set, 1)

        @block.gpsimd
        def _(pool):
            for s_ in stat:
                nc.gpsimd.memset(s_[:], 1.0).then_inc(stats_set, 1)
            nc.gpsimd.memset(neg_half[:], -0.5).then_inc(stats_set, 1)
            pool.wait_ge(stats_set, len(stat) + 1)

            def roots(var, rstd, parts, s_):
                for n, b in enumerate(parts):
                    root(n, b, var, rstd, s_)

            def root(n, b, var, rstd, s_):
                pool.wait_ge(var, n + 1)
                nc.gpsimd.tensor_tensor(s_[:, b[0]:b[-1] + 1, 9], s_[:, b[0]:b[-1] + 1, 8],
                                        neg_half[:].broadcast_to([P, len(b)]), ALU.pow).then_inc(rstd, 1)

            def attention(a, softmax):
                shape = [TG, HU, TG]
                for s in range(UNITS + 2):
                    if not softmax and s % 2 == 0 and s >= 2:
                        (w, hi, lo), k, cols = wf_chunks[s // 2 - 1]
                        pool.wait_ge(w_high, 6 * KD + s // 2)
                        nc.gpsimd.tensor_tensor(lo[:, k, cols], w[:, k, cols], hi[:, k, cols].bitcast(F32),
                                                ALU.subtract).then_inc(wf_split, 1)
                    if s >= 2:
                        b = (s - 2) % NPM
                        p3 = pm[0:TG, b, :].rearrange("p (h t) -> p h t", h=HU)
                        pool.wait_ge(a.summed, s - 1)
                        nc.gpsimd.tensor_tensor(p3, p3, att_small[0:TG, 0 if softmax else 1, b, 2, :].unsqueeze(2)
                                                .broadcast_to(shape), ALU.mult).then_inc(a.p, 1)
                    if softmax and s < UNITS:
                        p3 = pm[0:TG, s % NPM, :].rearrange("p (h t) -> p h t", h=HU)
                        pool.wait_ge(a.maxed, s + 1)
                        nc.gpsimd.tensor_tensor(p3, p3, att_small[0:TG, 0, s % NPM, 0, :].unsqueeze(2)
                                                .broadcast_to(shape), ALU.subtract).then_inc(a.shifted, 1)

            def low_parts(part, before, made, done):
                w, hi, lo = part
                for n, (k, cols) in enumerate(chunks(w)):
                    pool.wait_ge(made, before + n + 1)
                    nc.gpsimd.tensor_tensor(lo[:, k, cols], w[:, k, cols], hi[:, k, cols].bitcast(F32),
                                            ALU.subtract).then_inc(done, 1)

            roots(r_tok.var, r_tok.rstd, PAIRS, stat[0])
            low_parts(parts0[2], len(chunks(wkvd)) + len(chunks(wq0)), w0_high, w0_split_up)
            attention(a0, True)
            roots(r_out0.var, r_out0.rstd, SINGLES, stat[1])
            pool.wait_ge(r_out0.turned, NT)
            for i, (_, size) in enumerate(TILES):
                pool.wait_ge(xg_high, i + 1)
                nc.gpsimd.tensor_tensor(x_lo[0:size, i, :], x[0:size, i, :], x_hi[0:size, i, :].bitcast(F32),
                                        ALU.subtract).then_inc(xg_split, 1)

            def two(r, parts, s_a, s_b):
                for s in range(len(parts) + 1):
                    if s < len(parts):
                        root(s, parts[s], r.var, r.rstd, s_a)
                    if s >= 1:
                        root(s - 1, parts[s - 1], r.var2, r.rstd2, s_b)
            low_parts(parts1[0], 0, w_high, w_split)
            low_parts(parts1[1], 2 * KD, w_high, w_split)
            two(r_mid, PAIRS, stat[2], stat[3])
            low_parts(parts1[2], 4 * KD, w_high, w_split)
            attention(a1, False)
            roots(r_out1.var, r_out1.rstd, PAIRS, stat[4])
            two(r_ffn, SINGLES, stat[5], stat[0])

            pool.wait_ge(d_zeroed, 16)
            pool.wait_ge(pos_set, 1)
            for n in range(2):
                for i, (_, size) in enumerate(TILES):
                    nc.gpsimd.indirect_dma_start(
                        out=xs, out_offset=bass.IndirectOffsetOnAxis(ap=pos[0:size, n, i:i + 1], axis=0),
                        in_=xn1[0:size, i, :], in_offset=None).then_inc(d_sorted[n], 16)
            pool.sem_inc(d_y, 16)
            for n, done in enumerate((d_low, None)):
                pool.wait_ge(stored, n + 1)
                for i, (_, size) in enumerate(TILES):
                    nc.gpsimd.indirect_dma_start(
                        out=picked[0:size, n, i, :], out_offset=None, in_=xs,
                        in_offset=bass.IndirectOffsetOnAxis(ap=pos[0:size, n, i:i + 1], axis=0))\
                        .then_inc(done or d_high[i], 16)


def _constants():
    import numpy as np
    c = np.zeros((P, NCONST), np.float32)
    p = np.arange(P)

    def put(name, value):
        a, b = CONST[name]
        c[0:value.shape[0], a:b] = value
    t = np.arange(TG)
    seen = (t[:, None] // SEQ == t[None, :] // SEQ) & (t[None, :] <= t[:, None])
    put("ident", np.eye(P))
    put("addmask", np.where(seen, 0.0, MASKED))
    put("mulmask", np.where(seen, 1.0, 0.0))
    put("same_group", p[:, None] // EXPERTS == np.arange(NG)[None, :])
    put("same_expert", p[:, None] % EXPERTS == np.arange(EXPERTS)[None, :])
    put("token_of_row", p[:, None] + P * np.arange(NT)[None, :])
    put("image_start", TG * (p[:, None] // EXPERTS) + SEQ * np.arange(2)[None, :])
    put("filled", np.broadcast_to(np.array([-1] + [P * n for n in range(1, LEVELS)])[None, :], (P, LEVELS)))
    put("tokens", np.broadcast_to(np.arange(TOK)[None, :], (P, TOK)))
    put("before", p[:, None] < p[None, :])
    put("experts", np.broadcast_to(np.arange(EXPERTS)[None, :], (P, EXPERTS)))
    return c


def kernel(**inputs):
    import numpy as np
    import concourse.bacc as _bacc
    from concourse import mybir as _mybir
    from concourse.bass_utils import run_bass_kernel_spmd as _run

    a = {k: np.asarray(v) for k, v in inputs.items()}
    f = np.float32

    def blocks(w):
        return np.ascontiguousarray(w.reshape(-1, P, w.shape[-1]).transpose(1, 0, 2))

    n, c, hh, ww = a["x"].shape
    ph = 16
    side = hh // ph
    pt = a["x"].reshape(n, c, side, ph, side, ph).transpose(1, 3, 5, 0, 2, 4).reshape(PD, n, side * side)
    patches = np.zeros((PD, n, SEQ), a["x"].dtype)
    patches[:, :, 1:] = pt
    cls, pos = a["L0_tok_cls_token"][0], a["L0_tok_pos_embed"][0]
    first = np.concatenate([cls, np.broadcast_to(a["L0_tok_b"][None, :], (SEQ - 1, D))], 0)
    places = (np.arange(SEQ)[:, None] == np.arange(TOK)[None, :] % SEQ).astype(f)
    kvd = blocks(a["L0_attn_w_kv_down"])
    E = EXPERTS
    e0 = np.concatenate(
        [a["L0_ffn_w_gate"].transpose(0, 2, 1).reshape(E, KD, P, I0).transpose(0, 2, 1, 3).reshape(E, P, KD * I0),
         a["L0_ffn_w_up"].transpose(0, 2, 1).reshape(E, KD, P, I0).transpose(0, 2, 1, 3).reshape(E, P, KD * I0),
         a["L0_ffn_w_down"].transpose(0, 2, 1).reshape(E, K0, P, D).transpose(0, 2, 1, 3).reshape(E, P, K0 * D)], 2)
    e1 = np.concatenate(
        [a["L1_ffn_w_up"].transpose(0, 2, 1).reshape(E, KD, P, 2 * I1).transpose(0, 2, 1, 3).reshape(E, P, -1),
         a["L1_ffn_w_down"].transpose(0, 2, 1).reshape(E, K1, P, D).transpose(0, 2, 1, 3).reshape(E, P, K1 * D)], 2)
    params = np.stack([a["L1_attn_ln1_g"], a["L1_attn_ln1_b"], a["L1_attn_ln2_g"], a["L1_attn_ln2_b"],
                       a["L1_ffn_norm_scale"]], 1)
    arrays = {
        "patches_a": blocks(patches.reshape(PD, TOK)[:, 0:EARLY]),
        "patches_b": blocks(patches.reshape(PD, TOK)[:, EARLY:]), "tok_w": blocks(a["L0_tok_W"].T),
        "places": places, "add_a": pos, "add_b": first,
        "w_q": blocks(a["L0_attn_w_q"]), "w_kvd": kvd, "w_kvu": a["L0_attn_w_kv_up"],
        "w_out": blocks(a["L0_attn_w_out"]), "gate_w": blocks(a["L0_ffn_gate_w"].T), "w_e0": e0,
        "l1_wq": blocks(a["L1_attn_Wq"]), "l1_wk": blocks(a["L1_attn_Wk"]), "l1_wv": blocks(a["L1_attn_Wv"]),
        "l1_wo": blocks(a["L1_attn_Wo"]), "l1_wf1": blocks(a["L1_attn_Wf1"]), "l1_wf2": blocks(a["L1_attn_Wf2"]),
        "params": blocks(params), "router": blocks(a["L1_ffn_w_router"].T), "w_e1": e1,
        "consts": _constants(),
    }
    arrays = {k: np.ascontiguousarray(v) for k, v in arrays.items()}
    nc = _bacc.Bacc("TRN2", target_bir_lowering=False, num_devices=1)
    args = [nc.dram_tensor(k, v.shape, _mybir.dt.from_np(v.dtype), kind="ExternalInput").ap()
            for k, v in arrays.items()]
    args.append(nc.dram_tensor("out_rows", (TOK, D), F32, kind="ExternalOutput").ap())
    vit_tower(nc, *args)
    r = _run(nc, [arrays], core_ids=[0])
    return np.ascontiguousarray(r.results[0]["out_rows"].reshape(IMAGES, SEQ, D))
```
